# Optimizing a Trainium2 kernel written in Bass

```python
import numpy as np
import jax
import jax.numpy as jnp

def _softmax(x, axis=-1):
    return jax.nn.softmax(x, axis=axis)

def _gelu(x):
    return jax.nn.gelu(x, approximate=True)

def _silu(x):
    return jax.nn.silu(x)

def _sigmoid(x):
    return jax.nn.sigmoid(x)

def _layernorm(x, axis=-1, eps=1e-05):
    m = jnp.mean(x, axis=axis, keepdims=True)
    v = jnp.var(x, axis=axis, keepdims=True)
    return (x - m) / jnp.sqrt(v + eps)

def _scatter_add(tgt, idx, src, axis=0):
    return tgt.at[idx].add(src)

def _segment_sum(src, seg, n):
    return jax.ops.segment_sum(src, seg, n)
kernel_name = 'mk_gnn_resnorm_d4_gnn_r16_31c671'

def setup_inputs(seed: int=0):
    np.random.seed(seed)
    _w = jnp.asarray

    def _rec_inputs():
        import jax
        import jax.numpy as jnp
        _gk = jax.random.key(seed)
        x = -0.0003713 + 1 * jax.random.normal(jax.random.fold_in(_gk, 1), (6250, 128), jnp.float32)
        src = jax.random.randint(jax.random.fold_in(_gk, 2), (100000,), 0, 6250, jnp.int32)
        dst = jax.random.randint(jax.random.fold_in(_gk, 3), (100000,), 0, 6250, jnp.int32)
        _o = jnp.argsort(dst, stable=True)
        src = src[_o]
        dst = dst[_o]
        edge_type_4 = jax.random.randint(jax.random.fold_in(_gk, 13), (100000,), 0, 4, jnp.int32)
        edge_type_9 = jax.random.randint(jax.random.fold_in(_gk, 14), (100000,), 0, 9, jnp.int32)
        return (x, src, dst, edge_type_4, edge_type_9)
    x, src, dst, edge_type_4, edge_type_9 = _rec_inputs()

    def _L0_gnn_setup():
        import jax, jax.numpy as jnp
        import numpy as np
        N = 6250
        E = 100000
        D_IN = 128
        D_OUT = 128
        HEADS = 4
        C = D_OUT // HEADS
        NEG_SLOPE = 0.2
        EPS_SOFTMAX = 1e-16
        EPS_LN = 1e-05

        def _gat_edge_conv(x, src, dst, W, att_src, att_dst, gat_bias, skip_W, skip_b, ln_g, ln_b):
            n = x.shape[0]
            h = (x @ W).reshape(n, HEADS, C)
            a_s = jnp.einsum('nhc,hc->nh', h, att_src)
            a_d = jnp.einsum('nhc,hc->nh', h, att_dst)
            e = jax.nn.leaky_relu(a_s[src] + a_d[dst], NEG_SLOPE)
            m = jax.ops.segment_max(e, dst, num_segments=n)
            p = jnp.exp(e - m[dst])
            z = jax.ops.segment_sum(p, dst, num_segments=n)
            alpha = p / (z[dst] + EPS_SOFTMAX)
            msg = h[src] * alpha[:, :, None]
            out = jax.ops.segment_sum(msg, dst, num_segments=n)
            out = out.reshape(n, HEADS * C) + gat_bias
            out = out + x @ skip_W + skip_b
            mu = out.mean(-1, keepdims=True)
            var = ((out - mu) ** 2).mean(-1, keepdims=True)
            return (out - mu) * jax.lax.rsqrt(var + EPS_LN) * ln_g + ln_b
        key = jax.random.key(seed)
        ks = jax.random.split(key, 10)
        x = jax.random.normal(ks[0], (N, D_IN), dtype=jnp.float32)
        edge_index = jax.random.randint(ks[1], (2, E), 0, N, dtype=jnp.int64)
        s = 1.0 / np.sqrt(D_IN)
        W = jax.random.normal(ks[2], (D_IN, HEADS * C), dtype=jnp.float32) * s
        att_src = jax.random.normal(ks[3], (HEADS, C), dtype=jnp.float32) * (1.0 / np.sqrt(C))
        att_dst = jax.random.normal(ks[4], (HEADS, C), dtype=jnp.float32) * (1.0 / np.sqrt(C))
        gat_bias = jax.random.normal(ks[5], (D_OUT,), dtype=jnp.float32) * 0.02
        skip_W = jax.random.normal(ks[6], (D_IN, D_OUT), dtype=jnp.float32) * s
        skip_b = jax.random.normal(ks[7], (D_OUT,), dtype=jnp.float32) * 0.02
        ln_g = jnp.ones((D_OUT,), dtype=jnp.float32)
        ln_b = jnp.zeros((D_OUT,), dtype=jnp.float32)
        return {'x': x, 'edge_index': edge_index, 'W': W, 'att_src': att_src, 'att_dst': att_dst, 'gat_bias': gat_bias, 'skip_W': skip_W, 'skip_b': skip_b, 'ln_g': ln_g, 'ln_b': ln_b}
    _L0_gnn_all = _L0_gnn_setup()
    _L0_gnn_in = {k: v for k, v in _L0_gnn_all.items() if k in ('W', 'att_src', 'att_dst', 'gat_bias', 'skip_W', 'skip_b', 'ln_g', 'ln_b')}
    del _L0_gnn_all

    def _L1_gnn_setup():
        import jax, jax.numpy as jnp
        import numpy as np
        N_NODES = 3125
        N_EDGES = 50000
        ENC_DIM = 128

        def _sage_layer(h, edge_src, edge_dst, W, b):
            n = h.shape[0]
            msg_sum = jax.ops.segment_sum(h[edge_src], edge_dst, num_segments=n)
            deg = jax.ops.segment_sum(jnp.ones_like(edge_dst, dtype=h.dtype), edge_dst, num_segments=n)
            m = msg_sum / jnp.maximum(deg, 1.0)[:, None]
            hc = jnp.concatenate([h, m], axis=1)
            return jax.nn.relu(hc @ W + b)
        key = jax.random.key(seed)
        k_h, k_s, k_d, k_w1, k_w2 = jax.random.split(key, 5)
        h = jax.random.normal(k_h, (N_NODES, ENC_DIM), dtype=jnp.float32)
        edge_src = jax.random.randint(k_s, (N_EDGES,), 0, N_NODES, dtype=jnp.int32)
        edge_dst = jax.random.randint(k_d, (N_EDGES,), 0, N_NODES, dtype=jnp.int32)
        scale = 1.0 / np.sqrt(2 * ENC_DIM)
        W1 = jax.random.normal(k_w1, (2 * ENC_DIM, ENC_DIM), dtype=jnp.float32) * scale
        b1 = jnp.zeros((ENC_DIM,), dtype=jnp.float32)
        W2 = jax.random.normal(k_w2, (2 * ENC_DIM, ENC_DIM), dtype=jnp.float32) * scale
        b2 = jnp.zeros((ENC_DIM,), dtype=jnp.float32)
        return {'h': h, 'edge_src': edge_src, 'edge_dst': edge_dst, 'W1': W1, 'b1': b1, 'W2': W2, 'b2': b2}
    _L1_gnn_all = _L1_gnn_setup()
    _L1_gnn_in = {k: v for k, v in _L1_gnn_all.items() if k in ('W1', 'b1', 'W2', 'b2')}
    del _L1_gnn_all

    def _L2_gnn_setup():
        import jax, jax.numpy as jnp
        import numpy as np
        NUM_EDGE_TYPES = 8
        HIDDEN = 128
        N_NODES = 3125
        N_EDGES = 37500

        def _gru_cell(x, h, W_ih, W_hh, b_ih, b_hh):
            H = h.shape[-1]
            gi = x @ W_ih.T + b_ih
            gh = h @ W_hh.T + b_hh
            i_r, i_z, i_n = (gi[:, :H], gi[:, H:2 * H], gi[:, 2 * H:])
            h_r, h_z, h_n = (gh[:, :H], gh[:, H:2 * H], gh[:, 2 * H:])
            r = jax.nn.sigmoid(i_r + h_r)
            z = jax.nn.sigmoid(i_z + h_z)
            n = jnp.tanh(i_n + r * h_n)
            return (1.0 - z) * n + z * h
        key = jax.random.key(seed)
        ks = jax.random.split(key, 10)
        H = HIDDEN
        h = jax.random.normal(ks[0], (N_NODES, H), dtype=jnp.float32)
        edge_index = jax.random.randint(ks[1], (2, N_EDGES), 0, N_NODES, dtype=jnp.int32)
        edge_type = jax.random.randint(ks[2], (N_EDGES,), 0, NUM_EDGE_TYPES + 1, dtype=jnp.int32)
        s = 1.0 / np.sqrt(H)
        W_msg = jax.random.uniform(ks[3], (H, H), jnp.float32, -s, s)
        b_msg = jax.random.uniform(ks[4], (H,), jnp.float32, -s, s)
        edge_embed = jax.random.normal(ks[5], (NUM_EDGE_TYPES + 1, H), dtype=jnp.float32)
        W_ih = jax.random.uniform(ks[6], (3 * H, H), jnp.float32, -s, s)
        W_hh = jax.random.uniform(ks[7], (3 * H, H), jnp.float32, -s, s)
        b_ih = jax.random.uniform(ks[8], (3 * H,), jnp.float32, -s, s)
        b_hh = jax.random.uniform(ks[9], (3 * H,), jnp.float32, -s, s)
        return {'h': h, 'edge_index': edge_index, 'edge_type': edge_type, 'num_nodes': N_NODES, 'W_msg': W_msg, 'b_msg': b_msg, 'edge_embed': edge_embed, 'W_ih': W_ih, 'W_hh': W_hh, 'b_ih': b_ih, 'b_hh': b_hh}
    _L2_gnn_all = _L2_gnn_setup()
    _L2_gnn_in = {k: v for k, v in _L2_gnn_all.items() if k in ('W_msg', 'b_msg', 'edge_embed', 'W_ih', 'W_hh', 'b_ih', 'b_hh')}
    del _L2_gnn_all

    def _L3_gnn_setup():
        import jax, jax.numpy as jnp
        import numpy as np
        N = 3125
        E = 50000
        IN = 128
        H = 256
        EMB = 128
        R = 4
        HEADS = 2

        def _segmean(msg, seg, num_segments):
            s = jax.ops.segment_sum(msg, seg, num_segments=num_segments)
            c = jax.ops.segment_sum(jnp.ones((seg.shape[0], 1), msg.dtype), seg, num_segments=num_segments)
            return s / jnp.maximum(c, 1.0)

        def _sage(x, src, dst, Wl, Wr, b, n):
            agg = _segmean(x[src], dst, n)
            return agg @ Wl + x @ Wr + b

        def _gat(x, src, dst, W, a_src, a_dst, b, n):
            loop = jnp.arange(n, dtype=src.dtype)
            src = jnp.concatenate([src, loop])
            dst = jnp.concatenate([dst, loop])
            h = (x @ W).reshape(n, HEADS, -1)
            al_src = (h * a_src).sum(-1)
            al_dst = (h * a_dst).sum(-1)
            e = jax.nn.leaky_relu(al_src[src] + al_dst[dst], 0.2)
            m = jax.ops.segment_max(e, dst, num_segments=n)
            ex = jnp.exp(e - m[dst])
            den = jax.ops.segment_sum(ex, dst, num_segments=n)
            alpha = ex / jnp.maximum(den[dst], 1e-16)
            out = jax.ops.segment_sum(alpha[:, :, None] * h[src], dst, num_segments=n)
            return out.mean(axis=1) + b

        def _rgcn(x, src, dst, etype, Wrel, Wroot, b, n, r):
            xt = jnp.einsum('nh,rhe->rne', x, Wrel)
            m = xt[etype, src]
            seg = dst * r + etype
            agg = _segmean(m, seg, n * r).reshape(n, r, -1).sum(axis=1)
            return agg + x @ Wroot + b
        key = jax.random.key(seed)
        ks = jax.random.split(key, 20)
        w = lambda k, shape: jax.random.normal(k, shape, dtype=jnp.float32) * 0.05
        return dict(x=jax.random.normal(ks[0], (N, IN), dtype=jnp.float32), edge_index=jax.random.randint(ks[1], (2, E), 0, N, dtype=jnp.int32), edge_type=jax.random.randint(ks[2], (E,), 0, R, dtype=jnp.int32), sage1_Wl=w(ks[3], (IN, H)), sage1_Wr=w(ks[4], (IN, H)), sage1_b=jnp.zeros((H,), jnp.float32), sage2_Wl=w(ks[5], (H, H)), sage2_Wr=w(ks[6], (H, H)), sage2_b=jnp.zeros((H,), jnp.float32), gat_W=w(ks[7], (H, HEADS * H)), gat_att_src=w(ks[8], (HEADS, H)), gat_att_dst=w(ks[9], (HEADS, H)), gat_b=jnp.zeros((H,), jnp.float32), rgcn_Wrel=w(ks[10], (R, H, EMB)), rgcn_Wroot=w(ks[11], (H, EMB)), rgcn_b=jnp.zeros((EMB,), jnp.float32), fusion_W=w(ks[12], (H + H + EMB, EMB)), fusion_b=jnp.zeros((EMB,), jnp.float32))
    _L3_gnn_all = _L3_gnn_setup()
    _L3_gnn_in = {k: v for k, v in _L3_gnn_all.items() if k in ('sage1_Wl', 'sage1_Wr', 'sage1_b', 'sage2_Wl', 'sage2_Wr', 'sage2_b', 'gat_W', 'gat_att_src', 'gat_att_dst', 'gat_b', 'rgcn_Wrel', 'rgcn_Wroot', 'rgcn_b', 'fusion_W', 'fusion_b')}
    del _L3_gnn_all
    return {'x': x, 'src': src, 'dst': dst, 'edge_type_4': edge_type_4, 'edge_type_9': edge_type_9, 'L0_gnn_W': _L0_gnn_in['W'], 'L0_gnn_att_src': _L0_gnn_in['att_src'], 'L0_gnn_att_dst': _L0_gnn_in['att_dst'], 'L0_gnn_gat_bias': _L0_gnn_in['gat_bias'], 'L0_gnn_skip_W': _L0_gnn_in['skip_W'], 'L0_gnn_skip_b': _L0_gnn_in['skip_b'], 'L0_gnn_ln_g': _L0_gnn_in['ln_g'], 'L0_gnn_ln_b': _L0_gnn_in['ln_b'], 'L1_gnn_W1': _L1_gnn_in['W1'], 'L1_gnn_b1': _L1_gnn_in['b1'], 'L1_gnn_W2': _L1_gnn_in['W2'], 'L1_gnn_b2': _L1_gnn_in['b2'], 'L2_gnn_W_msg': _L2_gnn_in['W_msg'], 'L2_gnn_b_msg': _L2_gnn_in['b_msg'], 'L2_gnn_edge_embed': _L2_gnn_in['edge_embed'], 'L2_gnn_W_ih': _L2_gnn_in['W_ih'], 'L2_gnn_W_hh': _L2_gnn_in['W_hh'], 'L2_gnn_b_ih': _L2_gnn_in['b_ih'], 'L2_gnn_b_hh': _L2_gnn_in['b_hh'], 'L3_gnn_sage1_Wl': _L3_gnn_in['sage1_Wl'], 'L3_gnn_sage1_Wr': _L3_gnn_in['sage1_Wr'], 'L3_gnn_sage1_b': _L3_gnn_in['sage1_b'], 'L3_gnn_sage2_Wl': _L3_gnn_in['sage2_Wl'], 'L3_gnn_sage2_Wr': _L3_gnn_in['sage2_Wr'], 'L3_gnn_sage2_b': _L3_gnn_in['sage2_b'], 'L3_gnn_gat_W': _L3_gnn_in['gat_W'], 'L3_gnn_gat_att_src': _L3_gnn_in['gat_att_src'], 'L3_gnn_gat_att_dst': _L3_gnn_in['gat_att_dst'], 'L3_gnn_gat_b': _L3_gnn_in['gat_b'], 'L3_gnn_rgcn_Wrel': _L3_gnn_in['rgcn_Wrel'], 'L3_gnn_rgcn_Wroot': _L3_gnn_in['rgcn_Wroot'], 'L3_gnn_rgcn_b': _L3_gnn_in['rgcn_b'], 'L3_gnn_fusion_W': _L3_gnn_in['fusion_W'], 'L3_gnn_fusion_b': _L3_gnn_in['fusion_b']}

def reference(x, src, dst, edge_type_4, edge_type_9, L0_gnn_W, L0_gnn_att_src, L0_gnn_att_dst, L0_gnn_gat_bias, L0_gnn_skip_W, L0_gnn_skip_b, L0_gnn_ln_g, L0_gnn_ln_b, L1_gnn_W1, L1_gnn_b1, L1_gnn_W2, L1_gnn_b2, L2_gnn_W_msg, L2_gnn_b_msg, L2_gnn_edge_embed, L2_gnn_W_ih, L2_gnn_W_hh, L2_gnn_b_ih, L2_gnn_b_hh, L3_gnn_sage1_Wl, L3_gnn_sage1_Wr, L3_gnn_sage1_b, L3_gnn_sage2_Wl, L3_gnn_sage2_Wr, L3_gnn_sage2_b, L3_gnn_gat_W, L3_gnn_gat_att_src, L3_gnn_gat_att_dst, L3_gnn_gat_b, L3_gnn_rgcn_Wrel, L3_gnn_rgcn_Wroot, L3_gnn_rgcn_b, L3_gnn_fusion_W, L3_gnn_fusion_b):
    import jax
    import jax.numpy as jnp

    def _L0_gnn_ref(x, edge_index, W, att_src, att_dst, gat_bias, skip_W, skip_b, ln_g, ln_b):
        import jax, jax.numpy as jnp
        import numpy as np
        N = 6250
        E = 100000
        D_IN = 128
        D_OUT = 128
        HEADS = 4
        C = D_OUT // HEADS
        NEG_SLOPE = 0.2
        EPS_SOFTMAX = 1e-16
        EPS_LN = 1e-05

        def _gat_edge_conv(x, src, dst, W, att_src, att_dst, gat_bias, skip_W, skip_b, ln_g, ln_b):
            n = x.shape[0]
            h = (x @ W).reshape(n, HEADS, C)
            a_s = jnp.einsum('nhc,hc->nh', h, att_src)
            a_d = jnp.einsum('nhc,hc->nh', h, att_dst)
            e = jax.nn.leaky_relu(a_s[src] + a_d[dst], NEG_SLOPE)
            m = jax.ops.segment_max(e, dst, num_segments=n)
            p = jnp.exp(e - m[dst])
            z = jax.ops.segment_sum(p, dst, num_segments=n)
            alpha = p / (z[dst] + EPS_SOFTMAX)
            msg = h[src] * alpha[:, :, None]
            out = jax.ops.segment_sum(msg, dst, num_segments=n)
            out = out.reshape(n, HEADS * C) + gat_bias
            out = out + x @ skip_W + skip_b
            mu = out.mean(-1, keepdims=True)
            var = ((out - mu) ** 2).mean(-1, keepdims=True)
            return (out - mu) * jax.lax.rsqrt(var + EPS_LN) * ln_g + ln_b
        n = x.shape[0]
        loops = jnp.arange(n, dtype=edge_index.dtype)
        src = jnp.concatenate([edge_index[0], loops])
        dst = jnp.concatenate([edge_index[1], loops])
        return _gat_edge_conv(x, src, dst, W, att_src, att_dst, gat_bias, skip_W, skip_b, ln_g, ln_b)

    def _L1_gnn_ref(h, edge_src, edge_dst, W1, b1, W2, b2):
        import jax, jax.numpy as jnp
        import numpy as np
        N_NODES = 3125
        N_EDGES = 50000
        ENC_DIM = 128

        def _sage_layer(h, edge_src, edge_dst, W, b):
            n = h.shape[0]
            msg_sum = jax.ops.segment_sum(h[edge_src], edge_dst, num_segments=n)
            deg = jax.ops.segment_sum(jnp.ones_like(edge_dst, dtype=h.dtype), edge_dst, num_segments=n)
            m = msg_sum / jnp.maximum(deg, 1.0)[:, None]
            hc = jnp.concatenate([h, m], axis=1)
            return jax.nn.relu(hc @ W + b)
        h = _sage_layer(h, edge_src, edge_dst, W1, b1)
        h = _sage_layer(h, edge_src, edge_dst, W2, b2)
        return h

    def _L2_gnn_ref(h, edge_index, edge_type, num_nodes, W_msg, b_msg, edge_embed, W_ih, W_hh, b_ih, b_hh):
        import jax, jax.numpy as jnp
        import numpy as np
        NUM_EDGE_TYPES = 8
        HIDDEN = 128
        N_NODES = 3125
        N_EDGES = 37500

        def _gru_cell(x, h, W_ih, W_hh, b_ih, b_hh):
            H = h.shape[-1]
            gi = x @ W_ih.T + b_ih
            gh = h @ W_hh.T + b_hh
            i_r, i_z, i_n = (gi[:, :H], gi[:, H:2 * H], gi[:, 2 * H:])
            h_r, h_z, h_n = (gh[:, :H], gh[:, H:2 * H], gh[:, 2 * H:])
            r = jax.nn.sigmoid(i_r + h_r)
            z = jax.nn.sigmoid(i_z + h_z)
            n = jnp.tanh(i_n + r * h_n)
            return (1.0 - z) * n + z * h
        src = edge_index[0]
        dst = edge_index[1]
        src_h = h[src] @ W_msg.T + b_msg
        emb = edge_embed[jnp.clip(edge_type, 0, NUM_EDGE_TYPES)]
        msg = src_h + emb
        messages = jax.ops.segment_sum(msg, dst, num_segments=num_nodes)
        h_new = _gru_cell(messages, h[:num_nodes], W_ih, W_hh, b_ih, b_hh)
        result = jnp.zeros_like(h).at[:num_nodes].set(h_new)
        return result

    def _L3_gnn_ref(x, edge_index, edge_type, sage1_Wl, sage1_Wr, sage1_b, sage2_Wl, sage2_Wr, sage2_b, gat_W, gat_att_src, gat_att_dst, gat_b, rgcn_Wrel, rgcn_Wroot, rgcn_b, fusion_W, fusion_b):
        import jax, jax.numpy as jnp
        import numpy as np
        N = 3125
        E = 50000
        IN = 128
        H = 256
        EMB = 128
        R = 4
        HEADS = 2

        def _segmean(msg, seg, num_segments):
            s = jax.ops.segment_sum(msg, seg, num_segments=num_segments)
            c = jax.ops.segment_sum(jnp.ones((seg.shape[0], 1), msg.dtype), seg, num_segments=num_segments)
            return s / jnp.maximum(c, 1.0)

        def _sage(x, src, dst, Wl, Wr, b, n):
            agg = _segmean(x[src], dst, n)
            return agg @ Wl + x @ Wr + b

        def _gat(x, src, dst, W, a_src, a_dst, b, n):
            loop = jnp.arange(n, dtype=src.dtype)
            src = jnp.concatenate([src, loop])
            dst = jnp.concatenate([dst, loop])
            h = (x @ W).reshape(n, HEADS, -1)
            al_src = (h * a_src).sum(-1)
            al_dst = (h * a_dst).sum(-1)
            e = jax.nn.leaky_relu(al_src[src] + al_dst[dst], 0.2)
            m = jax.ops.segment_max(e, dst, num_segments=n)
            ex = jnp.exp(e - m[dst])
            den = jax.ops.segment_sum(ex, dst, num_segments=n)
            alpha = ex / jnp.maximum(den[dst], 1e-16)
            out = jax.ops.segment_sum(alpha[:, :, None] * h[src], dst, num_segments=n)
            return out.mean(axis=1) + b

        def _rgcn(x, src, dst, etype, Wrel, Wroot, b, n, r):
            xt = jnp.einsum('nh,rhe->rne', x, Wrel)
            m = xt[etype, src]
            seg = dst * r + etype
            agg = _segmean(m, seg, n * r).reshape(n, r, -1).sum(axis=1)
            return agg + x @ Wroot + b
        src, dst = (edge_index[0], edge_index[1])
        n = x.shape[0]
        x1 = jax.nn.relu(_sage(x, src, dst, sage1_Wl, sage1_Wr, sage1_b, n))
        x_sage = jax.nn.relu(_sage(x1, src, dst, sage2_Wl, sage2_Wr, sage2_b, n))
        x_gat = jax.nn.relu(_gat(x_sage, src, dst, gat_W, gat_att_src, gat_att_dst, gat_b, n))
        x_rgcn = _rgcn(x_gat, src, dst, edge_type, rgcn_Wrel, rgcn_Wroot, rgcn_b, n, R)
        x_all = jnp.concatenate([x_sage, x_gat, x_rgcn], axis=1)
        out = x_all @ fusion_W + fusion_b
        norm = jnp.maximum(jnp.linalg.norm(out, axis=1, keepdims=True), 1e-12)
        return out / norm
    edge_index = jnp.stack([src, dst])
    x = _layernorm(x + _L0_gnn_ref(x, edge_index, L0_gnn_W, L0_gnn_att_src, L0_gnn_att_dst, L0_gnn_gat_bias, L0_gnn_skip_W, L0_gnn_skip_b, L0_gnn_ln_g, L0_gnn_ln_b), axis=-1)
    x = _layernorm(x + _L1_gnn_ref(x, src, dst, L1_gnn_W1, L1_gnn_b1, L1_gnn_W2, L1_gnn_b2), axis=-1)
    x = _layernorm(x + _L2_gnn_ref(x, edge_index, edge_type_9, 6250, L2_gnn_W_msg, L2_gnn_b_msg, L2_gnn_edge_embed, L2_gnn_W_ih, L2_gnn_W_hh, L2_gnn_b_ih, L2_gnn_b_hh), axis=-1)
    x = _layernorm(x + _L3_gnn_ref(x, edge_index, edge_type_4, L3_gnn_sage1_Wl, L3_gnn_sage1_Wr, L3_gnn_sage1_b, L3_gnn_sage2_Wl, L3_gnn_sage2_Wr, L3_gnn_sage2_b, L3_gnn_gat_W, L3_gnn_gat_att_src, L3_gnn_gat_att_dst, L3_gnn_gat_b, L3_gnn_rgcn_Wrel, L3_gnn_rgcn_Wroot, L3_gnn_rgcn_b, L3_gnn_fusion_W, L3_gnn_fusion_b), axis=-1)
    return x

_drawn_inputs = setup_inputs


def setup_inputs(seed=0):
    import zlib

    import numpy as np

    out = dict(_drawn_inputs(seed))
    spreads = {'L0_gnn_ln_g': (1.0, 0.2),
     'L0_gnn_ln_b': (0.0, 0.1),
     'L1_gnn_b1': (0.0, 0.1),
     'L1_gnn_b2': (0.0, 0.1),
     'L3_gnn_sage1_b': (0.0, 0.719),
     'L3_gnn_sage2_b': (0.0, 0.463),
     'L3_gnn_gat_b': (0.0, 0.342),
     'L3_gnn_rgcn_b': (0.0, 1.326),
     'L3_gnn_fusion_b': (0.0, 0.839)}
    factors = {'L0_gnn_skip_b': 2.982,
     'L2_gnn_b_ih': 6.391,
     'L2_gnn_b_hh': 8.0,
     'L3_gnn_gat_att_src': 64.0,
     'L3_gnn_gat_att_dst': 64.0,
     'L3_gnn_rgcn_Wroot': 4.547,
     'L3_gnn_sage1_Wl': 4.968,
     'L3_gnn_sage1_Wr': 3.014}
    for name, (base, spread) in spreads.items():
        noise = np.random.default_rng([zlib.crc32(name.encode()), seed]).standard_normal(out[name].shape)
        drawn = base * np.exp(spread * noise) if base else spread * noise
        out[name] = jnp.asarray(drawn.astype(out[name].dtype))
    for name, factor in factors.items():
        out[name] = (out[name] * factor).astype(out[name].dtype)
    return out
```

```python
import concourse.bass as bass
from concourse import mybir
from contextlib import ExitStack

FP32 = mybir.dt.float32
I32 = mybir.dt.int32
ALU = mybir.AluOpType
ACT = mybir.ActivationFunctionType
AX = mybir.AxisListType

PARTS = 128
NODES = 6250
EDGES = 100000
TILES = -(-NODES // PARTS)
NODE_ROWS = TILES * PARTS
GROUP = 7
GROUPS = TILES // GROUP
LANES = 8
ITEM_BOUND = (EDGES + 127 * TILES) // 128
ITEMS = -(-ITEM_BOUND // 16) * 16
ITEM_ROWS = ITEMS // LANES
ROW = LANES * PARTS
SLOTS = 16
HALF = 8
BIG = 1.0e30
assert GROUPS * GROUP == TILES and ITEM_ROWS <= PARTS


def bc(ap, shape):
    return ap.to_broadcast(shape)


class Scope:

    def __init__(self, nc, ctx, tag):
        self.nc, self.ctx, self.tag, self.sems = nc, ctx, tag, []
        ctx.callback(self.clear)

    def clear(self):
        if self.sems:
            self.nc.clear_and_free_semaphores(self.sems)
            self.nc.all_engine_barrier()

    def sb(self, name, shape, dt=FP32):
        return self.ctx.enter_context(self.nc.sbuf_tensor(f"{self.tag}_{name}", shape, dt))

    def ps(self, name, shape, dt=FP32):
        return self.ctx.enter_context(self.nc.psum_tensor(f"{self.tag}_{name}", shape, dt))

    def sem(self, name):
        self.sems.append(self.nc.alloc_semaphore(f"{self.tag}_{name}"))
        return self.sems[-1]


def node_view(table, g):
    return table.rearrange("(t p) d -> p t d", p=PARTS)[:, bass.ds(g * GROUP, GROUP), :]


def prepare(nc, src, dst, et4, et9, K):
    with ExitStack() as ctx:
        m = Scope(nc, ctx, "prep")
        LR, LC = 125, EDGES // 125
        dst_i = m.sb("dst_i", [LR, LC], I32)
        dst_f = m.sb("dst_f", [LR, LC])
        below = m.sb("below", [LR, LC])
        bounds_i = m.sb("bounds_i", [PARTS, TILES + 1], I32)
        bounds = m.sb("bounds", [PARTS, TILES + 1])
        below_count = m.sb("below_count", [LR, TILES + 1])
        ones = m.sb("ones", [PARTS, PARTS])
        first = m.sb("first", [PARTS, TILES + 1])
        size_f = m.sb("size_f", [PARTS, TILES])
        size_i = m.sb("size_i", [PARTS, TILES], I32)
        n_items = m.sb("n_items", [PARTS, TILES])
        zero_t = m.sb("zero_t", [PARTS, TILES])
        item_end = m.sb("item_end", [PARTS, TILES])
        item_start = m.sb("item_start", [PARTS, TILES])
        edge_base = m.sb("edge_base", [PARTS, TILES])
        item_i = m.sb("item_i", [ITEM_ROWS, LANES], I32)
        item = m.sb("item", [ITEM_ROWS, LANES])
        sel_a = m.sb("sel_a", [ITEM_ROWS, LANES, TILES])
        sel_b = m.sb("sel_b", [ITEM_ROWS, LANES, TILES])
        tile_of = m.sb("tile_of", [ITEM_ROWS, LANES])
        tile_i = m.sb("tile_i", [ITEM_ROWS, LANES], I32)
        e_start = m.sb("e_start", [ITEM_ROWS, LANES])
        e_end = m.sb("e_end", [ITEM_ROWS, LANES])
        e_read = m.sb("e_read", [ITEM_ROWS, LANES])
        e_read_i = m.sb("e_read_i", [ITEM_ROWS, LANES], I32)
        raw = {n: m.sb("raw_" + n, [ITEM_ROWS, ROW], I32) for n in ("src", "dst", "et4", "et9")}
        f_src = m.sb("f_src", [ITEM_ROWS, ROW])
        f_et4 = m.sb("f_et4", [ITEM_ROWS, ROW])
        f_et9 = m.sb("f_et9", [ITEM_ROWS, ROW])
        f_xt = m.sb("f_xt", [ITEM_ROWS, ROW])
        f_dst = m.sb("f_dst", [ITEM_ROWS, ROW])
        dst_local = m.sb("dst_local", [ITEM_ROWS, ROW])
        pos = m.sb("pos", [ITEM_ROWS, ROW])
        valid = m.sb("valid", [ITEM_ROWS, ROW])
        v_end = m.sb("v_end", [ITEM_ROWS, ROW])
        key = m.sb("key", [ITEM_ROWS, ROW + 2])
        cont = m.sb("cont", [ITEM_ROWS, ROW + 1])
        last = m.sb("last", [ITEM_ROWS, ROW])
        ps_b = m.ps("ps_b", [PARTS, 512])
        ps_t = m.ps("ps_t", [PARTS, 2, 2, 512])
        s_in, s_pool, s_v, s_pe, s_read, s_keys, s_tr, s_out, s_tile, s_pad = (
            m.sem(n) for n in ("s_in", "s_pool", "s_v", "s_pe", "s_read", "s_keys", "s_tr", "s_out", "s_tile", "s_pad"))
        fields = ["src", "dst", "et4", "et9"]
        arrays = {"src": src, "dst": dst, "et4": et4, "et9": et9}
        moved = [(f_src, K["src_e"]), (f_xt, K["xt_e"]), (dst_local, K["dst_e"]),
                 (f_et4, K["et4_e"]), (f_et9, K["et9_e"]), (last, K["last_e"])]
        mark = {}
        block = ctx.enter_context(nc.Block())

        @block.gpsimd
        def _(pool):
            def step(ins):
                step.n += 1
                ins.then_inc(s_pool, 1)
            step.n = 0
            step(pool.iota(bounds_i[:, :], [[PARTS, TILES + 1]], base=0, channel_multiplier=0))
            step(pool.iota(item_i[:, :], [[1, LANES]], base=0, channel_multiplier=LANES))
            step(pool.iota(K["iota_i"][:, :], [[1, PARTS]], base=0, channel_multiplier=0))
            step(pool.iota(K["iota_pi"][:, :], [[1, 1]], base=0, channel_multiplier=1))
            step(pool.memset(ones[:, :], 1.0))
            step(pool.memset(K["ident"][:, :], 0.0))
            step(pool.memset(K["zero_i"][:, :], 0))
            pool.wait_ge(s_pool, 7)
            step(pool.affine_select(out=K["ident"][:, :], in_=K["ident"][:, :], compare_op=ALU.not_equal,
                                    fill=1.0, base=0, pattern=[[-1, PARTS]], channel_multiplier=1))
            pool.wait_ge(s_v, mark_read)
            pool.wait_ge(s_pad, 16 * 2 * len(fields))
            for n in fields:
                for j in range(LANES):
                    pool.indirect_dma_start(
                        raw[n][:, j * PARTS:(j + 1) * PARTS], None, K["edges_" + n].unsqueeze(1),
                        bass.IndirectOffsetOnAxis(ap=e_read_i[:, j:j + 1], axis=0)).then_inc(s_read, 16)

        @block.vector
        def _(dve):
            v = nc.vector
            count = [0]

            def step(ins):
                count[0] += 1
                ins.then_inc(s_v, 1)
                dve.wait_ge(s_v, count[0])

            dve.wait_ge(s_in, 16)
            step(v.tensor_copy(dst_f[:, :], dst_i[:, :]))
            dve.wait_ge(s_pool, 8)
            step(v.tensor_copy(bounds[:, :], bounds_i[:, :]))
            step(v.tensor_copy(K["iota"][:, :], K["iota_i"][:, :]))
            step(v.tensor_copy(K["iota_p"][:, :], K["iota_pi"][:, :]))
            step(v.tensor_copy(item[:, :], item_i[:, :]))
            for t in range(TILES + 1):
                step(v.tensor_scalar(below[:, :], dst_f[:, :], float(PARTS * t), None, ALU.is_lt, ALU.add,
                                     accum_out=below_count[:, t:t + 1]))
            assert count[0] == mark_count, count[0]
            dve.wait_ge(s_pe, 1)
            step(v.tensor_copy(first[:, :], ps_b[:, 0:TILES + 1]))
            step(v.tensor_tensor(size_f[:, :], first[:, 1:TILES + 1], first[:, 0:TILES], ALU.subtract))
            step(v.tensor_scalar(size_i[:, :], size_f[:, :], float(PARTS - 1), None, ALU.add))
            step(v.tensor_scalar(size_i[:, :], size_i[:, :], 7, None, ALU.arith_shift_right))
            step(v.tensor_copy(n_items[:, :], size_i[:, :]))
            step(v.memset(zero_t[:, :], 0.0))
            step(v.tensor_tensor_scan(item_end[:, :], n_items[:, :], zero_t[:, :], 0.0, ALU.add, ALU.add))
            step(v.tensor_tensor(item_start[:, :], item_end[:, :], n_items[:, :], ALU.subtract))
            step(v.scalar_tensor_tensor(edge_base[:, :], item_start[:, :], -float(PARTS), first[:, 0:TILES],
                                        ALU.mult, ALU.add))
            shape = [ITEM_ROWS, LANES, TILES]
            it = bc(item[:, :].unsqueeze(2), shape)

            def per_tile(x):
                return bc(x.unsqueeze(1), shape)
            step(v.tensor_tensor(sel_b[:, :, :], per_tile(item_end[0:ITEM_ROWS, :]), it, ALU.is_gt))
            step(v.tensor_reduce(tile_of[:, :], sel_b[:, :, :], AX.X, ALU.add))
            step(v.tensor_scalar(tile_of[:, :], tile_of[:, :], -1.0, float(TILES), ALU.mult, ALU.add))
            step(v.tensor_scalar(tile_of[:, :], tile_of[:, :], float(TILES - 1), None, ALU.min))
            step(v.tensor_copy(tile_i[:, :], tile_of[:, :]))
            assert count[0] == mark_tile, count[0]
            step(v.tensor_tensor(sel_a[:, :, :], per_tile(item_start[0:ITEM_ROWS, :]), it, ALU.is_le))
            step(v.tensor_tensor(sel_a[:, :, :], sel_a[:, :, :], sel_b[:, :, :], ALU.mult))
            step(v.tensor_tensor(sel_b[:, :, :], sel_a[:, :, :], per_tile(edge_base[0:ITEM_ROWS, :]), ALU.mult))
            step(v.tensor_reduce(e_start[:, :], sel_b[:, :, :], AX.X, ALU.add))
            step(v.scalar_tensor_tensor(e_start[:, :], item[:, :], float(PARTS), e_start[:, :], ALU.mult, ALU.add))
            step(v.tensor_tensor(sel_b[:, :, :], sel_a[:, :, :], per_tile(first[0:ITEM_ROWS, 1:TILES + 1]),
                                 ALU.mult))
            step(v.tensor_reduce(e_end[:, :], sel_b[:, :, :], AX.X, ALU.add))
            step(v.tensor_scalar(e_read[:, :], e_start[:, :], float(EDGES), None, ALU.min))
            step(v.tensor_copy(e_read_i[:, :], e_read[:, :]))
            assert count[0] == mark_read, count[0]
            dve.wait_ge(s_read, 16 * LANES * len(fields))
            step(v.tensor_copy(f_src[:, :], raw["src"][:, :]))
            step(v.tensor_copy(f_dst[:, :], raw["dst"][:, :]))
            step(v.tensor_copy(f_et4[:, :], raw["et4"][:, :]))
            step(v.tensor_scalar(f_et9[:, :], raw["et9"][:, :], 0.0, 8.0, ALU.max, ALU.min))
            step(v.scalar_tensor_tensor(f_xt[:, :], f_src[:, :], 4.0, f_et4[:, :], ALU.mult, ALU.add))
            wide = [ITEM_ROWS, LANES, PARTS]

            def lanes(x):
                return x.rearrange("p (j e) -> p j e", e=PARTS)

            def per_item(x):
                return bc(x.unsqueeze(2), wide)
            step(v.tensor_tensor(lanes(pos[:, :]), bc(K["iota"][0:ITEM_ROWS, :].unsqueeze(1), wide),
                                 per_item(e_read[:, :]), ALU.add))
            step(v.tensor_tensor(lanes(valid[:, :]), lanes(pos[:, :]), per_item(e_start[:, :]), ALU.is_ge))
            step(v.tensor_tensor(lanes(v_end[:, :]), lanes(pos[:, :]), per_item(e_end[:, :]), ALU.is_lt))
            step(v.tensor_tensor(valid[:, :], valid[:, :], v_end[:, :], ALU.mult))
            step(v.tensor_scalar(tile_of[:, :], tile_of[:, :], float(PARTS), None, ALU.mult))
            step(v.tensor_tensor(lanes(dst_local[:, :]), lanes(f_dst[:, :]), per_item(tile_of[:, :]), ALU.subtract))
            step(v.scalar_tensor_tensor(dst_local[:, :], dst_local[:, :], 1.0, valid[:, :], ALU.add, ALU.mult))
            step(v.tensor_scalar(dst_local[:, :], dst_local[:, :], -1.0, None, ALU.add))
            assert count[0] == mark_local, count[0]
            step(v.memset(key[:, :], -1.0))
            step(v.scalar_tensor_tensor(key[:, 1:ROW + 1], f_dst[:, :], 1.0, valid[:, :], ALU.add, ALU.mult))
            assert count[0] == mark_key, count[0]
            dve.wait_ge(s_keys, 32)
            step(v.tensor_tensor(cont[:, :], key[:, 0:ROW + 1], key[:, 1:ROW + 2], ALU.is_equal))
            step(v.tensor_scalar(K["brk"][:, :], cont[:, :], -1.0, BIG, ALU.add, ALU.mult))
            step(v.tensor_scalar(last[:, :], cont[:, 1:ROW + 1], -1.0, 1.0, ALU.mult, ALU.add))
            step(v.tensor_reduce(K["row_brk"][:, 0:1], K["brk"][:, 0:ROW], AX.X, ALU.min))
            step(v.tensor_reduce(K["row_brk"][:, 1:2], K["brk"][:, 1:ROW + 1], AX.X, ALU.min))
            assert count[0] == mark_fields, count[0]
            for k, (_, to) in enumerate(moved):
                for half in range(2):
                    dve.wait_ge(s_tr, 2 * k + half + 1)
                    view = to[:, :].rearrange("p (i j) -> p j i", j=LANES)[:, 4 * half:4 * half + 4, :]
                    step(v.tensor_copy(view, ps_t[:, k % 2, half, 0:4 * ITEM_ROWS]
                                       .rearrange("p (j i) -> p j i", j=4)))

        @block.tensor
        def _(pe):
            pe.wait_ge(s_v, mark_count)
            pe.wait_ge(s_pool, 8)
            nc.tensor.matmul(ps_b[:, 0:TILES + 1], ones[0:LR, :], below_count[:, :], start=True, stop=True)\
              .then_inc(s_pe, 1)
            pe.wait_ge(s_v, mark_fields)
            for k, (frm, _) in enumerate(moved):
                if k >= 2:
                    pe.wait_ge(s_v, mark_fields + 2 * (k - 1))
                for j in range(LANES):
                    ins = nc.tensor.transpose(
                        ps_t[:, k % 2, j // 4, (j % 4) * ITEM_ROWS:(j % 4 + 1) * ITEM_ROWS],
                        frm[:, j * PARTS:(j + 1) * PARTS], K["ident"][0:ITEM_ROWS, 0:ITEM_ROWS])
                    if j % 4 == 3:
                        ins.then_inc(s_tr, 1)

        @block.scalar
        def _(act):
            for n in fields:
                act.dma_start(K["edges_" + n][0:EDGES].rearrange("(p c) -> p c", p=16),
                              arrays[n].rearrange("(p c) -> p c", p=16)).then_inc(s_pad, 16)
            act.wait_ge(s_pool, 8)
            for n in fields:
                act.dma_start(K["edges_" + n][EDGES:EDGES + PARTS].rearrange("(p c) -> p c", p=16),
                              K["zero_i"][0:16, 0:8]).then_inc(s_pad, 16)

        @block.sync
        def _(sp):
            sp.dma_start(dst_i[:, :], dst.rearrange("(p c) -> p c", p=LR)).then_inc(s_in, 16)
            sp.wait_ge(s_v, mark_tile)
            sp.dma_start(K["tiles_d"].rearrange("(p j) -> p j", j=LANES), tile_i[:, :]).then_inc(s_tile, 16)
            sp.wait_ge(s_v, mark_local)
            sp.dma_start(K["dst_rows_d"].rearrange("(p c) -> p c", c=ROW), dst_local[:, :]).then_inc(s_out, 16)
            sp.wait_ge(s_v, mark_key)
            sp.dma_start(key[1:ITEM_ROWS, 0:1], key[0:ITEM_ROWS - 1, ROW:ROW + 1]).then_inc(s_keys, 16)
            sp.dma_start(key[0:ITEM_ROWS - 1, ROW + 1:ROW + 2], key[1:ITEM_ROWS, 1:2]).then_inc(s_keys, 16)
            sp.wait_ge(s_tile, 16)
            sp.dma_start(K["tiles"][:, :], K["tiles_d"].unsqueeze(0)).then_inc(s_tile, 16)
            sp.wait_ge(s_tile, 32)
            sp.wait_ge(s_out, 16)


mark_count = 5 + TILES + 1
mark_tile = mark_count + 14
mark_read = mark_tile + 9
mark_local = mark_read + 13
mark_key = mark_local + 2
mark_fields = mark_key + 5


def edge_pass(nc, tag, table, width, index_e, K, acc, weight_e=None):
    with ExitStack() as ctx:
        m = Scope(nc, ctx, tag)
        ring = m.sb("ring", [PARTS, SLOTS, width])
        hot = m.sb("hot", [PARTS, SLOTS, PARTS])
        stage = m.sb("stage", [PARTS, 2, HALF], I32)
        per_bank = 512 // width
        BANKS = 8
        ps = m.ps("ps", [PARTS, BANKS, 512])
        s_row = [m.sem(f"s_row{j}") for j in range(SLOTS)]
        s_stage, s_gate, s_hot, s_mm, s_add, s_zero = (
            m.sem(n) for n in ("s_stage", "s_gate", "s_hot", "s_mm", "s_add", "s_zero"))
        block = ctx.enter_context(nc.Block())
        LOOPS = ITEMS // SLOTS

        @block.gpsimd
        def _(pool):
            with pool.Fori(0, LOOPS) as i:
                for h in range(2):
                    pool.wait_ge(s_mm, i * SLOTS + HALF * h + HALF)
                    pool.sem_inc(s_gate, 1)
                    nc.gpsimd.tensor_copy(stage[:, h, :], index_e[:, bass.ds(i * SLOTS + HALF * h, HALF)])\
                      .then_inc(s_stage, 1)
                    pool.wait_ge(s_stage, 2 * i + h + 1)
                    pool.sem_inc(s_gate, 1)
                    for j in range(HALF):
                        pool.indirect_dma_start(
                            ring[:, HALF * h + j, :], None, table,
                            bass.IndirectOffsetOnAxis(ap=stage[:, h, j:j + 1], axis=0))\
                            .then_inc(s_row[HALF * h + j], 16)

        @block.vector
        def _(dve):
            v = nc.vector
            v.memset(acc[:, :, :], 0.0).then_inc(s_zero, 1)
            dve.wait_ge(s_zero, 1)
            dve.sem_inc(s_add, BANKS)
            steps = 1 if weight_e is None else 2

            def one_hot(i, h):
                dve.wait_ge(s_mm, i * SLOTS + HALF * h + HALF)
                v.tensor_tensor(
                    hot[:, HALF * h:HALF * h + HALF, :],
                    bc(K["iota"][:, :].unsqueeze(1), [PARTS, HALF, PARTS]),
                    bc(K["dst_e"][:, bass.ds(i * SLOTS + HALF * h, HALF)].unsqueeze(2), [PARTS, HALF, PARTS]),
                    ALU.is_equal).then_inc(s_hot, 1)
                if weight_e is not None:
                    dve.wait_ge(s_hot, (2 * i + h) * steps + 1)
                    v.tensor_tensor(
                        hot[:, HALF * h:HALF * h + HALF, :], hot[:, HALF * h:HALF * h + HALF, :],
                        bc(weight_e[:, bass.ds(i * SLOTS + HALF * h, HALF)].unsqueeze(2),
                           [PARTS, HALF, PARTS]), ALU.mult).then_inc(s_hot, 1)

            with dve.Fori(0, LOOPS) as i:
                one_hot(i, 0)
                one_hot(i, 1)
                for j in range(SLOTS):
                    t = dve.value_load(K["tiles"][0:1, bass.ds(i * SLOTS + j, 1)], min_val=0, max_val=TILES - 1)
                    dve.wait_ge(s_mm, i * SLOTS + j + 1 + SLOTS)
                    dve.wait_ge(s_add, i * SLOTS + j + BANKS)
                    row = acc[:, bass.ds(t, 1), :].squeeze(1)
                    v.tensor_tensor(row, ps[:, j % BANKS, 0:width], row, ALU.add).then_inc(s_add, 1)

        @block.tensor
        def _(pe):
            steps = 1 if weight_e is None else 2
            pe.sem_inc(s_mm, SLOTS)
            with pe.Fori(0, LOOPS) as i:
                for j in range(SLOTS):
                    pe.wait_ge(s_row[j], i * 16 + 16)
                    if j % HALF == 0:
                        pe.wait_ge(s_hot, (2 * i + j // HALF + 1) * steps)
                    pe.wait_ge(s_add, i * SLOTS + j + 1)
                    nc.tensor.matmul(ps[:, j % BANKS, 0:width], hot[:, j, :], ring[:, j, :],
                                     start=True, stop=True).then_inc(s_mm, 1)



class Chain:

    def __init__(self, eng, sem, per_round=0):
        self.eng, self.sem, self.per_round = eng, sem, per_round
        self.base, self.n, self.marks = 1, 0, {}
        eng.sem_inc(sem, 1)

    def round(self, i):
        self.base, self.n = i * self.per_round + 1, 0

    def op(self, f, *args, **kw):
        self.eng.wait_ge(self.sem, self.base + self.n)
        f(*args, **kw).then_inc(self.sem, 1)
        self.n += 1

    def mark(self, name):
        self.marks[name] = self.n

    def check(self):
        assert self.n == self.per_round, (self.n, self.per_round)


class NodeStage:

    def __init__(self, nc, m, n_turns, n_prods, n_acts, vec_steps, n_blocks):
        self.nc, self.m = nc, m
        self.n_turns, self.n_prods, self.n_acts, self.vec_steps = n_turns, n_prods, n_acts, vec_steps
        self.turned = m.sb("turned", [PARTS, n_blocks, GROUP, PARTS])
        self.ps_t = [m.ps(f"ps_t{k}", [PARTS, 1024]) for k in range(2)]
        self.ps_o = [m.ps(f"ps_o{k}", [PARTS, 1024]) for k in range(2)]
        self.s_vec, self.s_turn, self.s_copy, self.s_prod, self.s_act, self.s_store, self.s_stored, self.s_w = (
            m.sem(n) for n in ("s_vec", "s_turn", "s_copy", "s_prod", "s_act", "s_store", "s_stored", "s_w"))
        self.marks = None

    def prod(self, o, width=PARTS):
        return self.ps_o[o % 2][:, 0:GROUP * PARTS].rearrange("p (t d) -> p t d", d=PARTS)[:, :, 0:width]

    def group_free(self, eng, i):
        eng.wait_ge(self.s_vec, i * self.vec_steps + 1)

    def vec_reached(self, eng, i, name):
        eng.wait_ge(self.s_vec, i * self.vec_steps + self.marks[name] + 1)

    def turn(self, pe, i, k, block):
        if k >= 2:
            pe.wait_ge(self.s_copy, i * self.n_turns + k - 1)
        for q in range(GROUP):
            ins = self.nc.tensor.transpose(self.ps_t[k % 2][:, q * PARTS:(q + 1) * PARTS], block[:, q, :],
                                           self.ident[:, :])
        ins.then_inc(self.s_turn, 1)

    def copy_turned(self, act, i, k, b):
        act.wait_ge(self.s_turn, i * self.n_turns + k + 1)
        self.nc.scalar.activation(self.turned[:, b, :, :].rearrange("p t d -> p (t d)"),
                                  self.ps_t[k % 2][:, 0:GROUP * PARTS], ACT.Copy).then_inc(self.s_copy, 1)

    def multiply(self, pe, i, o, copies, terms, width=PARTS):
        pe.wait_ge(self.s_copy, i * self.n_turns + copies)
        if o >= 2:
            self.vec_reached(pe, i, f"used{o - 2}")
        for q in range(GROUP):
            for n, (b, w) in enumerate(terms):
                ins = self.nc.tensor.matmul(self.ps_o[o % 2][:, q * PARTS:q * PARTS + width],
                                            self.turned[:, b, q, :], w,
                                            start=(n == 0), stop=(n == len(terms) - 1))
        ins.then_inc(self.s_prod, 1)

    def await_product(self, dve, i, o):
        dve.wait_ge(self.s_prod, i * self.n_prods + o + 1)

    def await_act(self, dve, i, a):
        dve.wait_ge(self.s_act, i * self.n_acts + a + 1)


G3 = [PARTS, GROUP, PARTS]


def layer_norm(nc, d, st, i, a, x, out, sq, stat):
    v = nc.vector
    cols = x.shape[2]
    mean, var, rstd = stat[:, 0, :], stat[:, 1, :], stat[:, 3, :]
    shape = [PARTS, GROUP, cols]
    d.op(v.tensor_reduce, mean, x, AX.X, ALU.add)
    d.op(v.tensor_scalar, mean, mean, 1.0 / cols, None, ALU.mult)
    d.op(v.tensor_tensor, out, x, bc(mean.unsqueeze(2), shape), ALU.subtract)
    d.op(v.tensor_tensor, sq, out, out, ALU.mult)
    d.op(v.tensor_reduce, var, sq, AX.X, ALU.add)
    d.mark(f"root{a}")
    st.await_act(d.eng, i, a)
    d.op(v.reciprocal, rstd, stat[:, 2, :])
    d.op(v.tensor_tensor, out, out, bc(rstd.unsqueeze(2), shape), ALU.mult)


LN_STEPS = 7


def root_of_variance(nc, act, st, i, a, stat, eps, cols=PARTS):
    st.vec_reached(act, i, f"root{a}")
    nc.scalar.activation(stat[:, 2, :], stat[:, 1, :], ACT.Sqrt, bias=eps, scale=1.0 / cols).then_inc(st.s_act, 1)


def spread(ap):
    return ap.partition_broadcast(PARTS)


def sage(nc, tag, K, x_table, acc, in_cols, out_cols, w_self, w_agg, bias, out_table, K_ident,
         residual=None):
    with ExitStack() as ctx:
        m = Scope(nc, ctx, tag)
        nb, no = in_cols // PARTS, out_cols // PARTS
        steps = nb + 2 * no + (1 + LN_STEPS if residual is not None else 0)
        st = NodeStage(nc, m, 2 * nb, no, 1, steps, 2 * nb)
        st.ident = K_ident
        x_in = m.sb("x_in", [PARTS, GROUP, in_cols])
        mean = m.sb("mean", [PARTS, GROUP, in_cols])
        y = m.sb("y", [PARTS, GROUP, out_cols])
        w = m.sb("w", [PARTS, 2 * nb, out_cols])
        b_row = m.sb("b_row", [PARTS, out_cols])
        s_x, s_r = m.sem("s_x"), m.sem("s_r")
        if residual is not None:
            r_in = m.sb("r_in", G3)
            z = m.sb("z", G3)
            sq = m.sb("sq", G3)
            stat = m.sb("stat", [PARTS, 4, GROUP])
        result = y if residual is None else z
        block = ctx.enter_context(nc.Block())
        marks = {}

        @block.vector
        def _(dve):
            v = nc.vector
            d = Chain(dve, st.s_vec, steps)
            dve.wait_ge(st.s_w, 48)
            with dve.Fori(0, GROUPS) as i:
                d.round(i)
                for b in range(nb):
                    d.op(v.tensor_tensor, mean[:, :, b * PARTS:(b + 1) * PARTS],
                         acc[:, bass.ds(i * GROUP, GROUP), b * PARTS:(b + 1) * PARTS],
                         bc(K["inv_deg"][:, bass.ds(i * GROUP, GROUP)].unsqueeze(2), G3), ALU.mult)
                    d.mark(f"mean{b}")
                for o in range(no):
                    part = y[:, :, o * PARTS:(o + 1) * PARTS]
                    st.await_product(dve, i, o)
                    if o == 0:
                        dve.wait_ge(st.s_stored, i + 1)
                    d.op(v.tensor_tensor, part, st.prod(o),
                         bc(b_row[:, o * PARTS:(o + 1) * PARTS].unsqueeze(1), G3), ALU.add)
                    d.mark(f"used{o}")
                    d.op(v.tensor_scalar, part, part, 0.0, None, ALU.max)
                if residual is not None:
                    dve.wait_ge(s_r, 16 * (i + 1))
                    d.op(v.tensor_tensor, y[:, :, :], y[:, :, :], r_in[:, :, :], ALU.add)
                    layer_norm(nc, d, st, i, 0, y[:, :, :], z[:, :, :], sq[:, :, :], stat)
                d.check()
            marks.update(d.marks)
            st.marks = marks

        @block.tensor
        def _(pe):
            with pe.Fori(0, GROUPS) as i:
                st.group_free(pe, i)
                for b in range(nb):
                    if b == 0:
                        pe.wait_ge(s_x, 16 * (i + 1))
                    st.turn(pe, i, b, x_in[:, :, b * PARTS:(b + 1) * PARTS])
                for b in range(nb):
                    st.vec_reached(pe, i, f"mean{b}")
                    st.turn(pe, i, nb + b, mean[:, :, b * PARTS:(b + 1) * PARTS])
                for o in range(no):
                    st.multiply(pe, i, o, 2 * nb,
                                [(b, w[:, b, o * PARTS:(o + 1) * PARTS]) for b in range(2 * nb)])

        @block.scalar
        def _(act):
            act.sem_inc(st.s_stored, 1)
            with act.Fori(0, GROUPS) as i:
                st.group_free(act, i)
                for k in range(2 * nb):
                    st.copy_turned(act, i, k, k)
                if residual is not None:
                    root_of_variance(nc, act, st, i, 0, stat, K["eps"][:, 0:1])

        @block.sync
        def _(sp):
            sp.dma_start(w[:, 0:nb, :], w_self.rearrange("(b p) n -> p b n", p=PARTS)).then_inc(st.s_w, 16)
            sp.dma_start(w[:, nb:2 * nb, :], w_agg.rearrange("(b p) n -> p b n", p=PARTS)).then_inc(st.s_w, 16)
            sp.dma_start(b_row[:, :], spread(bias)).then_inc(st.s_w, 16)
            sp.wait_ge(st.s_w, 48)
            with sp.Fori(0, GROUPS) as i:
                st.group_free(sp, i)
                sp.dma_start(x_in[:, :, :], node_view(x_table, i)).then_inc(s_x, 16)
                if residual is not None:
                    sp.dma_start(r_in[:, :, :], node_view(residual, i)).then_inc(s_r, 16)
                sp.wait_ge(st.s_vec, i * steps + steps + 1)
                sp.dma_start(node_view(out_table, i), result[:, :, :]).then_inc(st.s_store, 16)
                sp.wait_ge(st.s_store, 16 * (i + 1))
                sp.sem_inc(st.s_stored, 1)


def group_of(node_array, i):
    return node_array[:, bass.ds(i * GROUP, GROUP)]


def attention_in(nc, K, I, x_table, h_table, skip_table):
    heads, c = 4, 32
    with ExitStack() as ctx:
        m = Scope(nc, ctx, "n0")
        steps = 9
        st = NodeStage(nc, m, 1, 2, 1, steps, 1)
        st.ident = K["ident"]
        x_in, h, t, skip = (m.sb(n, G3) for n in ("x_in", "h", "t", "skip"))
        w = m.sb("w", [PARTS, 2, PARTS])
        rows = m.sb("rows", [PARTS, 4, PARTS])
        s_x = m.sem("s_x")
        block = ctx.enter_context(nc.Block())

        @block.vector
        def _(dve):
            v = nc.vector
            d = Chain(dve, st.s_vec, steps)
            dve.wait_ge(st.s_w, 16 * 6)
            dve.wait_ge(st.s_stored, 1)
            v.tensor_tensor(rows[:, 2, :], rows[:, 2, :], rows[:, 3, :], ALU.add).then_inc(st.s_w, 16)
            dve.wait_ge(st.s_w, 16 * 7)
            with dve.Fori(0, GROUPS) as i:
                d.round(i)
                st.await_product(dve, i, 0)
                dve.wait_ge(st.s_stored, i + 1)
                d.op(v.tensor_copy, h[:, :, :], st.prod(0))
                d.mark("used0")
                for k, name in ((0, "score_src"), (1, "score_dst")):
                    d.op(v.tensor_tensor, t[:, :, :], h[:, :, :],
                         bc(rows[:, k, :].unsqueeze(1), G3), ALU.mult)
                    d.op(v.tensor_reduce, K["scores_tmp"][:, :, k * heads:(k + 1) * heads],
                         t[:, :, :].rearrange("p t (h c) -> p t h c", c=c), AX.X, ALU.add)
                    d.op(v.tensor_scalar, group_of(K["scores"], i)[:, :, k * heads:(k + 1) * heads],
                         K["scores_tmp"][:, :, k * heads:(k + 1) * heads], 1.0, None, ALU.mult)
                st.await_product(dve, i, 1)
                d.op(v.tensor_tensor, skip[:, :, :], st.prod(1), bc(rows[:, 2, :].unsqueeze(1), G3), ALU.add)
                d.mark("used1")
                d.op(v.tensor_copy, t[:, :, 0:heads], K["scores_tmp"][:, :, 0:heads])
                d.check()
            st.marks = dict(d.marks)

        @block.tensor
        def _(pe):
            pe.wait_ge(st.s_w, 16 * 7)
            with pe.Fori(0, GROUPS) as i:
                st.group_free(pe, i)
                pe.wait_ge(s_x, 16 * (i + 1))
                st.turn(pe, i, 0, x_in)
                for o in range(2):
                    st.multiply(pe, i, o, 1, [(0, w[:, o, :])])

        @block.scalar
        def _(act):
            act.sem_inc(st.s_stored, 1)
            with act.Fori(0, GROUPS) as i:
                st.group_free(act, i)
                st.copy_turned(act, i, 0, 0)

        @block.sync
        def _(sp):
            for to, frm in ((w[:, 0, :], I["L0_gnn_W"]), (w[:, 1, :], I["L0_gnn_skip_W"]),
                            (rows[:, 0, :], spread(I["L0_gnn_att_src"].rearrange("h c -> (h c)"))),
                            (rows[:, 1, :], spread(I["L0_gnn_att_dst"].rearrange("h c -> (h c)"))),
                            (rows[:, 2, :], spread(I["L0_gnn_gat_bias"])),
                            (rows[:, 3, :], spread(I["L0_gnn_skip_b"]))):
                sp.dma_start(to, frm).then_inc(st.s_w, 16)
            sp.wait_ge(st.s_w, 16 * 7)
            with sp.Fori(0, GROUPS) as i:
                st.group_free(sp, i)
                sp.dma_start(x_in[:, :, :], node_view(x_table, i)).then_inc(s_x, 16)
                sp.wait_ge(st.s_vec, i * steps + steps + 1)
                sp.dma_start(node_view(h_table, i), h[:, :, :]).then_inc(st.s_store, 16)
                sp.dma_start(node_view(skip_table, i), skip[:, :, :]).then_inc(st.s_store, 16)
                sp.dma_start(node_view(K["score_table"][:, 0:heads], i), t[:, :, 0:heads]).then_inc(st.s_store, 16)
                sp.wait_ge(st.s_store, 48 * (i + 1))
                sp.sem_inc(st.s_stored, 1)


def combine_self(nc, d, st, i, a, K, heads, self_w, z, m_seg, deg_b, e, scale_z, cs, ch, both):
    v = nc.vector
    score_s, score_d = self_w
    shape = [PARTS, GROUP, heads]
    seg, own = both[:, :, 0:heads], both[:, :, heads:2 * heads]
    d.op(v.tensor_tensor, e, score_s, score_d, ALU.add)
    d.op(v.scalar_tensor_tensor, own, e, 0.2, e, ALU.mult, ALU.max)
    d.op(v.tensor_scalar, scale_z, deg_b, 0.0, -BIG, ALU.is_equal, ALU.mult)
    d.op(v.tensor_tensor, seg, m_seg, bc(scale_z.unsqueeze(2), shape), ALU.add)
    d.op(v.tensor_tensor, e, seg, own, ALU.max)
    d.op(v.tensor_tensor, seg, seg, e, ALU.subtract)
    d.op(v.tensor_tensor, own, own, e, ALU.subtract)
    d.mark(f"exp{a}")
    st.await_act(d.eng, i, a)
    d.op(v.tensor_tensor, e, z, seg, ALU.mult)
    d.op(v.scalar_tensor_tensor, e, e, 1e-16, own, ALU.add, ALU.add)
    d.op(v.reciprocal, e, e)
    d.op(v.tensor_tensor, cs, seg, e, ALU.mult)
    d.op(v.tensor_tensor, ch, own, e, ALU.mult)


SELF_STEPS = 12


def attention_out(nc, K, I, acc, x_table, h_table, skip_table, out_table):
    heads, c = 4, 32
    Z, M, C4, C9 = 128, 132, 136, 140
    with ExitStack() as ctx:
        m = Scope(nc, ctx, "n1")
        steps = 7 + SELF_STEPS + 5 + LN_STEPS + 3 + LN_STEPS + 3
        st = NodeStage(nc, m, 0, 0, 3, steps, 1)
        x_in, h, skip, t, y, z = (m.sb(n, G3) for n in ("x_in", "h", "skip", "t", "y", "z"))
        aux = m.sb("aux", [PARTS, GROUP, 21])
        e, cs, ch = (m.sb(n, [PARTS, GROUP, heads]) for n in ("e", "cs", "ch"))
        both = m.sb("both", [PARTS, GROUP, 2 * heads])
        sz = m.sb("sz", [PARTS, GROUP])
        deg = m.sb("deg", [PARTS, GROUP])
        rec = m.sb("rec", [PARTS, GROUP, 5])
        own = m.sb("own", [PARTS, GROUP, 2 * heads])
        stat = m.sb("stat", [PARTS, 4, GROUP])
        rows = m.sb("rows", [PARTS, 2, PARTS])
        s_x = m.sem("s_x")
        block = ctx.enter_context(nc.Block())

        @block.vector
        def _(dve):
            v = nc.vector
            d = Chain(dve, st.s_vec, steps)
            dve.wait_ge(st.s_w, 32)
            with dve.Fori(0, GROUPS) as i:
                d.round(i)
                d.op(v.tensor_scalar, aux[:, :, :], group_of(acc, i)[:, :, Z:Z + 21], 1.0, None, ALU.mult)
                d.op(v.tensor_scalar, own[:, :, :], group_of(K["scores"], i)[:, :, :], 1.0, None, ALU.mult)
                d.op(v.tensor_reduce, deg[:, :], aux[:, :, 12:21], AX.X, ALU.add)
                d.op(v.tensor_scalar, rec[:, :, 0:4], aux[:, :, 8:12], 1.0, None, ALU.max)
                d.op(v.tensor_scalar, rec[:, :, 4], deg[:, :], 1.0, None, ALU.max)
                d.op(v.reciprocal, rec[:, :, :], rec[:, :, :])
                d.op(v.tensor_scalar, group_of(K["inv4"], i), rec[:, :, 0:4], 1.0, None, ALU.mult)
                combine_self(nc, d, st, i, 0, K, heads, (own[:, :, 0:heads], own[:, :, heads:2 * heads]),
                             aux[:, :, 0:4], aux[:, :, 4:8], deg[:, :], e[:, :, :], sz[:, :],
                             cs[:, :, :], ch[:, :, :], both[:, :, :])
                dve.wait_ge(s_x, 48 * (i + 1))
                shape = [PARTS, GROUP * heads, c]

                def by_head(x):
                    return x.rearrange("p t (h c) -> p (t h) c", c=c)

                def factor(x):
                    return bc(x[:, :, :].rearrange("p t h -> p (t h)").unsqueeze(2), shape)
                d.op(v.tensor_scalar, t[:, :, :], group_of(acc, i)[:, :, 0:PARTS], 1.0, None, ALU.mult)
                d.op(v.tensor_tensor, by_head(t[:, :, :]), by_head(t[:, :, :]), factor(cs), ALU.mult)
                d.op(v.tensor_tensor, by_head(h[:, :, :]), by_head(h[:, :, :]), factor(ch), ALU.mult)
                d.op(v.tensor_tensor, t[:, :, :], t[:, :, :], h[:, :, :], ALU.add)
                d.op(v.tensor_tensor, t[:, :, :], t[:, :, :], skip[:, :, :], ALU.add)
                layer_norm(nc, d, st, i, 1, t[:, :, :], y[:, :, :], z[:, :, :], stat)
                d.op(v.tensor_tensor, y[:, :, :], y[:, :, :], bc(rows[:, 0, :].unsqueeze(1), G3), ALU.mult)
                d.op(v.tensor_tensor, y[:, :, :], y[:, :, :], bc(rows[:, 1, :].unsqueeze(1), G3), ALU.add)
                d.op(v.tensor_tensor, t[:, :, :], y[:, :, :], x_in[:, :, :], ALU.add)
                dve.wait_ge(st.s_stored, i + 1)
                layer_norm(nc, d, st, i, 2, t[:, :, :], y[:, :, :], z[:, :, :], stat)
                d.op(v.tensor_scalar, group_of(K["inv_deg"], i), rec[:, :, 4], 1.0, None, ALU.mult)
                d.op(v.tensor_scalar, group_of(K["counts"], i)[:, :, 0:9], aux[:, :, 12:21], 1.0, None, ALU.mult)
                d.op(v.tensor_scalar, group_of(K["counts"], i)[:, :, 9], deg[:, :], 1.0, None, ALU.mult)
                d.check()
            st.marks = dict(d.marks)

        @block.scalar
        def _(act):
            act.sem_inc(st.s_stored, 1)
            with act.Fori(0, GROUPS) as i:
                st.vec_reached(act, i, "exp0")
                nc.scalar.activation(both[:, :, :], both[:, :, :], ACT.Exp).then_inc(st.s_act, 1)
                root_of_variance(nc, act, st, i, 1, stat, K["eps"][:, 0:1])
                root_of_variance(nc, act, st, i, 2, stat, K["eps"][:, 0:1])

        @block.sync
        def _(sp):
            sp.dma_start(rows[:, 0, :], spread(I["L0_gnn_ln_g"])).then_inc(st.s_w, 16)
            sp.dma_start(rows[:, 1, :], spread(I["L0_gnn_ln_b"])).then_inc(st.s_w, 16)
            with sp.Fori(0, GROUPS) as i:
                st.group_free(sp, i)
                sp.dma_start(x_in[:, :, :], node_view(x_table, i)).then_inc(s_x, 16)
                sp.dma_start(h[:, :, :], node_view(h_table, i)).then_inc(s_x, 16)
                sp.dma_start(skip[:, :, :], node_view(skip_table, i)).then_inc(s_x, 16)
                sp.wait_ge(st.s_vec, i * steps + steps + 1)
                sp.dma_start(node_view(out_table, i), y[:, :, :]).then_inc(st.s_store, 16)
                sp.wait_ge(st.s_store, 16 * (i + 1))
                sp.sem_inc(st.s_stored, 1)


def gated_update(nc, K, I, acc, x_table, out_table):
    with ExitStack() as ctx:
        m = Scope(nc, ctx, "n4")
        steps = 14 + LN_STEPS
        X, A, C, M = range(4)
        st = NodeStage(nc, m, 4, 5, 4, steps, 4)
        st.ident = K["ident"]
        x_in, agg, cnt, msg, r, z, n_, y, sq = (m.sb(n, G3) for n in
                                                ("x_in", "agg", "cnt", "msg", "r", "z", "n", "y", "sq"))
        w_msg = m.sb("w_msg", [PARTS, 2, PARTS])
        w_ih = m.sb("w_ih", [PARTS, 3 * PARTS])
        w_hh = m.sb("w_hh", [PARTS, 3 * PARTS])
        b_ih = m.sb("b_ih", [PARTS, 3, PARTS])
        b_hh = m.sb("b_hh", [PARTS, 3, PARTS])
        stat = m.sb("stat", [PARTS, 4, GROUP])
        s_x, s_init = m.sem("s_x"), m.sem("s_init")
        block = ctx.enter_context(nc.Block())

        @block.vector
        def _(dve):
            v = nc.vector
            v.memset(cnt[:, :, :], 0.0).then_inc(s_init, 1)
            v.memset(w_msg[:, 1, :], 0.0).then_inc(s_init, 1)
            dve.wait_ge(st.s_w, 16 * 7)
            v.tensor_tensor(b_ih[:, 0:2, :], b_ih[:, 0:2, :], b_hh[:, 0:2, :], ALU.add).then_inc(s_init, 1)
            dve.wait_ge(s_init, 3)
            d = Chain(dve, st.s_vec, steps)
            with dve.Fori(0, GROUPS) as i:
                d.round(i)
                d.op(v.tensor_scalar, agg[:, :, :], group_of(acc, i), 1.0, None, ALU.mult)
                d.op(v.tensor_scalar, cnt[:, :, 0:10], group_of(K["counts"], i), 1.0, None, ALU.mult)
                d.mark("sums")
                st.await_product(dve, i, 0)
                d.op(v.tensor_copy, msg[:, :, :], st.prod(0))
                d.mark("used0")
                for o, g in ((1, r), (2, z)):
                    st.await_product(dve, i, o)
                    d.op(v.tensor_tensor, g[:, :, :], st.prod(o), bc(b_ih[:, o - 1, :].unsqueeze(1), G3), ALU.add)
                    d.mark(f"used{o}")
                st.await_product(dve, i, 3)
                d.op(v.tensor_tensor, n_[:, :, :], st.prod(3), bc(b_hh[:, 2, :].unsqueeze(1), G3), ALU.add)
                d.mark("used3")
                st.await_act(dve, i, 0)
                d.op(v.tensor_tensor, n_[:, :, :], n_[:, :, :], r[:, :, :], ALU.mult)
                d.op(v.tensor_tensor, n_[:, :, :], n_[:, :, :], bc(b_ih[:, 2, :].unsqueeze(1), G3), ALU.add)
                st.await_product(dve, i, 4)
                d.op(v.tensor_tensor, n_[:, :, :], st.prod(4), n_[:, :, :], ALU.add)
                d.mark("used4")
                st.await_act(dve, i, 1)
                st.await_act(dve, i, 2)
                d.op(v.tensor_scalar, r[:, :, :], z[:, :, :], -1.0, 1.0, ALU.mult, ALU.add)
                d.op(v.tensor_tensor, r[:, :, :], r[:, :, :], n_[:, :, :], ALU.mult)
                d.op(v.tensor_tensor, z[:, :, :], z[:, :, :], x_in[:, :, :], ALU.mult)
                d.op(v.tensor_tensor, r[:, :, :], r[:, :, :], z[:, :, :], ALU.add)
                d.op(v.tensor_tensor, r[:, :, :], r[:, :, :], x_in[:, :, :], ALU.add)
                dve.wait_ge(st.s_stored, i + 1)
                layer_norm(nc, d, st, i, 3, r[:, :, :], y[:, :, :], sq[:, :, :], stat)
                d.check()
            st.marks = dict(d.marks)

        @block.tensor
        def _(pe):
            pe.wait_ge(st.s_w, 16 * 7)
            with pe.Fori(0, GROUPS) as i:
                st.group_free(pe, i)
                pe.wait_ge(s_x, 16 * (i + 1))
                st.turn(pe, i, 0, x_in)
                st.vec_reached(pe, i, "sums")
                st.turn(pe, i, 1, agg)
                st.turn(pe, i, 2, cnt)
                st.multiply(pe, i, 0, 3, [(A, w_msg[:, 0, :]), (C, w_msg[:, 1, :])])
                st.vec_reached(pe, i, "used0")
                st.turn(pe, i, 3, msg)
                for o in range(2):
                    cols = slice(o * PARTS, (o + 1) * PARTS)
                    st.multiply(pe, i, 1 + o, 4, [(M, w_ih[:, cols]), (X, w_hh[:, cols])])
                st.multiply(pe, i, 3, 4, [(X, w_hh[:, 2 * PARTS:3 * PARTS])])
                st.multiply(pe, i, 4, 4, [(M, w_ih[:, 2 * PARTS:3 * PARTS])])

        @block.scalar
        def _(act):
            a = nc.scalar
            act.sem_inc(st.s_stored, 1)
            with act.Fori(0, GROUPS) as i:
                st.group_free(act, i)
                for k, b in enumerate((X, A, C, M)):
                    st.copy_turned(act, i, k, b)
                st.vec_reached(act, i, "used1")
                a.activation(r[:, :, :], r[:, :, :], ACT.Sigmoid).then_inc(st.s_act, 1)
                st.vec_reached(act, i, "used2")
                a.activation(z[:, :, :], z[:, :, :], ACT.Sigmoid).then_inc(st.s_act, 1)
                st.vec_reached(act, i, "used4")
                a.activation(n_[:, :, :], n_[:, :, :], ACT.Tanh).then_inc(st.s_act, 1)
                root_of_variance(nc, act, st, i, 3, stat, K["eps"][:, 0:1])

        @block.sync
        def _(sp):
            sp.dma_start(w_msg[:, 0, :], I["L2_W_msg_T"]).then_inc(st.s_w, 16)
            sp.dma_start(w_ih[:, :], I["L2_W_ih_T"]).then_inc(st.s_w, 16)
            sp.dma_start(w_hh[:, :], I["L2_W_hh_T"]).then_inc(st.s_w, 16)
            sp.dma_start(b_ih[:, :, :].rearrange("p a b -> p (a b)"), spread(I["L2_gnn_b_ih"])).then_inc(st.s_w, 16)
            sp.dma_start(b_hh[:, :, :].rearrange("p a b -> p (a b)"), spread(I["L2_gnn_b_hh"])).then_inc(st.s_w, 16)
            sp.wait_ge(s_init, 2)
            sp.dma_start(w_msg[0:9, 1, :], I["L2_gnn_edge_embed"]).then_inc(st.s_w, 16)
            sp.dma_start(w_msg[9:10, 1, :], I["L2_gnn_b_msg"].unsqueeze(0)).then_inc(st.s_w, 16)
            with sp.Fori(0, GROUPS) as i:
                st.group_free(sp, i)
                sp.dma_start(x_in[:, :, :], node_view(x_table, i)).then_inc(s_x, 16)
                sp.wait_ge(st.s_vec, i * steps + steps + 1)
                sp.dma_start(node_view(out_table, i), y[:, :, :]).then_inc(st.s_store, 16)
                sp.wait_ge(st.s_store, 16 * (i + 1))
                sp.sem_inc(st.s_stored, 1)


def score_pass(nc, tag, K, score_table, heads, node_vals, cols, src_e, vals_e):
    with ExitStack() as ctx:
        m = Scope(nc, ctx, tag)
        ring = m.sb("ring", [PARTS, SLOTS, heads])
        stage = m.sb("stage", [PARTS, 2, HALF], I32)
        rows = m.sb("rows", [PARTS, 2, HALF * PARTS])
        hot_t = m.sb("hot_t", [PARTS, 2, HALF, PARTS])
        ps = m.ps("ps", [PARTS, 2, 512])
        s_row = [m.sem(f"s_row{h}") for h in range(2)]
        s_dst = [m.sem(f"s_dst{h}") for h in range(2)]
        s_stage, s_gate, s_hot, s_mm, s_src, s_val, s_agate = (
            m.sem(n) for n in ("s_stage", "s_gate", "s_hot", "s_mm", "s_src", "s_val", "s_agate"))
        block = ctx.enter_context(nc.Block())
        LOOPS = ITEMS // SLOTS

        @block.gpsimd
        def _(pool):
            with pool.Fori(0, LOOPS) as i:
                for h in range(2):
                    pool.wait_ge(s_src, 2 * i + h + 1)
                    pool.sem_inc(s_gate, 1)
                    nc.gpsimd.tensor_copy(stage[:, h, :], K["src_e"][:, bass.ds(i * SLOTS + HALF * h, HALF)])\
                      .then_inc(s_stage, 1)
                    pool.wait_ge(s_stage, 2 * i + h + 1)
                    pool.sem_inc(s_gate, 1)
                    for j in range(HALF):
                        pool.indirect_dma_start(
                            ring[:, HALF * h + j, :], None, score_table,
                            bass.IndirectOffsetOnAxis(ap=stage[:, h, j:j + 1], axis=0)).then_inc(s_row[h], 16)

        @block.sync
        def _(sp):
            with sp.Fori(0, LOOPS) as i:
                for h in range(2):
                    sp.wait_ge(s_hot, 2 * i + h + 1)
                    sp.dma_start(rows[:, h, :], K["dst_rows_d"][bass.ds((i * SLOTS + HALF * h) * PARTS, HALF * PARTS)]
                                 .partition_broadcast(PARTS)).then_inc(s_dst[h], 16)

        @block.vector
        def _(dve):
            dve.sem_inc(s_hot, 2)
            with dve.Fori(0, LOOPS) as i:
                for h in range(2):
                    dve.wait_ge(s_dst[h], 16 * (i + 1))
                    dve.wait_ge(s_mm, i * SLOTS + HALF * h + HALF)
                    nc.vector.tensor_scalar(hot_t[:, h, :, :].rearrange("p j e -> p (j e)"), rows[:, h, :],
                                            K["iota_p"][:, 0:1], None, ALU.is_equal).then_inc(s_hot, 1)

        @block.tensor
        def _(pe):
            pe.sem_inc(s_mm, SLOTS)
            with pe.Fori(0, LOOPS) as i:
                for h in range(2):
                    for j in range(HALF):
                        t = pe.value_load(K["tiles"][0:1, bass.ds(i * SLOTS + HALF * h + j, 1)],
                                          min_val=0, max_val=TILES - 1)
                        if j == 0:
                            pe.wait_ge(s_hot, 2 * i + h + 3)
                            pe.wait_ge(s_val, 2 * i + h + 1)
                        nc.tensor.matmul(ps[:, h, j * cols:(j + 1) * cols], hot_t[:, h, j, :],
                                         node_vals[:, bass.ds(t, 1), :].squeeze(1),
                                         start=True, stop=True).then_inc(s_mm, 1)

        @block.scalar
        def _(act):
            act.sem_inc(s_src, 2)
            act.sem_inc(s_val, 2)
            with act.Fori(0, LOOPS) as i:
                for h in range(2):
                    at = bass.ds(i * SLOTS + HALF * h, HALF)
                    act.wait_ge(s_row[h], 16 * HALF * (i + 1))
                    act.sem_inc(s_agate, 1)
                    nc.scalar.activation(src_e[:, at, :], ring[:, HALF * h:HALF * h + HALF, :], ACT.Copy)\
                      .then_inc(s_src, 1)
                    act.wait_ge(s_mm, i * SLOTS + HALF * h + HALF + SLOTS)
                    act.sem_inc(s_agate, 1)
                    nc.scalar.activation(vals_e[:, at, :], ps[:, h, 0:HALF * cols]
                                         .rearrange("p (j c) -> p j c", c=cols), ACT.Copy).then_inc(s_val, 1)


def softmax_numerators(nc, tag, K, heads, src_e, dst_e, w_e, max_e):
    with ExitStack() as ctx:
        m = Scope(nc, ctx, tag)
        score = m.sb("score", [PARTS, ITEMS, heads])
        rows_a = m.sb("rows_a", [ITEM_ROWS, heads, ROW])
        rows_b = m.sb("rows_b", [ITEM_ROWS, heads, ROW])
        ends = m.sb("ends", [ITEM_ROWS, 2, heads])
        ends_t = m.sb("ends_t", [heads, 2, ITEM_ROWS])
        carry_t = m.sb("carry_t", [heads, ITEM_ROWS + 2])
        carry = m.sb("carry", [ITEM_ROWS, 2, heads])
        ps = m.ps("ps", [PARTS, 4, 512])
        ps_s = m.ps("ps_s", [PARTS, 512])
        s_v, s_pe, s_exp = m.sem("s_v"), m.sem("s_pe"), m.sem("s_exp")
        marks, turns = {}, [0]
        block = ctx.enter_context(nc.Block())
        QUARTERS = 2 * heads
        E1, C1, E2, C2 = QUARTERS + 1, QUARTERS + 2, QUARTERS + 3, QUARTERS + 4

        @block.vector
        def _(dve):
            v = nc.vector
            d = Chain(dve, s_v)
            d.op(v.tensor_tensor, score[:, :, :], src_e, dst_e, ALU.add)
            d.op(v.scalar_tensor_tensor, score[:, :, :], score[:, :, :], 0.2, score[:, :, :], ALU.mult, ALU.max)
            d.mark("score")
            for q in range(QUARTERS):
                hd, half = q // 2, q % 2
                dve.wait_ge(s_pe, q + 1)
                d.op(v.tensor_copy, rows_a[:, hd, half * 512:half * 512 + 512], ps[0:ITEM_ROWS, q % 4, :])
                d.mark(f"forth{q}")
            for way in range(2):
                brk = K["brk"][:, 0:ROW] if way == 0 else K["brk"][:, 1:ROW + 1][:, ::-1]
                for hd in range(heads):
                    if way == 0:
                        a, b = rows_a[:, hd, :], rows_b[:, hd, :]
                    else:
                        a, b = rows_b[:, hd, :][:, ::-1], rows_a[:, hd, :][:, ::-1]
                    d.op(v.tensor_tensor_scan, b, brk, a, -BIG, ALU.add, ALU.max)
                    d.op(v.tensor_copy, ends[:, 0, hd:hd + 1], b[:, ROW - 1:ROW])
                    d.op(v.tensor_copy, ends[:, 1, hd:hd + 1], K["row_brk"][:, way:way + 1])
                d.mark(f"ends{way}")
                dve.wait_ge(s_pe, (E1, E2)[way])
                d.op(v.tensor_copy, ends_t[:, :, :], ps_s[0:heads, 0:2 * ITEM_ROWS]
                     .rearrange("p (a r) -> p a r", a=2))
                d.op(v.memset, carry_t[:, :], -BIG)
                if way == 0:
                    d.op(v.tensor_tensor_scan, carry_t[:, 1:ITEM_ROWS + 1], ends_t[:, 1, :], ends_t[:, 0, :],
                         -BIG, ALU.add, ALU.max)
                else:
                    d.op(v.tensor_tensor_scan, carry_t[:, 1:ITEM_ROWS + 1][:, ::-1], ends_t[:, 1, :][:, ::-1],
                         ends_t[:, 0, :][:, ::-1], -BIG, ALU.add, ALU.max)
                d.mark(f"carry{way}")
                dve.wait_ge(s_pe, (C1, C2)[way])
                d.op(v.tensor_copy, carry[:, way, :], ps_s[0:ITEM_ROWS, 256:256 + heads])
                for hd in range(heads):
                    if way == 0:
                        a, b = rows_a[:, hd, :], rows_b[:, hd, :]
                    else:
                        a, b = rows_b[:, hd, :][:, ::-1], rows_a[:, hd, :][:, ::-1]
                    d.op(v.tensor_tensor_scan, b, brk, a, carry[:, way, hd:hd + 1], ALU.add, ALU.max)
            d.mark("max")
            for q in range(QUARTERS):
                hd, half = q // 2, q % 2
                dve.wait_ge(s_pe, C2 + q + 1)
                d.op(v.tensor_copy,
                     max_e[:, :, hd].rearrange("p (i j) -> p j i", j=LANES)[:, 4 * half:4 * half + 4, :],
                     ps[:, q % 4, 0:4 * ITEM_ROWS].rearrange("p (j i) -> p j i", j=4))
                d.mark(f"back{q}")
            d.op(v.tensor_tensor, w_e, score[:, :, :], max_e, ALU.subtract)
            d.mark("shifted")
            d.op(v.tensor_tensor, max_e, max_e, bc(K["last_e"][:, :].unsqueeze(2), [PARTS, ITEMS, heads]), ALU.mult)
            marks.update(d.marks)

        @block.tensor
        def _(pe):
            pe.wait_ge(s_v, marks["score"] + 1)
            for q in range(QUARTERS):
                hd, half = q // 2, q % 2
                if q >= 4:
                    pe.wait_ge(s_v, marks[f"forth{q - 4}"] + 1)
                for j in range(4):
                    view = score[:, :, hd].rearrange("p (i j) -> p j i", j=LANES)
                    ins = nc.tensor.transpose(ps[0:ITEM_ROWS, q % 4, j * PARTS:(j + 1) * PARTS],
                                              view[:, 4 * half + j, :], K["ident"][:, :])
                ins.then_inc(s_pe, 1)
            for way in range(2):
                pe.wait_ge(s_v, marks[f"ends{way}"] + 1)
                for a in range(2):
                    ins = nc.tensor.transpose(ps_s[0:heads, a * ITEM_ROWS:(a + 1) * ITEM_ROWS], ends[:, a, :],
                                              K["ident"][0:ITEM_ROWS, 0:ITEM_ROWS])
                ins.then_inc(s_pe, 1)
                pe.wait_ge(s_v, marks[f"carry{way}"] + 1)
                off = 0 if way == 0 else 2
                nc.tensor.transpose(ps_s[0:ITEM_ROWS, 256:256 + heads], carry_t[:, off:off + ITEM_ROWS],
                                    K["ident"][0:heads, 0:heads]).then_inc(s_pe, 1)
            pe.wait_ge(s_v, marks["max"] + 1)
            for q in range(QUARTERS):
                hd, half = q // 2, q % 2
                if q >= 4:
                    pe.wait_ge(s_v, marks[f"back{q - 4}"] + 1)
                for j in range(4):
                    at = (4 * half + j) * PARTS
                    ins = nc.tensor.transpose(ps[:, q % 4, j * ITEM_ROWS:(j + 1) * ITEM_ROWS],
                                              rows_a[:, hd, at:at + PARTS], K["ident"][0:ITEM_ROWS, 0:ITEM_ROWS])
                ins.then_inc(s_pe, 1)

        @block.scalar
        def _(act):
            act.wait_ge(s_v, marks["shifted"] + 1)
            nc.scalar.activation(w_e, w_e, ACT.Exp).then_inc(s_exp, 1)
            act.wait_ge(s_exp, 1)


def attention_pass(nc, K, h_table, w_e, max_e, acc):
    heads, c = 4, 32
    W = PARTS + 2 * heads + 13
    with ExitStack() as ctx:
        m = Scope(nc, ctx, "p0")
        ring = m.sb("ring", [PARTS, SLOTS, PARTS])
        msg = m.sb("msg", [PARTS, SLOTS, W])
        hot = m.sb("hot", [PARTS, SLOTS, PARTS])
        stage = m.sb("stage", [PARTS, 2, HALF], I32)
        BANKS = 8
        ps = m.ps("ps", [PARTS, BANKS, 512])
        s_row = [m.sem(f"s_row{h}") for h in range(2)]
        s_stage, s_gate, s_hot, s_mm, s_add, s_zero, s_msg, s_aux, s_agate = (
            m.sem(n) for n in ("s_stage", "s_gate", "s_hot", "s_mm", "s_add", "s_zero", "s_msg", "s_aux", "s_agate"))
        block = ctx.enter_context(nc.Block())
        LOOPS = ITEMS // SLOTS

        @block.gpsimd
        def _(pool):
            with pool.Fori(0, LOOPS) as i:
                for h in range(2):
                    pool.wait_ge(s_msg, 2 * i + h + 1)
                    pool.sem_inc(s_gate, 1)
                    nc.gpsimd.tensor_copy(stage[:, h, :], K["src_e"][:, bass.ds(i * SLOTS + HALF * h, HALF)])\
                      .then_inc(s_stage, 1)
                    pool.wait_ge(s_stage, 2 * i + h + 1)
                    pool.sem_inc(s_gate, 1)
                    for j in range(HALF):
                        pool.indirect_dma_start(
                            ring[:, HALF * h + j, :], None, h_table,
                            bass.IndirectOffsetOnAxis(ap=stage[:, h, j:j + 1], axis=0)).then_inc(s_row[h], 16)

        @block.scalar
        def _(act):
            act.sem_inc(s_aux, 2)
            with act.Fori(0, LOOPS) as i:
                for h in range(2):
                    at = bass.ds(i * SLOTS + HALF * h, HALF)
                    half = slice(HALF * h, HALF * h + HALF)
                    act.wait_ge(s_mm, i * SLOTS + HALF * h + HALF)
                    act.sem_inc(s_agate, 1)
                    nc.scalar.activation(msg[:, half, PARTS:PARTS + heads], w_e[:, at, :], ACT.Copy)\
                      .then_inc(s_aux, 1)
                    nc.scalar.activation(msg[:, half, PARTS + heads:PARTS + 2 * heads], max_e[:, at, :], ACT.Copy)\
                      .then_inc(s_aux, 1)

        @block.vector
        def _(dve):
            v = nc.vector
            v.memset(acc[:, :, :], 0.0).then_inc(s_zero, 1)
            dve.wait_ge(s_zero, 1)
            dve.sem_inc(s_add, BANKS)
            dve.sem_inc(s_msg, 2)

            with dve.Fori(0, LOOPS) as i:
                for h in range(2):
                    at = bass.ds(i * SLOTS + HALF * h, HALF)
                    half = slice(HALF * h, HALF * h + HALF)
                    dve.wait_ge(s_mm, i * SLOTS + HALF * h + HALF)
                    v.tensor_tensor(hot[:, half, :], bc(K["iota"][:, :].unsqueeze(1), [PARTS, HALF, PARTS]),
                                    bc(K["dst_e"][:, at].unsqueeze(2), [PARTS, HALF, PARTS]),
                                    ALU.is_equal).then_inc(s_hot, 1)
                    for at_col, n, types in ((PARTS + 2 * heads, 4, K["et4_e"]), (PARTS + 2 * heads + 4, 9, K["et9_e"])):
                        v.tensor_tensor(msg[:, half, at_col:at_col + n],
                                        bc(K["iota"][:, 0:n].unsqueeze(1), [PARTS, HALF, n]),
                                        bc(types[:, at].unsqueeze(2), [PARTS, HALF, n]),
                                        ALU.is_equal).then_inc(s_hot, 1)
                    dve.wait_ge(s_row[h], 16 * HALF * (i + 1))
                    v.tensor_tensor(
                        msg[:, half, 0:PARTS].rearrange("p j (h c) -> p j h c", c=c),
                        ring[:, half, :].rearrange("p j (h c) -> p j h c", c=c),
                        bc(w_e[:, at, :].unsqueeze(3), [PARTS, HALF, heads, c]), ALU.mult).then_inc(s_msg, 1)
                for j in range(SLOTS):
                    t = dve.value_load(K["tiles"][0:1, bass.ds(i * SLOTS + j, 1)], min_val=0, max_val=TILES - 1)
                    dve.wait_ge(s_mm, i * SLOTS + j + 1 + SLOTS)
                    dve.wait_ge(s_add, i * SLOTS + j + BANKS)
                    row = acc[:, bass.ds(t, 1), :].squeeze(1)
                    v.tensor_tensor(row, ps[:, j % BANKS, 0:W], row, ALU.add).then_inc(s_add, 1)

        @block.tensor
        def _(pe):
            pe.sem_inc(s_mm, SLOTS)
            with pe.Fori(0, LOOPS) as i:
                for j in range(SLOTS):
                    if j % HALF == 0:
                        h = j // HALF
                        pe.wait_ge(s_hot, 3 * (2 * i + h + 1))
                        pe.wait_ge(s_msg, 2 * i + h + 3)
                        pe.wait_ge(s_aux, 2 * (2 * i + h + 1) + 2)
                    pe.wait_ge(s_add, i * SLOTS + j + 1)
                    nc.tensor.matmul(ps[:, j % BANKS, 0:W], hot[:, j, :], msg[:, j, :],
                                     start=True, stop=True).then_inc(s_mm, 1)


def copy_in(nc, K, x, table):
    with ExitStack() as ctx:
        m = Scope(nc, ctx, "ci")
        rest = NODE_ROWS - NODES
        zero = m.sb("zero", [rest, PARTS])
        s_z, s_d = m.sem("s_z"), m.sem("s_d")
        block = ctx.enter_context(nc.Block())

        @block.vector
        def _(dve):
            nc.vector.memset(zero[:, :], 0.0).then_inc(s_z, 1)
            nc.vector.memset(K["eps"][:, :], 1e-5).then_inc(s_z, 1)

        @block.sync
        def _(sp):
            sp.dma_start(table[0:NODES, :].rearrange("(p r) d -> p (r d)", p=125),
                         x.rearrange("(p r) d -> p (r d)", p=125)).then_inc(s_d, 16)
            sp.wait_ge(s_z, 2)
            sp.dma_start(table[NODES:NODE_ROWS, :], zero[:, :]).then_inc(s_d, 16)
            sp.wait_ge(s_d, 32)


def copy_out(nc, table, out):
    with ExitStack() as ctx:
        m = Scope(nc, ctx, "co")
        s_d = m.sem("s_d")
        block = ctx.enter_context(nc.Block())

        @block.sync
        def _(sp):
            sp.dma_start(out.rearrange("(p r) d -> p (r d)", p=125),
                         table[0:NODES, :].rearrange("(p r) d -> p (r d)", p=125)).then_inc(s_d, 16)
            sp.wait_ge(s_d, 16)


def attention2_in(nc, K, I, xs_table, score_table):
    heads, c = 2, 256
    with ExitStack() as ctx:
        m = Scope(nc, ctx, "n6")
        steps = 4
        st = NodeStage(nc, m, 2, 1, 0, steps, 2)
        st.ident = K["ident"]
        x_in = m.sb("x_in", [PARTS, GROUP, c])
        s_sb = m.sb("s_sb", [PARTS, GROUP, 4])
        w = m.sb("w", [PARTS, 2, heads * c])
        att = m.sb("att", [PARTS, 2, heads * c])
        t = m.sb("t", [PARTS, 2, heads * c])
        va = m.sb("va", [PARTS, 2, 2 * heads])
        s_x, s_va = m.sem("s_x"), m.sem("s_va")
        block = ctx.enter_context(nc.Block())

        @block.vector
        def _(dve):
            v = nc.vector
            dve.wait_ge(st.s_w, 48)
            done = 0
            for k in range(2):
                dve.wait_ge(s_va, done) if done else None
                v.tensor_tensor(t[:, :, :], w[:, :, :], bc(att[:, k, :].unsqueeze(1), [PARTS, 2, heads * c]),
                                ALU.mult).then_inc(s_va, 1)
                dve.wait_ge(s_va, done + 1)
                v.tensor_reduce(va[:, :, k * heads:(k + 1) * heads],
                                t[:, :, :].rearrange("p b (h c) -> p b h c", c=c), AX.X, ALU.add).then_inc(s_va, 1)
                done += 2
            d = Chain(dve, st.s_vec, steps)
            with dve.Fori(0, GROUPS) as i:
                d.round(i)
                st.await_product(dve, i, 0)
                dve.wait_ge(st.s_stored, i + 1)
                d.op(v.tensor_copy, s_sb[:, :, :], st.prod(0, 4))
                d.mark("used0")
                d.op(v.tensor_scalar, group_of(K["own"], i), s_sb[:, :, :], 1.0, None, ALU.mult)
                d.op(v.tensor_scalar, group_of(K["expand"], i)[:, :, 0:2], s_sb[:, :, 2:4], 1.0, None, ALU.mult)
                d.op(v.tensor_scalar, group_of(K["expand"], i)[:, :, 2:6], group_of(K["inv4"], i), 1.0, None, ALU.mult)
                d.check()
            st.marks = dict(d.marks)

        @block.tensor
        def _(pe):
            pe.wait_ge(s_va, 4)
            with pe.Fori(0, GROUPS) as i:
                st.group_free(pe, i)
                pe.wait_ge(s_x, 16 * (i + 1))
                for b in range(2):
                    st.turn(pe, i, b, x_in[:, :, b * PARTS:(b + 1) * PARTS])
                st.multiply(pe, i, 0, 2, [(b, va[:, b, :]) for b in range(2)], width=4)

        @block.scalar
        def _(act):
            act.sem_inc(st.s_stored, 1)
            with act.Fori(0, GROUPS) as i:
                st.group_free(act, i)
                for k in range(2):
                    st.copy_turned(act, i, k, k)

        @block.sync
        def _(sp):
            sp.dma_start(w[:, :, :], I["L3_gnn_gat_W"].rearrange("(b p) n -> p b n", p=PARTS)).then_inc(st.s_w, 16)
            for k, n in enumerate(("L3_gnn_gat_att_src", "L3_gnn_gat_att_dst")):
                sp.dma_start(att[:, k, :], spread(I[n].rearrange("h c -> (h c)"))).then_inc(st.s_w, 16)
            with sp.Fori(0, GROUPS) as i:
                st.group_free(sp, i)
                sp.dma_start(x_in[:, :, :], node_view(xs_table, i)).then_inc(s_x, 16)
                sp.wait_ge(st.s_vec, i * steps + steps + 1)
                sp.dma_start(node_view(score_table, i), s_sb[:, :, 0:2]).then_inc(st.s_store, 16)
                sp.wait_ge(st.s_store, 16 * (i + 1))
                sp.sem_inc(st.s_stored, 1)


def type_weights(nc, K, vals_e, w7_e):
    with ExitStack() as ctx:
        m = Scope(nc, ctx, "tw")
        t = m.sb("t", [PARTS, ITEMS])
        s_v = m.sem("s_v")
        block = ctx.enter_context(nc.Block())

        @block.vector
        def _(dve):
            v = nc.vector
            d = Chain(dve, s_v)
            for r in range(4):
                to = w7_e if r == 0 else t
                d.op(v.scalar_tensor_tensor, to[:, :], K["et4_e"][:, :], float(r), vals_e[:, :, 2 + r],
                     ALU.is_equal, ALU.mult)
                if r:
                    d.op(v.tensor_tensor, w7_e[:, :], w7_e[:, :], t[:, :], ALU.add)
            dve.wait_ge(s_v, d.n + 1)


def attention2_pass(nc, K, xs_table, w_e, max_e, acc):
    heads, c = 2, 256
    W = heads * c + 2 * heads
    with ExitStack() as ctx:
        m = Scope(nc, ctx, "p6")
        ring = m.sb("ring", [PARTS, SLOTS, c])
        aux = m.sb("aux", [PARTS, SLOTS, 2 * heads])
        hot = m.sb("hot", [PARTS, 2, HALF, PARTS])
        hot_w = m.sb("hot_w", [PARTS, 4, heads, PARTS])
        stage = m.sb("stage", [PARTS, 2, HALF], I32)
        ps = m.ps("ps", [PARTS, 4, 2, 512])
        s_row = [m.sem(f"s_row{j}") for j in range(SLOTS)]
        s_stage, s_gate, s_hot, s_mm, s_add, s_zero, s_aux, s_agate, s_w = (
            m.sem(n) for n in ("s_stage", "s_gate", "s_hot", "s_mm", "s_add", "s_zero", "s_aux", "s_agate", "s_w"))
        block = ctx.enter_context(nc.Block())
        LOOPS = ITEMS // SLOTS

        @block.gpsimd
        def _(pool):
            with pool.Fori(0, LOOPS) as i:
                for h in range(2):
                    pool.wait_ge(s_mm, i * SLOTS + HALF * h + HALF)
                    pool.sem_inc(s_gate, 1)
                    nc.gpsimd.tensor_copy(stage[:, h, :], K["src_e"][:, bass.ds(i * SLOTS + HALF * h, HALF)])\
                      .then_inc(s_stage, 1)
                    pool.wait_ge(s_stage, 2 * i + h + 1)
                    pool.sem_inc(s_gate, 1)
                    for j in range(HALF):
                        pool.indirect_dma_start(
                            ring[:, HALF * h + j, :], None, xs_table,
                            bass.IndirectOffsetOnAxis(ap=stage[:, h, j:j + 1], axis=0))\
                            .then_inc(s_row[HALF * h + j], 16)

        @block.scalar
        def _(act):
            a = nc.scalar
            act.sem_inc(s_aux, 2)
            with act.Fori(0, LOOPS) as i:
                for h in range(2):
                    at = bass.ds(i * SLOTS + HALF * h, HALF)
                    half = slice(HALF * h, HALF * h + HALF)
                    act.wait_ge(s_mm, i * SLOTS + HALF * h + HALF)
                    act.sem_inc(s_agate, 1)
                    a.activation(aux[:, half, 0:heads], w_e[:, at, :], ACT.Copy).then_inc(s_aux, 1)
                    a.activation(aux[:, half, heads:2 * heads], max_e[:, at, :], ACT.Copy).then_inc(s_aux, 1)
                    for j in range(HALF):
                        if j == 0:
                            act.wait_ge(s_hot, 2 * i + h + 1)
                            act.wait_ge(s_aux, 2 * (2 * i + h + 1) + 2)
                            act.sem_inc(s_agate, 1)
                        act.wait_ge(s_mm, i * SLOTS + HALF * h + j + SLOTS - 3)
                        for hd in range(heads):
                            a.activation(hot_w[:, j % 4, hd, :], hot[:, h, j, :], ACT.Copy,
                                         scale=aux[:, HALF * h + j, hd:hd + 1]).then_inc(s_w, 1)

        @block.vector
        def _(dve):
            v = nc.vector
            v.memset(acc[:, :, :], 0.0).then_inc(s_zero, 1)
            dve.wait_ge(s_zero, 1)
            dve.sem_inc(s_zero, 7)

            with dve.Fori(0, LOOPS) as i:
                for h in range(2):
                    dve.wait_ge(s_mm, i * SLOTS + HALF * h + HALF)
                    v.tensor_tensor(hot[:, h, :, :], bc(K["iota"][:, :].unsqueeze(1), [PARTS, HALF, PARTS]),
                                    bc(K["dst_e"][:, bass.ds(i * SLOTS + HALF * h, HALF)].unsqueeze(2),
                                       [PARTS, HALF, PARTS]), ALU.is_equal).then_inc(s_hot, 1)
                for j in range(SLOTS):
                    t = dve.value_load(K["tiles"][0:1, bass.ds(i * SLOTS + j, 1)], min_val=0, max_val=TILES - 1)
                    dve.wait_ge(s_mm, i * SLOTS + j + 1 + SLOTS)
                    dve.wait_ge(s_zero, 2 * (i * SLOTS + j) + 8)
                    row = acc[:, bass.ds(t, 1), 0:heads * c].squeeze(1)
                    v.tensor_tensor(row, ps[:, j % 4, 0, :], row, ALU.add).then_inc(s_zero, 1)
                    row = acc[:, bass.ds(t, 1), heads * c:W].squeeze(1)
                    dve.wait_ge(s_zero, 2 * (i * SLOTS + j) + 9)
                    v.tensor_tensor(row, ps[:, j % 4, 1, 0:2 * heads], row, ALU.add).then_inc(s_zero, 1)
            
        @block.tensor
        def _(pe):
            pe.sem_inc(s_mm, SLOTS)
            with pe.Fori(0, LOOPS) as i:
                for j in range(SLOTS):
                    pe.wait_ge(s_row[j], i * 16 + 16)
                    pe.wait_ge(s_w, 2 * (i * SLOTS + j + 1))
                    pe.wait_ge(s_zero, 2 * (i * SLOTS + j) + 2)
                    for hd in range(heads):
                        nc.tensor.matmul(ps[:, j % 4, 0, hd * c:(hd + 1) * c], hot_w[:, j % 4, hd, :], ring[:, j, :],
                                         start=True, stop=True)
                    nc.tensor.matmul(ps[:, j % 4, 1, 0:2 * heads], hot[:, j // HALF, j % HALF, :], aux[:, j, :],
                                     start=True, stop=True).then_inc(s_mm, 1)


def attention2_out(nc, K, I, acc, xs_table, xg_table, xt_table):
    heads, c = 2, 256
    H3 = [PARTS, GROUP, c]
    with ExitStack() as ctx:
        m = Scope(nc, ctx, "n7")
        steps = 3 + SELF_STEPS + 6 + 2 * 3 + 4
        st = NodeStage(nc, m, 6, 6, 1, steps, 4)
        st.ident = K["ident"]
        xs = m.sb("xs", H3)
        agg = m.sb("agg", [PARTS, 2 * GROUP * c])
        t = m.sb("t", H3)
        aux = m.sb("aux", [PARTS, GROUP, 4])
        own = m.sb("own", [PARTS, GROUP, 4])
        deg = m.sb("deg", [PARTS, GROUP])
        sz = m.sb("sz", [PARTS, GROUP])
        e, cs, ch = (m.sb(n, [PARTS, GROUP, heads]) for n in ("e", "cs", "ch"))
        both = m.sb("both", [PARTS, GROUP, 2 * heads])
        w = m.sb("w", [PARTS, 2, heads * c])
        w_rel = m.sb("w_rel", [PARTS, 2, 4, PARTS])
        b_row = m.sb("b_row", [PARTS, c])
        s_x = m.sem("s_x")
        by_head = agg[:, :].rearrange("p (h t d) -> p h t d", h=heads, d=c)
        by_type = agg[:, :].rearrange("p (t r d) -> p t r d", r=4, d=PARTS)
        block = ctx.enter_context(nc.Block())

        @block.vector
        def _(dve):
            v = nc.vector
            d = Chain(dve, st.s_vec, steps)
            dve.wait_ge(st.s_w, 16 * 6)
            with dve.Fori(0, GROUPS) as i:
                d.round(i)
                d.op(v.tensor_scalar, aux[:, :, :], group_of(acc, i)[:, :, 2 * c:2 * c + 4], 1.0, None, ALU.mult)
                d.op(v.tensor_scalar, own[:, :, :], group_of(K["own"], i), 1.0, None, ALU.mult)
                d.op(v.tensor_scalar, deg[:, :], group_of(K["counts"], i)[:, :, 9], 1.0, None, ALU.mult)
                combine_self(nc, d, st, i, 0, K, heads, (own[:, :, 0:heads], own[:, :, heads:2 * heads]),
                             aux[:, :, 0:heads], aux[:, :, heads:2 * heads], deg[:, :], e[:, :, :], sz[:, :],
                             cs[:, :, :], ch[:, :, :], both[:, :, :])
                dve.wait_ge(s_x, 16 * (i + 1))
                dve.wait_ge(st.s_stored, i + 1)
                for hd in range(heads):
                    d.op(v.tensor_tensor, by_head[:, hd], group_of(acc, i)[:, :, hd * c:(hd + 1) * c],
                         bc(cs[:, :, hd:hd + 1], H3), ALU.mult)
                    d.op(v.tensor_tensor, t[:, :, :], xs[:, :, :], bc(ch[:, :, hd:hd + 1], H3), ALU.mult)
                    d.op(v.tensor_tensor, by_head[:, hd], by_head[:, hd], t[:, :, :], ALU.add)
                    d.mark(f"agg{hd}")
                for o in range(2):
                    cols = slice(o * PARTS, (o + 1) * PARTS)
                    st.await_product(dve, i, o)
                    d.op(v.tensor_scalar, t[:, :, cols], st.prod(o), 1.0 / heads, None, ALU.mult)
                    d.mark(f"used{o}")
                    d.op(v.tensor_tensor, t[:, :, cols], t[:, :, cols], bc(b_row[:, cols].unsqueeze(1), G3), ALU.add)
                    d.op(v.tensor_scalar, xs[:, :, cols], t[:, :, cols], 0.0, None, ALU.max)
                    d.mark(f"result{o}")
                for r in range(4):
                    st.await_product(dve, i, 2 + r)
                    d.op(v.tensor_copy, by_type[:, :, r, :], st.prod(2 + r))
                    d.mark(f"used{2 + r}")
                d.check()
            st.marks = dict(d.marks)

        @block.tensor
        def _(pe):
            with pe.Fori(0, GROUPS) as i:
                st.group_free(pe, i)
                for hd in range(heads):
                    st.vec_reached(pe, i, f"agg{hd}")
                    for b in range(2):
                        st.turn(pe, i, 2 * hd + b, by_head[:, hd, :, b * PARTS:(b + 1) * PARTS])
                for o in range(2):
                    st.multiply(pe, i, o, 4, [(2 * hd + b, w[:, b, hd * c + o * PARTS:hd * c + (o + 1) * PARTS])
                                              for hd in range(heads) for b in range(2)])
                for b in range(2):
                    st.vec_reached(pe, i, f"result{b}")
                    st.turn(pe, i, 4 + b, xs[:, :, b * PARTS:(b + 1) * PARTS])
                for r in range(4):
                    st.multiply(pe, i, 2 + r, 6, [(b, w_rel[:, b, r, :]) for b in range(2)])

        @block.scalar
        def _(act):
            act.sem_inc(st.s_stored, 1)
            with act.Fori(0, GROUPS) as i:
                st.vec_reached(act, i, "exp0")
                nc.scalar.activation(both[:, :, :], both[:, :, :], ACT.Exp).then_inc(st.s_act, 1)
                for k in range(6):
                    st.copy_turned(act, i, k, k % 4)

        @block.sync
        def _(sp):
            sp.dma_start(w[:, :, :], I["L3_gnn_gat_W"].rearrange("(b p) n -> p b n", p=PARTS)).then_inc(st.s_w, 16)
            for r in range(4):
                sp.dma_start(w_rel[:, :, r, :], I["L3_gnn_rgcn_Wrel"][r].rearrange("(b p) n -> p b n", p=PARTS))\
                  .then_inc(st.s_w, 16)
            sp.dma_start(b_row[:, :], spread(I["L3_gnn_gat_b"])).then_inc(st.s_w, 16)
            with sp.Fori(0, GROUPS) as i:
                st.group_free(sp, i)
                sp.dma_start(xs[:, :, :], node_view(xs_table, i)).then_inc(s_x, 16)
                sp.wait_ge(st.s_vec, i * steps + steps + 1)
                sp.dma_start(node_view(xg_table, i), xs[:, :, :]).then_inc(st.s_store, 16)
                sp.dma_start(node_view(xt_table, i), by_type.rearrange("p t r d -> p t (r d)")).then_inc(st.s_store, 16)
                sp.wait_ge(st.s_store, 32 * (i + 1))
                sp.sem_inc(st.s_stored, 1)


def fuse(nc, K, I, acc, x_table, xs_table, xg_table, out_table):
    with ExitStack() as ctx:
        m = Scope(nc, ctx, "n8")
        steps = 9 + LN_STEPS
        st = NodeStage(nc, m, 5, 2, 2, steps, 5)
        st.ident = K["ident"]
        x_in, rg, t, y, sq = (m.sb(n, G3) for n in ("x_in", "rg", "t", "y", "sq"))
        xs, xg = (m.sb(n, [PARTS, GROUP, 256]) for n in ("xs", "xg"))
        w_root = m.sb("w_root", [PARTS, 2, PARTS])
        w_fuse = m.sb("w_fuse", [PARTS, 5, PARTS])
        rows = m.sb("rows", [PARTS, 2, PARTS])
        stat = m.sb("stat", [PARTS, 4, GROUP])
        norm = m.sb("norm", [PARTS, 2, GROUP])
        s_x = m.sem("s_x")
        block = ctx.enter_context(nc.Block())

        @block.vector
        def _(dve):
            v = nc.vector
            d = Chain(dve, st.s_vec, steps)
            dve.wait_ge(st.s_w, 64)
            with dve.Fori(0, GROUPS) as i:
                d.round(i)
                d.op(v.tensor_tensor, rg[:, :, :], group_of(acc, i), bc(rows[:, 0, :].unsqueeze(1), G3), ALU.add)
                st.await_product(dve, i, 0)
                d.op(v.tensor_tensor, rg[:, :, :], st.prod(0), rg[:, :, :], ALU.add)
                d.mark("used0")
                st.await_product(dve, i, 1)
                d.op(v.tensor_tensor, t[:, :, :], st.prod(1), bc(rows[:, 1, :].unsqueeze(1), G3), ALU.add)
                d.mark("used1")
                d.op(v.tensor_tensor, sq[:, :, :], t[:, :, :], t[:, :, :], ALU.mult)
                d.op(v.tensor_reduce, norm[:, 0, :], sq[:, :, :], AX.X, ALU.add)
                d.mark("norm")
                st.await_act(dve, i, 0)
                d.op(v.tensor_scalar, norm[:, 1, :], norm[:, 1, :], 1e-12, None, ALU.max)
                d.op(v.reciprocal, norm[:, 1, :], norm[:, 1, :])
                d.op(v.tensor_tensor, t[:, :, :], t[:, :, :], bc(norm[:, 1, :].unsqueeze(2), G3), ALU.mult)
                dve.wait_ge(st.s_stored, i + 1)
                d.op(v.tensor_tensor, t[:, :, :], t[:, :, :], x_in[:, :, :], ALU.add)
                layer_norm(nc, d, st, i, 1, t[:, :, :], y[:, :, :], sq[:, :, :], stat)
                d.check()
            st.marks = dict(d.marks)

        @block.tensor
        def _(pe):
            with pe.Fori(0, GROUPS) as i:
                st.group_free(pe, i)
                pe.wait_ge(s_x, 48 * (i + 1))
                for k, (x, b) in enumerate(((xg, 0), (xg, 1), (xs, 0), (xs, 1))):
                    st.turn(pe, i, k, x[:, :, b * PARTS:(b + 1) * PARTS])
                st.multiply(pe, i, 0, 2, [(b, w_root[:, b, :]) for b in range(2)])
                st.vec_reached(pe, i, "used0")
                st.turn(pe, i, 4, rg)
                st.multiply(pe, i, 1, 5, [(2, w_fuse[:, 0, :]), (3, w_fuse[:, 1, :]), (0, w_fuse[:, 2, :]),
                                          (1, w_fuse[:, 3, :]), (4, w_fuse[:, 4, :])])

        @block.scalar
        def _(act):
            act.sem_inc(st.s_stored, 1)
            with act.Fori(0, GROUPS) as i:
                st.group_free(act, i)
                for k in range(5):
                    st.copy_turned(act, i, k, k)
                st.vec_reached(act, i, "norm")
                nc.scalar.activation(norm[:, 1, :], norm[:, 0, :], ACT.Sqrt).then_inc(st.s_act, 1)
                root_of_variance(nc, act, st, i, 1, stat, K["eps"][:, 0:1])

        @block.sync
        def _(sp):
            sp.dma_start(w_root[:, :, :], I["L3_gnn_rgcn_Wroot"].rearrange("(b p) n -> p b n", p=PARTS))\
              .then_inc(st.s_w, 16)
            sp.dma_start(w_fuse[:, :, :], I["L3_gnn_fusion_W"].rearrange("(b p) n -> p b n", p=PARTS))\
              .then_inc(st.s_w, 16)
            sp.dma_start(rows[:, 0, :], spread(I["L3_gnn_rgcn_b"])).then_inc(st.s_w, 16)
            sp.dma_start(rows[:, 1, :], spread(I["L3_gnn_fusion_b"])).then_inc(st.s_w, 16)
            with sp.Fori(0, GROUPS) as i:
                st.group_free(sp, i)
                sp.dma_start(xg[:, :, :], node_view(xg_table, i)).then_inc(s_x, 16)
                sp.dma_start(xs[:, :, :], node_view(xs_table, i)).then_inc(s_x, 16)
                sp.dma_start(x_in[:, :, :], node_view(x_table, i)).then_inc(s_x, 16)
                sp.wait_ge(st.s_vec, i * steps + steps + 1)
                sp.dma_start(node_view(out_table, i), y[:, :, :]).then_inc(st.s_store, 16)
                sp.wait_ge(st.s_store, 16 * (i + 1))
                sp.sem_inc(st.s_stored, 1)




def build(nc, I, out):
    with ExitStack() as ctx:
        g = Scope(nc, ctx, "k")
        K = {}
        K["ident"] = g.sb("ident", [PARTS, PARTS])
        K["iota_i"] = g.sb("iota_i", [PARTS, PARTS], I32)
        K["iota"] = g.sb("iota", [PARTS, PARTS])
        K["iota_pi"] = g.sb("iota_pi", [PARTS, 1], I32)
        K["iota_p"] = g.sb("iota_p", [PARTS, 1])
        K["eps"] = g.sb("eps", [PARTS, 1])
        K["tiles"] = g.sb("tiles", [1, ITEMS], I32)
        for n in ("src_e", "xt_e"):
            K[n] = g.sb(n, [PARTS, ITEMS], I32)
        for n in ("dst_e", "et4_e", "et9_e", "last_e"):
            K[n] = g.sb(n, [PARTS, ITEMS])
        K["brk"] = g.sb("brk", [ITEM_ROWS, ROW + 1])
        K["row_brk"] = g.sb("row_brk", [ITEM_ROWS, 2])
        K["inv_deg"] = g.sb("inv_deg", [PARTS, TILES])
        K["inv4"] = g.sb("inv4", [PARTS, TILES, 4])
        K["counts"] = g.sb("counts", [PARTS, TILES, 10])

        def dram(name, *shape, dt=FP32):
            return nc.dram_tensor(name, list(shape), dt).ap()
        K["zero_i"] = g.sb("zero_i", [16, 8], I32)
        for n in ("src", "dst", "et4", "et9"):
            K["edges_" + n] = dram("edges_" + n, EDGES + PARTS, dt=I32)
        K["tiles_d"] = dram("tiles_d", ITEMS, dt=I32)
        K["dst_rows_d"] = dram("dst_rows_d", ITEMS * PARTS)
        x0, x1, x2, x3, x4, hid, h_t, skip_t = (dram(n, NODE_ROWS, PARTS) for n in
                                                ("x0", "x1", "x2", "x3", "x4", "hid", "h_t", "skip_t"))
        K["score_table"] = dram("score_table", NODE_ROWS, 4)
        prepare(nc, I["src"], I["dst"], I["edge_type_4"], I["edge_type_9"], K)
        copy_in(nc, K, I["x"], x0)

        with ExitStack() as c:
            s = Scope(nc, c, "l0")
            K["scores"] = s.sb("scores", [PARTS, TILES, 8])
            K["scores_tmp"] = s.sb("scores_tmp", [PARTS, GROUP, 8])
            w_e = s.sb("w_e", [PARTS, ITEMS, 4])
            max_e = s.sb("max_e", [PARTS, ITEMS, 4])
            attention_in(nc, K, I, x0, h_t, skip_t)
            score_pass(nc, "s0", K, K["score_table"], 4, K["scores"][:, :, 4:8], 4, w_e, max_e)
            softmax_numerators(nc, "m0", K, 4, w_e[:, :, :], max_e[:, :, :], w_e[:, :, :], max_e[:, :, :])
            acc = s.sb("acc", [PARTS, TILES, 149])
            attention_pass(nc, K, h_t, w_e, max_e, acc)
            attention_out(nc, K, I, acc, x0, h_t, skip_t, x1)

        with ExitStack() as c:
            acc = Scope(nc, c, "l1").sb("acc", [PARTS, TILES, PARTS])
            W1, W2 = I["L1_gnn_W1"], I["L1_gnn_W2"]
            edge_pass(nc, "p1", x1, PARTS, K["src_e"], K, acc)
            sage(nc, "n2", K, x1, acc, PARTS, PARTS, W1[0:PARTS, :], W1[PARTS:, :], I["L1_gnn_b1"], hid, K["ident"])
            edge_pass(nc, "p2", hid, PARTS, K["src_e"], K, acc)
            sage(nc, "n3", K, hid, acc, PARTS, PARTS, W2[0:PARTS, :], W2[PARTS:, :], I["L1_gnn_b2"], x2, K["ident"],
                 residual=x1)

        with ExitStack() as c:
            acc = Scope(nc, c, "l2").sb("acc", [PARTS, TILES, PARTS])
            edge_pass(nc, "p3", x2, PARTS, K["src_e"], K, acc)
            gated_update(nc, K, I, acc, x2, x3)


        xs1, xs, xg = (dram(n, NODE_ROWS, 256) for n in ("xs1", "xs", "xg"))
        xt = dram("xt", NODE_ROWS, 4 * PARTS)
        score2 = dram("score2", NODE_ROWS, 2)
        with ExitStack() as c:
            acc = Scope(nc, c, "l3a").sb("acc", [PARTS, TILES, PARTS])
            edge_pass(nc, "p4", x3, PARTS, K["src_e"], K, acc)
            sage(nc, "n5", K, x3, acc, PARTS, 256, I["L3_gnn_sage1_Wr"], I["L3_gnn_sage1_Wl"], I["L3_gnn_sage1_b"],
                 xs1, K["ident"])
        with ExitStack() as c:
            acc = Scope(nc, c, "l3b").sb("acc", [PARTS, TILES, 256])
            edge_pass(nc, "p5", xs1, 256, K["src_e"], K, acc)
            sage(nc, "n55", K, xs1, acc, 256, 256, I["L3_gnn_sage2_Wr"], I["L3_gnn_sage2_Wl"], I["L3_gnn_sage2_b"],
                 xs, K["ident"])
        with ExitStack() as c:
            s = Scope(nc, c, "l3c")
            K["own"] = s.sb("own", [PARTS, TILES, 4])
            w7_e = s.sb("w7_e", [PARTS, ITEMS])
            with ExitStack() as c2:
                s = Scope(nc, c2, "l3d")
                w_e = s.sb("w_e", [PARTS, ITEMS, 2])
                max_e = s.sb("max_e", [PARTS, ITEMS, 2])
                with ExitStack() as c3:
                    s3 = Scope(nc, c3, "l3e")
                    K["expand"] = s3.sb("expand", [PARTS, TILES, 6])
                    vals_e = s3.sb("vals_e", [PARTS, ITEMS, 6])
                    attention2_in(nc, K, I, xs, score2)
                    score_pass(nc, "s3", K, score2, 2, K["expand"], 6, w_e, vals_e)
                    type_weights(nc, K, vals_e, w7_e)
                    softmax_numerators(nc, "m3", K, 2, w_e[:, :, :], vals_e[:, :, 0:2], w_e[:, :, :],
                                       max_e[:, :, :])
                acc = s.sb("acc", [PARTS, TILES, 516])
                attention2_pass(nc, K, xs, w_e, max_e, acc)
                attention2_out(nc, K, I, acc, xs, xg, xt)
            acc = Scope(nc, c, "l3f").sb("acc", [PARTS, TILES, PARTS])
            edge_pass(nc, "p7", xt.rearrange("n (r d) -> (n r) d", d=PARTS), PARTS, K["xt_e"], K, acc,
                      weight_e=w7_e)
            fuse(nc, K, I, acc, x3, xs, xg, x4)
        copy_out(nc, x4, out)


_INS = ['x', 'src', 'dst', 'edge_type_4', 'edge_type_9', 'L0_gnn_W', 'L0_gnn_att_src', 'L0_gnn_att_dst',
        'L0_gnn_gat_bias', 'L0_gnn_skip_W', 'L0_gnn_skip_b', 'L0_gnn_ln_g', 'L0_gnn_ln_b', 'L1_gnn_W1',
        'L1_gnn_b1', 'L1_gnn_W2', 'L1_gnn_b2', 'L2_gnn_b_msg', 'L2_gnn_edge_embed', 'L2_gnn_b_ih', 'L2_gnn_b_hh',
        'L3_gnn_sage1_Wl', 'L3_gnn_sage1_Wr', 'L3_gnn_sage1_b', 'L3_gnn_sage2_Wl', 'L3_gnn_sage2_Wr',
        'L3_gnn_sage2_b', 'L3_gnn_gat_W', 'L3_gnn_gat_att_src', 'L3_gnn_gat_att_dst', 'L3_gnn_gat_b',
        'L3_gnn_rgcn_Wrel', 'L3_gnn_rgcn_Wroot', 'L3_gnn_rgcn_b', 'L3_gnn_fusion_W', 'L3_gnn_fusion_b']


def kernel(**inputs):
    import numpy as _np
    import concourse.bacc as _bacc
    from concourse import mybir as _mybir
    from concourse.bass_utils import run_bass_kernel_spmd as _run

    laid = {name: inputs[name] for name in _INS}
    for name in ("W_msg", "W_ih", "W_hh"):
        laid[f"L2_{name}_T"] = _np.asarray(inputs[f"L2_gnn_{name}"]).T
    nc = _bacc.Bacc("TRN2", target_bir_lowering=False, num_devices=1)
    arrays, args = {}, {}
    for name, a in laid.items():
        a = _np.ascontiguousarray(a)
        arrays[f"in_{name}"] = a
        args[name] = nc.dram_tensor(f"in_{name}", a.shape, _mybir.dt.from_np(a.dtype), kind="ExternalInput").ap()
    out = nc.dram_tensor("out_0", (NODES, PARTS), _mybir.dt.float32, kind="ExternalOutput").ap()
    build(nc, args, out)
    r = _run(nc, [arrays], core_ids=[0])
    return r.results[0]["out_0"]
```

```python
import concourse.bass as bass
from concourse import mybir
from contextlib import ExitStack

FP32 = mybir.dt.float32
I32 = mybir.dt.int32
ALU = mybir.AluOpType
ACT = mybir.ActivationFunctionType
AX = mybir.AxisListType

PARTS = 128
NODES = 6250
EDGES = 100000
TILES = -(-NODES // PARTS)
NODE_ROWS = TILES * PARTS
GROUP = 7
GROUPS = TILES // GROUP
LANES = 8
ITEM_BOUND = (EDGES + 127 * TILES) // 128
ITEMS = -(-ITEM_BOUND // 16) * 16
ITEM_ROWS = ITEMS // LANES
ROW = LANES * PARTS
BIG = 1.0e30
assert GROUPS * GROUP == TILES and ITEM_ROWS <= PARTS


def bc(ap, shape):
    return ap.to_broadcast(shape)


class Scope:

    def __init__(self, nc, ctx, tag):
        self.nc, self.ctx, self.tag, self.sems = nc, ctx, tag, []
        ctx.callback(self.clear)

    def clear(self):
        if self.sems:
            self.nc.clear_and_free_semaphores(self.sems)
            self.nc.all_engine_barrier()

    def sb(self, name, shape, dt=FP32):
        return self.ctx.enter_context(self.nc.sbuf_tensor(f"{self.tag}_{name}", shape, dt))

    def ps(self, name, shape, dt=FP32):
        return self.ctx.enter_context(self.nc.psum_tensor(f"{self.tag}_{name}", shape, dt))

    def sem(self, name):
        self.sems.append(self.nc.alloc_semaphore(f"{self.tag}_{name}"))
        return self.sems[-1]


def node_view(table, g):
    return table.rearrange("(t p) d -> p t d", p=PARTS)[:, bass.ds(g * GROUP, GROUP), :]


def prepare(nc, src, dst, et4, et9, K):
    with ExitStack() as ctx:
        m = Scope(nc, ctx, "prep")
        LR, LC = 125, EDGES // 125
        dst_i = m.sb("dst_i", [LR, LC], I32)
        dst_f = m.sb("dst_f", [LR, LC])
        below = m.sb("below", [LR, LC])
        bounds_i = m.sb("bounds_i", [PARTS, TILES + 1], I32)
        bounds = m.sb("bounds", [PARTS, TILES + 1])
        below_count = m.sb("below_count", [LR, TILES + 1])
        ones = m.sb("ones", [PARTS, PARTS])
        first = m.sb("first", [PARTS, TILES + 1])
        size_f = m.sb("size_f", [PARTS, TILES])
        size_i = m.sb("size_i", [PARTS, TILES], I32)
        n_items = m.sb("n_items", [PARTS, TILES])
        zero_t = m.sb("zero_t", [PARTS, TILES])
        item_end = m.sb("item_end", [PARTS, TILES])
        item_start = m.sb("item_start", [PARTS, TILES])
        edge_base = m.sb("edge_base", [PARTS, TILES])
        item_i = m.sb("item_i", [ITEM_ROWS, LANES], I32)
        item = m.sb("item", [ITEM_ROWS, LANES])
        sel_a = m.sb("sel_a", [ITEM_ROWS, LANES, TILES])
        sel_b = m.sb("sel_b", [ITEM_ROWS, LANES, TILES])
        tile_of = m.sb("tile_of", [ITEM_ROWS, LANES])
        tile_i = m.sb("tile_i", [ITEM_ROWS, LANES], I32)
        e_start = m.sb("e_start", [ITEM_ROWS, LANES])
        e_end = m.sb("e_end", [ITEM_ROWS, LANES])
        e_read = m.sb("e_read", [ITEM_ROWS, LANES])
        e_read_i = m.sb("e_read_i", [ITEM_ROWS, LANES], I32)
        raw = {n: m.sb("raw_" + n, [ITEM_ROWS, ROW], I32) for n in ("src", "dst", "et4", "et9")}
        f_src = m.sb("f_src", [ITEM_ROWS, ROW])
        f_et4 = m.sb("f_et4", [ITEM_ROWS, ROW])
        f_et9 = m.sb("f_et9", [ITEM_ROWS, ROW])
        f_xt = m.sb("f_xt", [ITEM_ROWS, ROW])
        f_dst = m.sb("f_dst", [ITEM_ROWS, ROW])
        dst_local = m.sb("dst_local", [ITEM_ROWS, ROW])
        pos = m.sb("pos", [ITEM_ROWS, ROW])
        valid = m.sb("valid", [ITEM_ROWS, ROW])
        v_end = m.sb("v_end", [ITEM_ROWS, ROW])
        key = m.sb("key", [ITEM_ROWS, ROW + 2])
        cont = m.sb("cont", [ITEM_ROWS, ROW + 1])
        last = m.sb("last", [ITEM_ROWS, ROW])
        ps_b = m.ps("ps_b", [PARTS, 512])
        ps_t = m.ps("ps_t", [PARTS, 2, 2, 512])
        s_in, s_pool, s_v, s_pe, s_read, s_keys, s_tr, s_out, s_tile, s_pad = (
            m.sem(n) for n in ("s_in", "s_pool", "s_v", "s_pe", "s_read", "s_keys", "s_tr", "s_out", "s_tile", "s_pad"))
        fields = ["src", "dst", "et4", "et9"]
        arrays = {"src": src, "dst": dst, "et4": et4, "et9": et9}
        moved = [(f_src, K["src_e"]), (f_xt, K["xt_e"]), (dst_local, K["dst_e"]),
                 (f_et4, K["et4_e"]), (f_et9, K["et9_e"]), (last, K["last_e"])]
        mark = {}
        block = ctx.enter_context(nc.Block())

        @block.gpsimd
        def _(pool):
            def step(ins):
                step.n += 1
                ins.then_inc(s_pool, 1)
            step.n = 0
            step(pool.iota(bounds_i[:, :], [[PARTS, TILES + 1]], base=0, channel_multiplier=0))
            step(pool.iota(item_i[:, :], [[1, LANES]], base=0, channel_multiplier=LANES))
            step(pool.iota(K["iota_i"][:, :], [[1, PARTS]], base=0, channel_multiplier=0))
            step(pool.iota(K["iota_pi"][:, :], [[1, 1]], base=0, channel_multiplier=1))
            step(pool.memset(ones[:, :], 1.0))
            step(pool.memset(K["ident"][:, :], 0.0))
            step(pool.memset(K["zero_i"][:, :], 0))
            pool.wait_ge(s_pool, 7)
            step(pool.affine_select(out=K["ident"][:, :], in_=K["ident"][:, :], compare_op=ALU.not_equal,
                                    fill=1.0, base=0, pattern=[[-1, PARTS]], channel_multiplier=1))
            pool.wait_ge(s_v, mark_read)
            pool.wait_ge(s_pad, 16 * 2 * len(fields))
            for n in fields:
                for j in range(LANES):
                    pool.indirect_dma_start(
                        raw[n][:, j * PARTS:(j + 1) * PARTS], None, K["edges_" + n].unsqueeze(1),
                        bass.IndirectOffsetOnAxis(ap=e_read_i[:, j:j + 1], axis=0)).then_inc(s_read, 16)

        @block.vector
        def _(dve):
            v = nc.vector
            count = [0]

            def step(ins):
                count[0] += 1
                ins.then_inc(s_v, 1)
                dve.wait_ge(s_v, count[0])

            dve.wait_ge(s_in, 16)
            step(v.tensor_copy(dst_f[:, :], dst_i[:, :]))
            dve.wait_ge(s_pool, 8)
            step(v.tensor_copy(bounds[:, :], bounds_i[:, :]))
            step(v.tensor_copy(K["iota"][:, :], K["iota_i"][:, :]))
            step(v.tensor_copy(K["iota_p"][:, :], K["iota_pi"][:, :]))
            step(v.tensor_copy(item[:, :], item_i[:, :]))
            for t in range(TILES + 1):
                step(v.tensor_scalar(below[:, :], dst_f[:, :], float(PARTS * t), None, ALU.is_lt, ALU.add,
                                     accum_out=below_count[:, t:t + 1]))
            assert count[0] == mark_count, count[0]
            dve.wait_ge(s_pe, 1)
            step(v.tensor_copy(first[:, :], ps_b[:, 0:TILES + 1]))
            step(v.tensor_tensor(size_f[:, :], first[:, 1:TILES + 1], first[:, 0:TILES], ALU.subtract))
            step(v.tensor_scalar(size_i[:, :], size_f[:, :], float(PARTS - 1), None, ALU.add))
            step(v.tensor_scalar(size_i[:, :], size_i[:, :], 7, None, ALU.arith_shift_right))
            step(v.tensor_copy(n_items[:, :], size_i[:, :]))
            step(v.memset(zero_t[:, :], 0.0))
            step(v.tensor_tensor_scan(item_end[:, :], n_items[:, :], zero_t[:, :], 0.0, ALU.add, ALU.add))
            step(v.tensor_tensor(item_start[:, :], item_end[:, :], n_items[:, :], ALU.subtract))
            step(v.scalar_tensor_tensor(edge_base[:, :], item_start[:, :], -float(PARTS), first[:, 0:TILES],
                                        ALU.mult, ALU.add))
            shape = [ITEM_ROWS, LANES, TILES]
            it = bc(item[:, :].unsqueeze(2), shape)

            def per_tile(x):
                return bc(x.unsqueeze(1), shape)
            step(v.tensor_tensor(sel_b[:, :, :], per_tile(item_end[0:ITEM_ROWS, :]), it, ALU.is_gt))
            step(v.tensor_reduce(tile_of[:, :], sel_b[:, :, :], AX.X, ALU.add))
            step(v.tensor_scalar(tile_of[:, :], tile_of[:, :], -1.0, float(TILES), ALU.mult, ALU.add))
            step(v.tensor_scalar(tile_of[:, :], tile_of[:, :], float(TILES - 1), None, ALU.min))
            step(v.tensor_copy(tile_i[:, :], tile_of[:, :]))
            assert count[0] == mark_tile, count[0]
            step(v.tensor_tensor(sel_a[:, :, :], per_tile(item_start[0:ITEM_ROWS, :]), it, ALU.is_le))
            step(v.tensor_tensor(sel_a[:, :, :], sel_a[:, :, :], sel_b[:, :, :], ALU.mult))
            step(v.tensor_tensor(sel_b[:, :, :], sel_a[:, :, :], per_tile(edge_base[0:ITEM_ROWS, :]), ALU.mult))
            step(v.tensor_reduce(e_start[:, :], sel_b[:, :, :], AX.X, ALU.add))
            step(v.scalar_tensor_tensor(e_start[:, :], item[:, :], float(PARTS), e_start[:, :], ALU.mult, ALU.add))
            step(v.tensor_tensor(sel_b[:, :, :], sel_a[:, :, :], per_tile(first[0:ITEM_ROWS, 1:TILES + 1]),
                                 ALU.mult))
            step(v.tensor_reduce(e_end[:, :], sel_b[:, :, :], AX.X, ALU.add))
            step(v.tensor_scalar(e_read[:, :], e_start[:, :], float(EDGES), None, ALU.min))
            step(v.tensor_copy(e_read_i[:, :], e_read[:, :]))
            assert count[0] == mark_read, count[0]
            dve.wait_ge(s_read, 16 * LANES * len(fields))
            step(v.tensor_copy(f_src[:, :], raw["src"][:, :]))
            step(v.tensor_copy(f_dst[:, :], raw["dst"][:, :]))
            step(v.tensor_copy(f_et4[:, :], raw["et4"][:, :]))
            step(v.tensor_scalar(f_et9[:, :], raw["et9"][:, :], 0.0, 8.0, ALU.max, ALU.min))
            step(v.scalar_tensor_tensor(f_xt[:, :], f_src[:, :], 4.0, f_et4[:, :], ALU.mult, ALU.add))
            wide = [ITEM_ROWS, LANES, PARTS]

            def lanes(x):
                return x.rearrange("p (j e) -> p j e", e=PARTS)

            def per_item(x):
                return bc(x.unsqueeze(2), wide)
            step(v.tensor_tensor(lanes(pos[:, :]), bc(K["iota"][0:ITEM_ROWS, :].unsqueeze(1), wide),
                                 per_item(e_read[:, :]), ALU.add))
            step(v.tensor_tensor(lanes(valid[:, :]), lanes(pos[:, :]), per_item(e_start[:, :]), ALU.is_ge))
            step(v.tensor_tensor(lanes(v_end[:, :]), lanes(pos[:, :]), per_item(e_end[:, :]), ALU.is_lt))
            step(v.tensor_tensor(valid[:, :], valid[:, :], v_end[:, :], ALU.mult))
            step(v.tensor_scalar(tile_of[:, :], tile_of[:, :], float(PARTS), None, ALU.mult))
            step(v.tensor_tensor(lanes(dst_local[:, :]), lanes(f_dst[:, :]), per_item(tile_of[:, :]), ALU.subtract))
            step(v.scalar_tensor_tensor(dst_local[:, :], dst_local[:, :], 1.0, valid[:, :], ALU.add, ALU.mult))
            step(v.tensor_scalar(dst_local[:, :], dst_local[:, :], -1.0, None, ALU.add))
            assert count[0] == mark_local, count[0]
            step(v.memset(key[:, :], -1.0))
            step(v.scalar_tensor_tensor(key[:, 1:ROW + 1], f_dst[:, :], 1.0, valid[:, :], ALU.add, ALU.mult))
            assert count[0] == mark_key, count[0]
            dve.wait_ge(s_keys, 32)
            step(v.tensor_tensor(cont[:, :], key[:, 0:ROW + 1], key[:, 1:ROW + 2], ALU.is_equal))
            step(v.tensor_scalar(K["brk"][:, :], cont[:, :], -1.0, BIG, ALU.add, ALU.mult))
            step(v.tensor_scalar(last[:, :], cont[:, 1:ROW + 1], -1.0, 1.0, ALU.mult, ALU.add))
            step(v.tensor_reduce(K["row_brk"][:, 0:1], K["brk"][:, 0:ROW], AX.X, ALU.min))
            step(v.tensor_reduce(K["row_brk"][:, 1:2], K["brk"][:, 1:ROW + 1], AX.X, ALU.min))
            assert count[0] == mark_fields, count[0]
            for k, (_, to) in enumerate(moved):
                for half in range(2):
                    dve.wait_ge(s_tr, 2 * k + half + 1)
                    view = to[:, 0:ITEMS].rearrange("p (i j) -> p j i", j=LANES)[:, 4 * half:4 * half + 4, :]
                    step(v.tensor_copy(view, ps_t[:, k % 2, half, 0:4 * ITEM_ROWS]
                                       .rearrange("p (j i) -> p j i", j=4)))

        @block.tensor
        def _(pe):
            pe.wait_ge(s_v, mark_count)
            pe.wait_ge(s_pool, 8)
            nc.tensor.matmul(ps_b[:, 0:TILES + 1], ones[0:LR, :], below_count[:, :], start=True, stop=True)\
              .then_inc(s_pe, 1)
            pe.wait_ge(s_v, mark_fields)
            for k, (frm, _) in enumerate(moved):
                if k >= 2:
                    pe.wait_ge(s_v, mark_fields + 2 * (k - 1))
                for j in range(LANES):
                    ins = nc.tensor.transpose(
                        ps_t[:, k % 2, j // 4, (j % 4) * ITEM_ROWS:(j % 4 + 1) * ITEM_ROWS],
                        frm[:, j * PARTS:(j + 1) * PARTS], K["ident"][0:ITEM_ROWS, 0:ITEM_ROWS])
                    if j % 4 == 3:
                        ins.then_inc(s_tr, 1)

        @block.scalar
        def _(act):
            for n in fields:
                act.dma_start(K["edges_" + n][0:EDGES].rearrange("(p c) -> p c", p=16),
                              arrays[n].rearrange("(p c) -> p c", p=16)).then_inc(s_pad, 16)
            act.wait_ge(s_pool, 8)
            for n in fields:
                act.dma_start(K["edges_" + n][EDGES:EDGES + PARTS].rearrange("(p c) -> p c", p=16),
                              K["zero_i"][0:16, 0:8]).then_inc(s_pad, 16)

        @block.sync
        def _(sp):
            sp.dma_start(dst_i[:, :], dst.rearrange("(p c) -> p c", p=LR)).then_inc(s_in, 16)
            sp.wait_ge(s_v, mark_tile)
            sp.dma_start(K["tiles_d"].rearrange("(p j) -> p j", j=LANES), tile_i[:, :]).then_inc(s_tile, 16)
            sp.wait_ge(s_v, mark_local)
            sp.dma_start(K["dst_rows_d"].rearrange("(p c) -> p c", c=ROW), dst_local[:, :]).then_inc(s_out, 16)
            sp.wait_ge(s_v, mark_key)
            sp.dma_start(key[1:ITEM_ROWS, 0:1], key[0:ITEM_ROWS - 1, ROW:ROW + 1]).then_inc(s_keys, 16)
            sp.dma_start(key[0:ITEM_ROWS - 1, ROW + 1:ROW + 2], key[1:ITEM_ROWS, 1:2]).then_inc(s_keys, 16)
            sp.wait_ge(s_tile, 16)
            sp.dma_start(K["tiles"][:, :], K["tiles_d"].unsqueeze(0)).then_inc(s_tile, 16)
            sp.wait_ge(s_tile, 32)
            sp.wait_ge(s_out, 16)


mark_count = 5 + TILES + 1
mark_tile = mark_count + 14
mark_read = mark_tile + 9
mark_local = mark_read + 13
mark_key = mark_local + 2
mark_fields = mark_key + 5


class Chain:

    def __init__(self, eng, sem, per_round=0):
        self.eng, self.sem, self.per_round = eng, sem, per_round
        self.base, self.n, self.marks, self.fellows = 1, 0, {}, 0
        eng.sem_inc(sem, 1 + per_round)
        self.base += per_round

    def round(self, i):
        self.base, self.n = i * self.per_round + 1 + self.per_round, 0

    def op(self, f, *args, **kw):
        self.eng.wait_ge(self.sem, self.base + self.n)
        f(*args, **kw).then_inc(self.sem, 1)
        self.n += 1

    def together(self, f, *args, **kw):
        if self.fellows == 0:
            self.eng.wait_ge(self.sem, self.base + self.n)
        f(*args, **kw).then_inc(self.sem, 1)
        self.n += 1
        self.fellows += 1

    def join(self):
        self.fellows = 0

    def mark(self, name):
        self.marks[name] = self.n

    def check(self):
        assert self.n == self.per_round, (self.n, self.per_round)


class Step:

    def __init__(self, g, side, r):
        self.g, self.side, self.r = g, side, r


def groups(eng):
    with eng.Fori(0, GROUPS // 2) as r:
        for side in range(2):
            yield Step(r * 2 + side, side, r)
    yield Step(GROUPS - 1, 0, GROUPS // 2)


def skewed(eng, before, after):
    before(Step(0, 0, 0))
    with eng.Fori(0, GROUPS // 2) as r:
        before(Step(r * 2 + 1, 1, r))
        after(Step(r * 2, 0, r))
        before(Step(r * 2 + 2, 0, r + 1))
        after(Step(r * 2 + 1, 1, r))
    after(Step(GROUPS - 1, 0, GROUPS // 2))


def far_skewed(eng, before, after):
    before(Step(0, 0, 0))
    before(Step(1, 1, 0))
    with eng.Fori(0, GROUPS // 2 - 1) as r:
        before(Step(r * 2 + 2, 0, r + 1))
        after(Step(r * 2, 0, r))
        before(Step(r * 2 + 3, 1, r + 1))
        after(Step(r * 2 + 1, 1, r))
    last = GROUPS // 2
    before(Step(GROUPS - 1, 0, last))
    for k in range(3):
        after(Step(GROUPS - 3 + k, k % 2, last - (k < 2)))


class NodeStage:

    def __init__(self, nc, m, n_turns, n_prods, n_acts, vec_steps, n_blocks):
        self.nc, self.m = nc, m
        self.n_turns, self.n_prods, self.n_acts, self.vec_steps = n_turns, n_prods, n_acts, vec_steps
        self.turned = m.sb("turned", [PARTS, 2, max(n_blocks, 1), GROUP, PARTS]) if n_blocks else None
        self.ps_t = [m.ps(f"ps_t{k}", [PARTS, 1024]) for k in range(2)]
        self.ps_o = [m.ps(f"ps_o{k}", [PARTS, 1024]) for k in range(2)]
        self.s_vec, self.s_turn, self.s_copy, self.s_prod, self.s_act, self.s_store, self.s_stored, self.s_w = (
            m.sem(n) for n in ("s_vec", "s_turn", "s_copy", "s_prod", "s_act", "s_store", "s_stored", "s_w"))
        self.s_load = [m.sem(f"s_load{k}") for k in range(2)]
        self.s_late = [m.sem(f"s_late{k}") for k in range(2)]
        self.s_gate = m.sem("s_gate")
        self.marks = None

    def start(self, pe):
        pe.sem_inc(self.s_turn, self.n_turns + 1)
        pe.sem_inc(self.s_prod, self.n_prods + 1)

    def prod(self, s, o, width=PARTS):
        slot = (s.side * self.n_prods + o) % 2
        return self.ps_o[slot][:, 0:GROUP * PARTS].rearrange("p (t d) -> p t d", d=PARTS)[:, :, 0:width]

    def group_free(self, eng, s):
        eng.wait_ge(self.s_vec, s.g * self.vec_steps + 1)

    def turns_done(self, eng, s):
        eng.wait_ge(self.s_turn, s.g * self.n_turns + 1)

    def products_done(self, eng, s):
        eng.wait_ge(self.s_prod, s.g * self.n_prods + 1)

    def vec_reached(self, eng, s, name):
        eng.wait_ge(self.s_vec, s.g * self.vec_steps + self.marks[name] + self.vec_steps + 1)

    def turn(self, pe, s, k, block):
        pe.wait_ge(self.s_copy, s.g * self.n_turns + k + 1)
        slot = (s.side * self.n_turns + k) % 2
        for q in range(GROUP):
            ins = self.nc.tensor.transpose(self.ps_t[slot][:, q * PARTS:(q + 1) * PARTS], block[:, q, :],
                                           self.ident[:, :])
        ins.then_inc(self.s_turn, 1)

    def copy_turned(self, act, s, k, b, func=ACT.Copy, **kw):
        act.wait_ge(self.s_turn, (s.g + 1) * self.n_turns + k + 2)
        slot = (s.side * self.n_turns + k) % 2
        self.nc.scalar.activation(self.turned[:, s.side, b, :, :].rearrange("p t d -> p (t d)"),
                                  self.ps_t[slot][:, 0:GROUP * PARTS], func, **kw).then_inc(self.s_copy, 1)

    def turned_block(self, s, b):
        return self.turned[:, s.side, b, :, :]

    def multiply(self, pe, s, o, copies, terms, width=PARTS):
        pe.wait_ge(self.s_copy, s.g * self.n_turns + copies + 2)
        if o >= 2:
            self.vec_reached(pe, s, f"used{o - 2}")
        elif self.n_prods >= 2:
            pe.wait_ge(self.s_vec, s.g * self.vec_steps + self.marks[f"used{self.n_prods - 2 + o}"] + 1)
        else:
            self.group_free(pe, s)
        slot = (s.side * self.n_prods + o) % 2
        for q in range(GROUP):
            for n, (block, w) in enumerate(terms):
                ins = self.nc.tensor.matmul(self.ps_o[slot][:, q * PARTS:q * PARTS + width],
                                            block[:, q, :], w, start=(n == 0), stop=(n == len(terms) - 1))
        ins.then_inc(self.s_prod, 1)

    def multiply_turned(self, pe, s, k, copies, terms, extra=None):
        pe.wait_ge(self.s_copy, s.g * self.n_turns + max(copies, k - 1) + 2)
        slot = (s.side * self.n_turns + k) % 2
        for q0, q1 in ((0, 4), (4, GROUP)):
            out = self.ps_t[slot][:, q0 * PARTS:q1 * PARTS]
            for n, (block, w) in enumerate(terms):
                last = n == len(terms) - 1 and extra is None
                ins = self.nc.tensor.matmul(out, w, block[:, q0:q1, :].rearrange("p t d -> p (t d)"),
                                            start=(n == 0), stop=last)
            if extra is not None:
                for q in range(q0, q1):
                    ins = self.nc.tensor.matmul(self.ps_t[slot][:, q * PARTS:(q + 1) * PARTS], extra[:, q, :],
                                                self.ident[:, :], start=False, stop=(q == q1 - 1))
        ins.then_inc(self.s_turn, 1)

    def await_product(self, dve, s, o):
        dve.wait_ge(self.s_prod, (s.g + 1) * self.n_prods + o + 2)

    def await_act(self, dve, s, a):
        dve.wait_ge(self.s_act, s.g * self.n_acts + a + 1)

    def await_loads(self, eng, s, n):
        eng.wait_ge(self.s_load[s.side], 16 * n * (s.r + 1))

    def await_stored(self, dve, s):
        dve.wait_ge(self.s_stored, s.g + 1)

    def await_late(self, eng, s):
        eng.wait_ge(self.s_late[s.side], 16 * (s.r + 1))

    def load_late(self, sp, s, to, table):
        self.group_free(sp, s)
        sp.dma_start(to, node_view(table, s.g)).then_inc(self.s_late[s.side], 16)

    def load(self, sp, s, tables, views=(), free=None):
        (free or self.group_free)(sp, s)
        for to, frm in [(to, node_view(table, s.g)) for to, table in tables] + list(views):
            sp.dma_start(to, frm).then_inc(self.s_load[s.side], 16)

    def store(self, pool, s, tables, views=()):
        pool.wait_ge(self.s_vec, (s.g + 2) * self.vec_steps + 1)
        pool.sem_inc(self.s_gate, 1)
        for to, frm in [(node_view(table, s.g), frm) for table, frm in tables] + list(views):
            self.nc.gpsimd.dma_start(to, frm).then_inc(self.s_store, 16)
        pool.wait_ge(self.s_store, 16 * (len(tables) + len(views)) * (s.g + 1))
        pool.sem_inc(self.s_stored, 1)


G3 = [PARTS, GROUP, PARTS]
D3 = [PARTS, 2, GROUP, PARTS]


def layer_norm(nc, d, st, s, a, x, out, sums, stat):
    v = nc.vector
    mean, gap, var, root, rstd = (stat[:, k, :] for k in range(5))
    for q in range(GROUP):
        d.together(v.bn_stats, sums[:, q, :], x[:, q, :])
    d.join()
    d.together(v.tensor_tensor, gap, sums[:, :, 1], sums[:, :, 4], ALU.subtract)
    d.together(v.tensor_tensor, mean, sums[:, :, 1], sums[:, :, 4], ALU.add)
    d.together(v.tensor_tensor, var, sums[:, :, 2], sums[:, :, 5], ALU.add)
    d.join()
    d.together(v.tensor_tensor, gap, gap, gap, ALU.mult)
    d.together(v.tensor_scalar, mean, mean, 0.5, None, ALU.mult)
    d.join()
    d.op(v.scalar_tensor_tensor, var, gap, PARTS / 4.0, var, ALU.mult, ALU.add)
    d.mark(f"root{a}")
    st.await_act(d.eng, s, a)
    d.op(v.reciprocal, rstd, root)
    for q in range(GROUP):
        d.together(v.tensor_scalar, out[:, q, :], x[:, q, :], mean[:, q:q + 1], rstd[:, q:q + 1],
                   ALU.subtract, ALU.mult)
    d.join()


LN_STEPS = 2 * GROUP + 7


def root_of_variance(nc, act, st, s, a, stat, eps):
    st.vec_reached(act, s, f"root{a}")
    nc.scalar.activation(stat[:, 3, :], stat[:, 2, :], ACT.Sqrt, bias=eps, scale=1.0 / PARTS).then_inc(st.s_act, 1)


def spread(ap):
    return ap.partition_broadcast(PARTS)


def group_of(node_array, i):
    return node_array[:, bass.ds(i * GROUP, GROUP)]


def attention_in(nc, K, I, x_table, h_table, skip_table):
    heads, c = 4, 32
    with ExitStack() as ctx:
        m = Scope(nc, ctx, "n0")
        steps = 9
        st = NodeStage(nc, m, 1, 2, 1, steps, 1)
        st.ident = K["ident"]
        x_in2, h2, t2, skip2 = (m.sb(n, D3) for n in ("x_in", "h", "t", "skip"))
        w = m.sb("w", [PARTS, 2, PARTS])
        rows = m.sb("rows", [PARTS, 4, PARTS])
        block = ctx.enter_context(nc.Block())

        @block.vector
        def _(dve):
            v = nc.vector
            d = Chain(dve, st.s_vec, steps)
            dve.wait_ge(st.s_w, 16 * 6)
            v.tensor_tensor(rows[:, 2, :], rows[:, 2, :], rows[:, 3, :], ALU.add).then_inc(st.s_w, 16)
            dve.wait_ge(st.s_w, 16 * 7)
            for s in groups(dve):
                h = h2[:, s.side]
                skip = skip2[:, s.side]
                t = t2[:, s.side]
                d.round(s.g)
                st.await_product(dve, s, 0)
                st.await_stored(dve, s)
                d.op(v.tensor_copy, h[:, :, :], st.prod(s, 0))
                d.mark("used0")
                for k, name in ((0, "score_src"), (1, "score_dst")):
                    d.op(v.tensor_tensor, t[:, :, :], h[:, :, :],
                         bc(rows[:, k, :].unsqueeze(1), G3), ALU.mult)
                    d.op(v.tensor_reduce, K["scores_tmp"][:, :, k * heads:(k + 1) * heads],
                         t[:, :, :].rearrange("p t (h c) -> p t h c", c=c), AX.X, ALU.add)
                    d.op(v.tensor_scalar, group_of(K["scores"], s.g)[:, :, k * heads:(k + 1) * heads],
                         K["scores_tmp"][:, :, k * heads:(k + 1) * heads], 1.0, None, ALU.mult)
                st.await_product(dve, s, 1)
                d.op(v.tensor_tensor, skip[:, :, :], st.prod(s, 1), bc(rows[:, 2, :].unsqueeze(1), G3), ALU.add)
                d.mark("used1")
                d.op(v.tensor_copy, t[:, :, 0:heads], K["scores_tmp"][:, :, 0:heads])
                d.check()
            st.marks = dict(d.marks)

        @block.tensor
        def _(pe):
            pe.wait_ge(st.s_w, 16 * 7)
            st.start(pe)

            def before(s):
                st.await_loads(pe, s, 1)
                st.turn(pe, s, 0, x_in2[:, s.side])

            def after(s):
                for o in range(2):
                    st.multiply(pe, s, o, 1, [(st.turned_block(s, 0), w[:, o, :])])
            skewed(pe, before, after)

        @block.scalar
        def _(act):
            act.sem_inc(st.s_copy, 2)
            for s in groups(act):
                st.products_done(act, s)
                st.copy_turned(act, s, 0, 0)

        @block.sync
        def _(sp):
            for to, frm in ((w[:, 0, :], I["L0_gnn_W"]), (w[:, 1, :], I["L0_gnn_skip_W"]),
                            (rows[:, 0, :], spread(I["L0_gnn_att_src"].rearrange("h c -> (h c)"))),
                            (rows[:, 1, :], spread(I["L0_gnn_att_dst"].rearrange("h c -> (h c)"))),
                            (rows[:, 2, :], spread(I["L0_gnn_gat_bias"])),
                            (rows[:, 3, :], spread(I["L0_gnn_skip_b"]))):
                sp.dma_start(to, frm).then_inc(st.s_w, 16)
            sp.wait_ge(st.s_w, 16 * 7)
            for s in groups(sp):
                st.load(sp, s, [(x_in2[:, s.side], x_table)], free=st.turns_done)

        @block.gpsimd
        def _(pool):
            pool.sem_inc(st.s_stored, 2)
            for s in groups(pool):
                st.store(pool, s, [(h_table[:, 0:PARTS], h2[:, s.side]), (skip_table, skip2[:, s.side]),
                                   (h_table[:, PARTS:PARTS + heads], t2[:, s.side][:, :, 0:heads])])


def combine_self(nc, d, st, s, a, K, heads, self_w, z, m_seg, deg_b, e, scale_z, cs, ch, both):
    v = nc.vector
    score_s, score_d = self_w
    shape = [PARTS, GROUP, heads]
    seg, own = both[:, :, 0:heads], both[:, :, heads:2 * heads]
    d.op(v.tensor_tensor, e, score_s, score_d, ALU.add)
    d.op(v.scalar_tensor_tensor, own, e, 0.2, e, ALU.mult, ALU.max)
    d.op(v.tensor_scalar, scale_z, deg_b, 0.0, -BIG, ALU.is_equal, ALU.mult)
    d.op(v.tensor_tensor, seg, m_seg, bc(scale_z.unsqueeze(2), shape), ALU.add)
    d.op(v.tensor_tensor, e, seg, own, ALU.max)
    d.op(v.tensor_tensor, seg, seg, e, ALU.subtract)
    d.op(v.tensor_tensor, own, own, e, ALU.subtract)
    d.mark(f"exp{a}")
    st.await_act(d.eng, s, a)
    d.op(v.tensor_tensor, e, z, seg, ALU.mult)
    d.op(v.scalar_tensor_tensor, e, e, 1e-16, own, ALU.add, ALU.add)
    d.op(v.reciprocal, e, e)
    d.op(v.tensor_tensor, cs, seg, e, ALU.mult)
    d.op(v.tensor_tensor, ch, own, e, ALU.mult)


SELF_STEPS = 12


def sage(nc, tag, K, x_table, acc, in_cols, out_cols, w_self, w_agg, bias, out_table, residual=None):
    with ExitStack() as ctx:
        m = Scope(nc, ctx, tag)
        nb, no = in_cols // PARTS, out_cols // PARTS
        steps = 2 * no + (LN_STEPS if residual is not None else 0)
        st = NodeStage(nc, m, 2 * nb, no, 1, steps, 2 * nb)
        st.ident = K["ident"]
        x_in = m.sb("x_in", [PARTS, 2, GROUP, in_cols])
        mean = m.sb("mean", [PARTS, 2, GROUP, in_cols])
        y = m.sb("y", [PARTS, 2, GROUP, out_cols])
        w = m.sb("w", [PARTS, 2 * nb, out_cols])
        b_row = m.sb("b_row", [PARTS, out_cols])
        s_mean = m.sem("s_mean")
        if residual is not None:
            r_in = m.sb("r_in", D3)
            t = m.sb("t", G3)
            sums = m.sb("sums", [PARTS, GROUP, 6])
            stat = m.sb("stat", [PARTS, 5, GROUP])
        block = ctx.enter_context(nc.Block())

        @block.vector
        def _(dve):
            v = nc.vector
            dve.wait_ge(st.s_w, 48)
            d = Chain(dve, st.s_vec, steps)
            for s in groups(dve):
                d.round(s.g)
                for o in range(no):
                    part = y[:, s.side, :, o * PARTS:(o + 1) * PARTS]
                    st.await_product(dve, s, o)
                    if o == 0:
                        st.await_stored(dve, s)
                    to = part if residual is None else t[:, :, :]
                    d.op(v.tensor_tensor, to, st.prod(s, o),
                         bc(b_row[:, o * PARTS:(o + 1) * PARTS].unsqueeze(1), G3), ALU.add)
                    d.mark(f"used{o}")
                    if residual is None:
                        d.op(v.tensor_scalar, part, part, 0.0, None, ALU.max)
                if residual is not None:
                    st.await_late(dve, s)
                    d.op(v.scalar_tensor_tensor, t[:, :, :], t[:, :, :], 0.0, r_in[:, s.side], ALU.max, ALU.add)
                    layer_norm(nc, d, st, s, 0, t[:, :, :], y[:, s.side], sums, stat)
                d.check()
            st.marks = dict(d.marks)

        @block.tensor
        def _(pe):
            st.start(pe)

            def before(s):
                st.await_loads(pe, s, 1)
                for b in range(nb):
                    st.turn(pe, s, b, x_in[:, s.side, :, b * PARTS:(b + 1) * PARTS])
                for b in range(nb):
                    pe.wait_ge(s_mean, s.g * nb + b + 1)
                    st.turn(pe, s, nb + b, mean[:, s.side, :, b * PARTS:(b + 1) * PARTS])

            def after(s):
                for o in range(no):
                    st.multiply(pe, s, o, 2 * nb, [(st.turned_block(s, b), w[:, b, o * PARTS:(o + 1) * PARTS])
                                                   for b in range(2 * nb)])
            if residual is None:
                skewed(pe, before, after)
            else:
                for s in groups(pe):
                    before(s)
                    after(s)

        @block.scalar
        def _(act):
            act.sem_inc(st.s_copy, 2)

            def before(s):
                st.products_done(act, s)
                for k in range(2 * nb):
                    st.copy_turned(act, s, k, k)

            def after(s):
                if residual is not None:
                    root_of_variance(nc, act, st, s, 0, stat, K["eps"][:, 0:1])
            skewed(act, before, after)

        @block.sync
        def _(sp):
            sp.dma_start(w[:, 0:nb, :], w_self.rearrange("(b p) n -> p b n", p=PARTS)).then_inc(st.s_w, 16)
            sp.dma_start(w[:, nb:2 * nb, :], w_agg.rearrange("(b p) n -> p b n", p=PARTS)).then_inc(st.s_w, 16)
            sp.dma_start(b_row[:, :], spread(bias)).then_inc(st.s_w, 16)

            def after(s):
                if residual is not None:
                    st.load_late(sp, s, r_in[:, s.side], residual)
            skewed(sp, lambda s: st.load(sp, s, [(x_in[:, s.side], x_table)], free=st.turns_done), after)

        @block.gpsimd
        def _(pool):
            pool.sem_inc(st.s_stored, 2)

            def before(s):
                st.turns_done(pool, s)
                pool.sem_inc(st.s_gate, 1)
                for b in range(nb):
                    nc.gpsimd.tensor_tensor(mean[:, s.side, :, b * PARTS:(b + 1) * PARTS],
                                            group_of(acc, s.g)[:, :, b * PARTS:(b + 1) * PARTS],
                                            bc(group_of(K["inv_deg"], s.g).unsqueeze(2), G3), ALU.mult)\
                      .then_inc(s_mean, 1)
            far_skewed(pool, before, lambda s: st.store(pool, s, [(out_table, y[:, s.side])]))


def attention_out(nc, K, I, acc, x_table, h_table, skip_table, out_table):
    heads, c = 4, 32
    Z = PARTS
    with ExitStack() as ctx:
        m = Scope(nc, ctx, "n1")
        steps = 7 + SELF_STEPS + 2 + LN_STEPS + 2 + LN_STEPS + 3
        st = NodeStage(nc, m, 0, 0, 3, steps, 0)
        x_in, h, skip, y = (m.sb(n, D3) for n in ("x_in", "h", "skip", "y"))
        t, u = m.sb("t", G3), m.sb("u", G3)
        aux = m.sb("aux", [PARTS, GROUP, 21])
        e, cs, ch = (m.sb(n, [PARTS, GROUP, heads]) for n in ("e", "cs", "ch"))
        both = m.sb("both", [PARTS, GROUP, 2 * heads])
        sz = m.sb("sz", [PARTS, GROUP])
        deg = m.sb("deg", [PARTS, GROUP])
        rec = m.sb("rec", [PARTS, GROUP, 5])
        own = m.sb("own", [PARTS, GROUP, 2 * heads])
        sums = m.sb("sums", [PARTS, GROUP, 6])
        stat = m.sb("stat", [PARTS, 5, GROUP])
        rows = m.sb("rows", [PARTS, 2, PARTS])
        s_mix = m.sem("s_mix")
        block = ctx.enter_context(nc.Block())

        def heads_of(x):
            return x.rearrange("p t (h c) -> p t h c", c=c)

        def factor(x):
            return bc(x[:, :, :].unsqueeze(3), [PARTS, GROUP, heads, c])

        @block.vector
        def _(dve):
            v = nc.vector
            dve.wait_ge(st.s_w, 32)
            d = Chain(dve, st.s_vec, steps)
            for s in groups(dve):
                d.round(s.g)
                d.op(v.tensor_scalar, aux[:, :, :], group_of(acc, s.g)[:, :, Z:Z + 21], 1.0, None, ALU.mult)
                d.op(v.tensor_scalar, own[:, :, :], group_of(K["scores"], s.g)[:, :, :], 1.0, None, ALU.mult)
                d.op(v.tensor_reduce, deg[:, :], aux[:, :, 12:21], AX.X, ALU.add)
                d.op(v.tensor_scalar, rec[:, :, 0:4], aux[:, :, 8:12], 1.0, None, ALU.max)
                d.op(v.tensor_scalar, rec[:, :, 4], deg[:, :], 1.0, None, ALU.max)
                d.op(v.reciprocal, rec[:, :, :], rec[:, :, :])
                d.op(v.tensor_scalar, group_of(K["inv4"], s.g), rec[:, :, 0:4], 1.0, None, ALU.mult)
                combine_self(nc, d, st, s, 0, K, heads, (own[:, :, 0:heads], own[:, :, heads:2 * heads]),
                             aux[:, :, 0:4], aux[:, :, 4:8], deg[:, :], e[:, :, :], sz[:, :],
                             cs[:, :, :], ch[:, :, :], both[:, :, :])
                d.mark("factors")
                d.op(v.tensor_tensor, heads_of(t[:, :, :]), heads_of(group_of(acc, s.g)[:, :, 0:PARTS]), factor(cs),
                     ALU.mult)
                dve.wait_ge(s_mix, 3 * (s.g + 1))
                d.op(v.tensor_tensor, t[:, :, :], t[:, :, :], h[:, s.side], ALU.add)
                layer_norm(nc, d, st, s, 1, t[:, :, :], u[:, :, :], sums, stat)
                d.op(v.tensor_tensor, u[:, :, :], u[:, :, :], bc(rows[:, 0, :].unsqueeze(1), G3), ALU.mult)
                d.op(v.tensor_tensor, t[:, :, :], u[:, :, :], x_in[:, s.side], ALU.add)
                st.await_stored(dve, s)
                layer_norm(nc, d, st, s, 2, t[:, :, :], y[:, s.side], sums, stat)
                d.op(v.tensor_scalar, group_of(K["inv_deg"], s.g), rec[:, :, 4], 1.0, None, ALU.mult)
                d.op(v.tensor_scalar, group_of(K["counts"], s.g)[:, :, 0:9], aux[:, :, 12:21], 1.0, None, ALU.mult)
                d.op(v.tensor_scalar, group_of(K["counts"], s.g)[:, :, 9], deg[:, :], 1.0, None, ALU.mult)
                d.check()
            st.marks = dict(d.marks)

        @block.gpsimd
        def _(pool):
            g = nc.gpsimd
            pool.sem_inc(st.s_stored, 2)
            pool.wait_ge(st.s_w, 32)
            for s in groups(pool):
                st.await_loads(pool, s, 3)
                g.tensor_tensor(x_in[:, s.side], x_in[:, s.side], bc(rows[:, 1, :].unsqueeze(1), G3), ALU.add)\
                 .then_inc(s_mix, 1)
                st.vec_reached(pool, s, "factors")
                g.tensor_tensor(heads_of(h[:, s.side]), heads_of(h[:, s.side]), factor(ch), ALU.mult).then_inc(s_mix, 1)
                pool.wait_ge(s_mix, s.g * 3 + 2)
                g.tensor_tensor(h[:, s.side], h[:, s.side], skip[:, s.side], ALU.add).then_inc(s_mix, 1)
                st.store(pool, s, [(out_table, y[:, s.side])])

        @block.scalar
        def _(act):
            for s in groups(act):
                st.vec_reached(act, s, "exp0")
                nc.scalar.activation(both[:, :, :], both[:, :, :], ACT.Exp).then_inc(st.s_act, 1)
                root_of_variance(nc, act, st, s, 1, stat, K["eps"][:, 0:1])
                root_of_variance(nc, act, st, s, 2, stat, K["eps"][:, 0:1])

        @block.sync
        def _(sp):
            sp.dma_start(rows[:, 0, :], spread(I["L0_gnn_ln_g"])).then_inc(st.s_w, 16)
            sp.dma_start(rows[:, 1, :], spread(I["L0_gnn_ln_b"])).then_inc(st.s_w, 16)
            for s in groups(sp):
                st.load(sp, s, [(x_in[:, s.side], x_table), (h[:, s.side], h_table[:, 0:PARTS]), (skip[:, s.side], skip_table)])


def gated_update(nc, K, I, acc, x_table, out_table):
    with ExitStack() as ctx:
        m = Scope(nc, ctx, "n4")
        steps = 10 + LN_STEPS
        X, A, C, M = range(4)
        st = NodeStage(nc, m, 4, 4, 4, steps, 4)
        st.ident = K["ident"]
        x_in, x_own, agg, cnt, y = (m.sb(n, D3) for n in ("x_in", "x_own", "agg", "cnt", "y"))
        r, z, n_ = (m.sb(n, G3) for n in ("r", "z", "n"))
        w_msg = m.sb("w_msg", [PARTS, 2, PARTS])
        w_ih = m.sb("w_ih", [PARTS, 3 * PARTS])
        w_hh = m.sb("w_hh", [PARTS, 3 * PARTS])
        b_ih = m.sb("b_ih", [PARTS, 3, PARTS])
        b_hh = m.sb("b_hh", [PARTS, 3, PARTS])
        sums = m.sb("sums", [PARTS, GROUP, 6])
        stat = m.sb("stat", [PARTS, 5, GROUP])
        s_init, s_pre = m.sem("s_init"), m.sem("s_pre")
        block = ctx.enter_context(nc.Block())

        @block.vector
        def _(dve):
            v = nc.vector
            v.memset(cnt[:, :, :, :], 0.0).then_inc(s_init, 1)
            v.memset(w_msg[:, 1, :], 0.0).then_inc(s_init, 1)
            dve.wait_ge(st.s_w, 16 * 7)
            v.tensor_tensor(b_ih[:, 0:2, :], b_ih[:, 0:2, :], b_hh[:, 0:2, :], ALU.add).then_inc(s_init, 1)
            dve.wait_ge(s_init, 3)
            d = Chain(dve, st.s_vec, steps)
            for s in groups(dve):
                x = x_own[:, s.side]
                d.round(s.g)
                for o, g in ((0, r), (1, z)):
                    st.await_product(dve, s, o)
                    d.op(v.tensor_tensor, g[:, :, :], st.prod(s, o), bc(b_ih[:, o, :].unsqueeze(1), G3), ALU.add)
                    d.mark(f"used{o}")
                st.await_product(dve, s, 2)
                d.op(v.tensor_tensor, n_[:, :, :], st.prod(s, 2), bc(b_hh[:, 2, :].unsqueeze(1), G3), ALU.add)
                d.mark("used2")
                st.await_act(dve, s, 0)
                d.op(v.tensor_tensor, n_[:, :, :], n_[:, :, :], r[:, :, :], ALU.mult)
                d.op(v.tensor_tensor, n_[:, :, :], n_[:, :, :], bc(b_ih[:, 2, :].unsqueeze(1), G3), ALU.add)
                st.await_product(dve, s, 3)
                d.op(v.tensor_tensor, n_[:, :, :], st.prod(s, 3), n_[:, :, :], ALU.add)
                d.mark("used3")
                st.await_act(dve, s, 2)
                st.await_late(dve, s)
                d.op(v.tensor_tensor, r[:, :, :], x, n_[:, :, :], ALU.subtract)
                d.op(v.tensor_tensor, r[:, :, :], r[:, :, :], z[:, :, :], ALU.mult)
                d.op(v.tensor_tensor, r[:, :, :], r[:, :, :], n_[:, :, :], ALU.add)
                d.op(v.tensor_tensor, r[:, :, :], r[:, :, :], x, ALU.add)
                st.await_stored(dve, s)
                layer_norm(nc, d, st, s, 3, r[:, :, :], y[:, s.side], sums, stat)
                d.check()
            st.marks = dict(d.marks)

        @block.tensor
        def _(pe):
            pe.wait_ge(st.s_w, 16 * 7)
            pe.wait_ge(s_init, 3)

            st.start(pe)

            def before(s):
                st.await_loads(pe, s, 1)
                st.turn(pe, s, 0, x_in[:, s.side])
                pe.wait_ge(s_pre, 2 * (s.g + 1))
                st.turn(pe, s, 1, agg[:, s.side])
                st.turn(pe, s, 2, cnt[:, s.side])
                st.multiply_turned(pe, s, 3, 3, [(st.turned_block(s, A), w_msg[:, 0, :]),
                                                 (st.turned_block(s, C), w_msg[:, 1, :])])

            def after(s):
                x, msg = st.turned_block(s, X), st.turned_block(s, M)
                for o in range(2):
                    cols = slice(o * PARTS, (o + 1) * PARTS)
                    st.multiply(pe, s, o, 4, [(msg, w_ih[:, cols]), (x, w_hh[:, cols])])
                st.multiply(pe, s, 2, 4, [(x, w_hh[:, 2 * PARTS:3 * PARTS])])
                st.multiply(pe, s, 3, 4, [(msg, w_ih[:, 2 * PARTS:3 * PARTS])])
            for s in groups(pe):
                before(s)
                after(s)

        @block.scalar
        def _(act):
            a = nc.scalar
            act.sem_inc(st.s_copy, 2)

            def before(s):
                st.products_done(act, s)
                for k, b in enumerate((X, A, C, M)):
                    st.copy_turned(act, s, k, b)

            def gates(s):
                st.vec_reached(act, s, "used0")
                a.activation(r[:, :, :], r[:, :, :], ACT.Sigmoid).then_inc(st.s_act, 1)
                st.vec_reached(act, s, "used1")
                a.activation(z[:, :, :], z[:, :, :], ACT.Sigmoid).then_inc(st.s_act, 1)
                st.vec_reached(act, s, "used3")
                a.activation(n_[:, :, :], n_[:, :, :], ACT.Tanh).then_inc(st.s_act, 1)

            def root(s):
                root_of_variance(nc, act, st, s, 3, stat, K["eps"][:, 0:1])

            before(Step(0, 0, 0))
            with act.Fori(0, GROUPS // 2) as i:
                for side in range(2):
                    s = Step(i * 2 + side, side, i)
                    gates(s)
                    before(Step(i * 2 + side + 1, 1 - side, i + side))
                    root(s)
            gates(Step(GROUPS - 1, 0, GROUPS // 2))
            root(Step(GROUPS - 1, 0, GROUPS // 2))

        @block.gpsimd
        def _(pool):
            pool.sem_inc(st.s_stored, 2)
            pool.wait_ge(s_init, 1)

            def before(s):
                st.turns_done(pool, s)
                pool.sem_inc(st.s_gate, 1)
                nc.gpsimd.tensor_copy(agg[:, s.side], group_of(acc, s.g)).then_inc(s_pre, 1)
                nc.gpsimd.tensor_copy(cnt[:, s.side, :, 0:10], group_of(K["counts"], s.g)).then_inc(s_pre, 1)
            far_skewed(pool, before, lambda s: st.store(pool, s, [(out_table, y[:, s.side])]))

        @block.sync
        def _(sp):
            sp.dma_start(w_msg[:, 0, :], I["L2_W_msg_T"]).then_inc(st.s_w, 16)
            sp.dma_start(w_ih[:, :], I["L2_W_ih_T"]).then_inc(st.s_w, 16)
            sp.dma_start(w_hh[:, :], I["L2_W_hh_T"]).then_inc(st.s_w, 16)
            sp.dma_start(b_ih[:, :, :].rearrange("p a b -> p (a b)"), spread(I["L2_gnn_b_ih"])).then_inc(st.s_w, 16)
            sp.dma_start(b_hh[:, :, :].rearrange("p a b -> p (a b)"), spread(I["L2_gnn_b_hh"])).then_inc(st.s_w, 16)
            sp.wait_ge(s_init, 2)
            sp.dma_start(w_msg[0:9, 1, :], I["L2_gnn_edge_embed"]).then_inc(st.s_w, 16)
            sp.dma_start(w_msg[9:10, 1, :], I["L2_gnn_b_msg"].unsqueeze(0)).then_inc(st.s_w, 16)
            skewed(sp, lambda s: st.load(sp, s, [(x_in[:, s.side], x_table)], free=st.turns_done),
                   lambda s: st.load_late(sp, s, x_own[:, s.side], x_table))


def turned_view(table, b, g):
    return table[b][:, bass.ds(g * GROUP * PARTS, GROUP * PARTS)]


def attention2_in(nc, K, I, xs_table, score_table, xs_turned):
    heads, c = 2, 256
    with ExitStack() as ctx:
        m = Scope(nc, ctx, "n6")
        steps = 4
        st = NodeStage(nc, m, 2, 1, 0, steps, 2)
        st.ident = K["ident"]
        x_in = m.sb("x_in", [PARTS, 2, GROUP, c])
        s_sb = m.sb("s_sb", [PARTS, 2, GROUP, 4])
        w = m.sb("w", [PARTS, 2, heads * c])
        att = m.sb("att", [PARTS, 2, heads * c])
        t = m.sb("t", [PARTS, 2, heads * c])
        va = m.sb("va", [PARTS, 2, 2 * heads])
        s_va = m.sem("s_va")
        block = ctx.enter_context(nc.Block())

        @block.vector
        def _(dve):
            v = nc.vector
            dve.wait_ge(st.s_w, 48)
            done = 0
            for k in range(2):
                if k:
                    dve.wait_ge(s_va, 2)
                v.tensor_tensor(t[:, :, :], w[:, :, :], bc(att[:, k, :].unsqueeze(1), [PARTS, 2, heads * c]),
                                ALU.mult).then_inc(s_va, 1)
                dve.wait_ge(s_va, 2 * k + 1)
                v.tensor_reduce(va[:, :, k * heads:(k + 1) * heads],
                                t[:, :, :].rearrange("p b (h c) -> p b h c", c=c), AX.X, ALU.add).then_inc(s_va, 1)
            d = Chain(dve, st.s_vec, steps)
            for s in groups(dve):
                d.round(s.g)
                scores = s_sb[:, s.side]
                st.await_product(dve, s, 0)
                st.await_stored(dve, s)
                d.op(v.tensor_copy, scores, st.prod(s, 0, 4))
                d.mark("used0")
                d.op(v.tensor_scalar, group_of(K["own"], s.g), scores, 1.0, None, ALU.mult)
                d.op(v.tensor_scalar, group_of(K["expand"], s.g)[:, :, 0:2], scores[:, :, 2:4], 1.0, None, ALU.mult)
                d.op(v.tensor_scalar, group_of(K["expand"], s.g)[:, :, 2:6], group_of(K["inv4"], s.g), 1.0, None,
                     ALU.mult)
                d.check()
            st.marks = dict(d.marks)

        @block.tensor
        def _(pe):
            pe.wait_ge(s_va, 4)

            st.start(pe)

            def before(s):
                st.await_loads(pe, s, 1)
                for b in range(2):
                    st.turn(pe, s, b, x_in[:, s.side, :, b * PARTS:(b + 1) * PARTS])

            def after(s):
                st.multiply(pe, s, 0, 2, [(st.turned_block(s, b), va[:, b, :]) for b in range(2)], width=4)
            skewed(pe, before, after)

        @block.scalar
        def _(act):
            act.sem_inc(st.s_copy, 2)
            for s in groups(act):
                st.products_done(act, s)
                st.await_stored(act, s)
                for k in range(2):
                    st.copy_turned(act, s, k, k)

        @block.sync
        def _(sp):
            sp.dma_start(w[:, :, :], I["L3_gnn_gat_W"].rearrange("(b p) n -> p b n", p=PARTS)).then_inc(st.s_w, 16)
            for k, n in enumerate(("L3_gnn_gat_att_src", "L3_gnn_gat_att_dst")):
                sp.dma_start(att[:, k, :], spread(I[n].rearrange("h c -> (h c)"))).then_inc(st.s_w, 16)
            for s in groups(sp):
                st.load(sp, s, [(x_in[:, s.side], xs_table)], free=st.turns_done)

        @block.gpsimd
        def _(pool):
            pool.sem_inc(st.s_stored, 2)
            for s in groups(pool):
                st.store(pool, s, [(score_table, s_sb[:, s.side, :, 0:2])],
                         [(turned_view(xs_turned, b, s.g), st.turned_block(s, b).rearrange("p t d -> p (t d)"))
                          for b in range(2)])


def attention2_mix(nc, K, acc, xs_table, mix_table):
    heads, c = 2, 256
    with ExitStack() as ctx:
        m = Scope(nc, ctx, "n7")
        steps = 3 + SELF_STEPS + heads * GROUP
        st = NodeStage(nc, m, 0, 0, 1 + heads * GROUP, steps, 0)
        xs = m.sb("xs", [PARTS, 2, GROUP, c])
        mix = m.sb("mix", [PARTS, 2, GROUP, heads * c])
        aux = m.sb("aux", [PARTS, GROUP, 4])
        own = m.sb("own", [PARTS, GROUP, 4])
        deg = m.sb("deg", [PARTS, GROUP])
        sz = m.sb("sz", [PARTS, GROUP])
        e, cs, ch = (m.sb(n, [PARTS, GROUP, heads]) for n in ("e", "cs", "ch"))
        both = m.sb("both", [PARTS, GROUP, 2 * heads])
        s_agate = m.sem("s_agate")
        block = ctx.enter_context(nc.Block())

        @block.vector
        def _(dve):
            v = nc.vector
            d = Chain(dve, st.s_vec, steps)
            for s in groups(dve):
                d.round(s.g)
                d.op(v.tensor_scalar, aux[:, :, :], group_of(acc, s.g)[:, :, 2 * c:2 * c + 4], 1.0, None, ALU.mult)
                d.op(v.tensor_scalar, own[:, :, :], group_of(K["own"], s.g), 1.0, None, ALU.mult)
                d.op(v.tensor_scalar, deg[:, :], group_of(K["counts"], s.g)[:, :, 9], 1.0, None, ALU.mult)
                combine_self(nc, d, st, s, 0, K, heads, (own[:, :, 0:heads], own[:, :, heads:2 * heads]),
                             aux[:, :, 0:heads], aux[:, :, heads:2 * heads], deg[:, :], e[:, :, :], sz[:, :],
                             cs[:, :, :], ch[:, :, :], both[:, :, :])
                d.mark("factors")
                st.await_loads(dve, s, 1)
                for q in range(GROUP):
                    for hd in range(heads):
                        part = mix[:, s.side, q, hd * c:(hd + 1) * c]
                        st.await_act(dve, s, 1 + q * heads + hd)
                        d.op(v.scalar_tensor_tensor, part, xs[:, s.side, q, :], ch[:, q, hd:hd + 1], part,
                             ALU.mult, ALU.add)
                d.check()
            st.marks = dict(d.marks)

        @block.scalar
        def _(act):
            for s in groups(act):
                st.vec_reached(act, s, "exp0")
                nc.scalar.activation(both[:, :, :], both[:, :, :], ACT.Exp).then_inc(st.s_act, 1)
                st.await_stored(act, s)
                act.sem_inc(s_agate, 1)
                st.vec_reached(act, s, "factors")
                act.sem_inc(s_agate, 1)
                for q in range(GROUP):
                    for hd in range(heads):
                        nc.scalar.activation(mix[:, s.side, q, hd * c:(hd + 1) * c],
                                             acc[:, bass.ds(s.g * GROUP + q, 1), hd * c:(hd + 1) * c].squeeze(1),
                                             ACT.Copy, scale=cs[:, q, hd:hd + 1]).then_inc(st.s_act, 1)

        @block.sync
        def _(sp):
            for s in groups(sp):
                st.load(sp, s, [(xs[:, s.side], xs_table)])

        @block.gpsimd
        def _(pool):
            pool.sem_inc(st.s_stored, 2)
            for s in groups(pool):
                st.store(pool, s, [(mix_table, mix[:, s.side])])


def attention2_out(nc, K, I, mix_table, xg_turned, xt_table):
    heads, c = 2, 256
    with ExitStack() as ctx:
        m = Scope(nc, ctx, "n75")
        steps = 4
        st = NodeStage(nc, m, 6, 4, 0, steps, 6)
        st.ident = K["ident"]
        mix = m.sb("mix", [PARTS, 2, GROUP, heads * c])
        by_type = m.sb("by_type", [PARTS, 2, GROUP, 4, PARTS])
        w = m.sb("w", [PARTS, 2, heads * c])
        w_rel = m.sb("w_rel", [PARTS, 2, 4, PARTS])
        b_col = m.sb("b_col", [PARTS, 2])
        block = ctx.enter_context(nc.Block())

        @block.vector
        def _(dve):
            v = nc.vector
            d = Chain(dve, st.s_vec, steps)
            for s in groups(dve):
                d.round(s.g)
                for r in range(4):
                    st.await_product(dve, s, r)
                    if r == 0:
                        st.await_stored(dve, s)
                    d.op(v.tensor_copy, by_type[:, s.side, :, r, :], st.prod(s, r))
                    d.mark(f"used{r}")
                d.check()
            st.marks = dict(d.marks)

        @block.tensor
        def _(pe):
            pe.wait_ge(st.s_w, 16 * 6)

            st.start(pe)

            def before(s):
                st.await_loads(pe, s, 1)
                for k in range(4):
                    st.turn(pe, s, k, mix[:, s.side, :, k * PARTS:(k + 1) * PARTS])
                for o in range(2):
                    st.multiply_turned(pe, s, 4 + o, 4, [
                        (st.turned_block(s, k), w[:, k % 2, (k // 2) * c + o * PARTS:(k // 2) * c + (o + 1) * PARTS])
                        for k in range(4)])

            def after(s):
                for r in range(4):
                    st.multiply(pe, s, r, 6, [(st.turned_block(s, 4 + b), w_rel[:, b, r, :]) for b in range(2)])
            skewed(pe, before, after)

        @block.scalar
        def _(act):
            act.sem_inc(st.s_copy, 2)
            act.wait_ge(st.s_w, 16 * 6)
            for s in groups(act):
                st.products_done(act, s)
                st.await_stored(act, s)
                for k in range(4):
                    st.copy_turned(act, s, k, k)
                for o in range(2):
                    st.copy_turned(act, s, 4 + o, 4 + o, ACT.Relu, bias=b_col[:, o:o + 1], scale=1.0 / heads)

        @block.sync
        def _(sp):
            sp.dma_start(w[:, :, :], I["L3_gnn_gat_W"].rearrange("(b p) n -> p b n", p=PARTS)).then_inc(st.s_w, 16)
            for r in range(4):
                sp.dma_start(w_rel[:, :, r, :], I["L3_gnn_rgcn_Wrel"][r].rearrange("(b p) n -> p b n", p=PARTS))\
                  .then_inc(st.s_w, 16)
            with nc.allow_non_contiguous_dma(reason="256 bias values, one per partition"):
                sp.dma_start(b_col[:, :], I["L3_gnn_gat_b"].rearrange("(b p) -> p b", p=PARTS)).then_inc(st.s_w, 16)
            for s in groups(sp):
                st.load(sp, s, [(mix[:, s.side], mix_table)], free=st.turns_done)

        @block.gpsimd
        def _(pool):
            pool.sem_inc(st.s_stored, 2)
            for s in groups(pool):
                st.store(pool, s, [(xt_table, by_type[:, s.side].rearrange("p t r d -> p t (r d)"))],
                         [(turned_view(xg_turned, b, s.g), st.turned_block(s, 4 + b).rearrange("p t d -> p (t d)"))
                          for b in range(2)])


def fuse(nc, K, I, acc, x_table, xs_turned, xg_turned, out_table):
    with ExitStack() as ctx:
        m = Scope(nc, ctx, "n8")
        steps = 7 + LN_STEPS
        st = NodeStage(nc, m, 1, 1, 2, steps, 1)
        st.ident = K["ident"]
        x_in, rel, y = (m.sb(n, D3) for n in ("x_in", "rel", "y"))
        t, sq = m.sb("t", G3), m.sb("sq", G3)
        given = m.sb("given", [PARTS, 2, 4, GROUP, PARTS])
        w_root = m.sb("w_root", [PARTS, 2, PARTS])
        w_fuse = m.sb("w_fuse", [PARTS, 5, PARTS])
        rows = m.sb("rows", [PARTS, 2, PARTS])
        sums = m.sb("sums", [PARTS, GROUP, 6])
        stat = m.sb("stat", [PARTS, 5, GROUP])
        norm = m.sb("norm", [PARTS, 2, GROUP])
        s_rel = m.sem("s_rel")
        block = ctx.enter_context(nc.Block())

        @block.vector
        def _(dve):
            v = nc.vector
            dve.wait_ge(st.s_w, 64)
            d = Chain(dve, st.s_vec, steps)
            for s in groups(dve):
                d.round(s.g)
                st.await_product(dve, s, 0)
                d.op(v.tensor_tensor, t[:, :, :], st.prod(s, 0), bc(rows[:, 1, :].unsqueeze(1), G3), ALU.add)
                d.mark("used0")
                d.op(v.tensor_tensor, sq[:, :, :], t[:, :, :], t[:, :, :], ALU.mult)
                d.op(v.tensor_reduce, norm[:, 0, :], sq[:, :, :], AX.X, ALU.add)
                d.mark("norm")
                st.await_act(dve, s, 0)
                d.op(v.tensor_scalar, norm[:, 1, :], norm[:, 1, :], 1e-12, None, ALU.max)
                d.op(v.reciprocal, norm[:, 1, :], norm[:, 1, :])
                d.op(v.tensor_tensor, t[:, :, :], t[:, :, :], bc(norm[:, 1, :].unsqueeze(2), G3), ALU.mult)
                st.await_stored(dve, s)
                st.await_late(dve, s)
                d.op(v.tensor_tensor, t[:, :, :], t[:, :, :], x_in[:, s.side], ALU.add)
                layer_norm(nc, d, st, s, 1, t[:, :, :], y[:, s.side], sums, stat)
                d.check()
            st.marks = dict(d.marks)

        @block.tensor
        def _(pe):
            st.start(pe)

            def before(s):
                st.await_loads(pe, s, 4)
                pe.wait_ge(s_rel, s.g + 1)
                st.multiply_turned(pe, s, 0, 0, [(given[:, s.side, 2 + b], w_root[:, b, :]) for b in range(2)],
                                   extra=rel[:, s.side])

            def after(s):
                st.multiply(pe, s, 0, 1, [(given[:, s.side, b], w_fuse[:, b, :]) for b in range(4)] +
                            [(st.turned_block(s, 0), w_fuse[:, 4, :])])
            pe.wait_ge(st.s_w, 64)
            for s in groups(pe):
                before(s)
                after(s)

        @block.scalar
        def _(act):
            act.sem_inc(st.s_copy, 2)

            def before(s):
                st.products_done(act, s)
                st.copy_turned(act, s, 0, 0)

            def after(s):
                st.vec_reached(act, s, "norm")
                nc.scalar.activation(norm[:, 1, :], norm[:, 0, :], ACT.Sqrt).then_inc(st.s_act, 1)
                root_of_variance(nc, act, st, s, 1, stat, K["eps"][:, 0:1])
            skewed(act, before, after)

        @block.sync
        def _(sp):
            sp.dma_start(w_root[:, :, :], I["L3_gnn_rgcn_Wroot"].rearrange("(b p) n -> p b n", p=PARTS))\
              .then_inc(st.s_w, 16)
            sp.dma_start(w_fuse[:, :, :], I["L3_gnn_fusion_W"].rearrange("(b p) n -> p b n", p=PARTS))\
              .then_inc(st.s_w, 16)
            sp.dma_start(rows[:, 0, :], spread(I["L3_gnn_rgcn_b"])).then_inc(st.s_w, 16)
            sp.dma_start(rows[:, 1, :], spread(I["L3_gnn_fusion_b"])).then_inc(st.s_w, 16)

            def before(s):
                st.load(sp, s, [], [(given[:, s.side, 2 * n + b].rearrange("p t d -> p (t d)"),
                                     turned_view(table, b, s.g))
                                    for n, table in enumerate((xs_turned, xg_turned)) for b in range(2)],
                        free=st.products_done)
            skewed(sp, before, lambda s: st.load_late(sp, s, x_in[:, s.side], x_table))

        @block.gpsimd
        def _(pool):
            pool.sem_inc(st.s_stored, 2)
            pool.wait_ge(st.s_w, 64)

            def before(s):
                st.turns_done(pool, s)
                pool.sem_inc(st.s_gate, 1)
                nc.gpsimd.tensor_tensor(rel[:, s.side], group_of(acc, s.g), bc(rows[:, 0, :].unsqueeze(1), G3),
                                        ALU.add).then_inc(s_rel, 1)
            far_skewed(pool, before, lambda s: st.store(pool, s, [(out_table, y[:, s.side])]))


def at_items(n, size):
    return bass.ds(n * size, size)


def runs(eng, ring_runs, size):
    with eng.Fori(0, ITEMS // (ring_runs * size)) as r:
        for q in range(ring_runs):
            yield r * ring_runs + q, q, r


def tile_ids(nc, engine, K, n, size):
    why = "prepare() writes tile numbers below TILES only"
    return nc.values_load_multi_w_load_instructions(
        K["tiles"][0:1, at_items(n, size)], engines=[engine], min_val=0, max_val=TILES - 1,
        skip_runtime_bounds_check_because=why)[1]


def gather_runs(nc, pool, m, table, index_e, ring, ring_runs, size, free, s_row):
    stage = m.sb("stage", [PARTS, ring_runs, size], I32)
    s_stage, s_gate = m.sem("s_stage"), m.sem("s_gate")
    yield
    for n, q, r in runs(pool, ring_runs, size):
        free(n, q, r)
        pool.sem_inc(s_gate, 1)
        nc.gpsimd.tensor_copy(stage[:, q, :], index_e[:, at_items(n, size)]).then_inc(s_stage, 1)
        pool.wait_ge(s_stage, n + 1)
        pool.sem_inc(s_gate, 1)
        for j in range(size):
            nc.gpsimd.indirect_dma_start(ring[:, q * size + j, :], None, table,
                                         bass.IndirectOffsetOnAxis(ap=stage[:, q, j:j + 1], axis=0))\
              .then_inc(s_row(q, j), 16)
    yield


def one_hots(nc, K, out, n, size):
    return nc.vector.tensor_tensor(out, bc(K["iota"][:, :].unsqueeze(1), [PARTS, size, PARTS]),
                                   bc(K["dst_e"][:, at_items(n, size)].unsqueeze(2), [PARTS, size, PARTS]),
                                   ALU.is_equal)


def edge_pass(nc, tag, table, width, index_e, K, acc, weight_e=None):
    RR, SZ, BANKS = 4, 8, 8
    SL = RR * SZ
    per_run = 1 if weight_e is None else 2
    with ExitStack() as ctx:
        m = Scope(nc, ctx, tag)
        ring = m.sb("ring", [PARTS, SL, width])
        hot = m.sb("hot", [PARTS, SL, PARTS])
        ps = m.ps("ps", [PARTS, BANKS, 512])
        s_row = [m.sem(f"s_row{j}") for j in range(SL)]
        s_hot, s_mm, s_add, s_zero = (m.sem(n) for n in ("s_hot", "s_mm", "s_add", "s_zero"))

        def free(n, q, r):
            pool_eng[0].wait_ge(s_mm, n * SZ + SZ)
        pool_eng = [None]
        parts = gather_runs(nc, nc.gpsimd, m, table, index_e, ring, RR, SZ, free,
                                  lambda q, j: s_row[q * SZ + j])
        next(parts)
        block = ctx.enter_context(nc.Block())

        @block.gpsimd
        def _(pool):
            pool_eng[0] = pool
            next(parts)

        @block.vector
        def _(dve):
            v = nc.vector
            v.memset(acc[:, :, :], 0.0).then_inc(s_zero, 1)
            dve.wait_ge(s_zero, 1)
            dve.sem_inc(s_add, BANKS)

            def make_hot(n, q):
                dve.wait_ge(s_mm, n * SZ + SZ)
                part = hot[:, q * SZ:(q + 1) * SZ, :]
                one_hots(nc, K, part, n, SZ).then_inc(s_hot, 1)
                if weight_e is not None:
                    dve.wait_ge(s_hot, n * per_run + 1)
                    v.tensor_tensor(part, part, bc(weight_e[:, at_items(n, SZ)].unsqueeze(2), [PARTS, SZ, PARTS]),
                                    ALU.mult).then_inc(s_hot, 1)

            make_hot(0, 0)
            for n, q, r in runs(dve, RR, SZ):
                make_hot(n + 1, (q + 1) % RR)
                tiles = tile_ids(nc, mybir.EngineType.DVE, K, n, SZ)
                for j, t in enumerate(tiles):
                    dve.wait_ge(s_mm, n * SZ + j + 1 + SL)
                    dve.wait_ge(s_add, n * SZ + j + BANKS)
                    row = acc[:, bass.ds(t, 1), :].squeeze(1)
                    v.tensor_tensor(row, ps[:, (q * SZ + j) % BANKS, 0:width], row, ALU.add).then_inc(s_add, 1)

        @block.tensor
        def _(pe):
            pe.sem_inc(s_mm, SL)
            for n, q, r in runs(pe, RR, SZ):
                pe.wait_ge(s_hot, (n + 1) * per_run)
                for j in range(SZ):
                    k = q * SZ + j
                    pe.wait_ge(s_row[k], r * 16 + 16)
                    pe.wait_ge(s_add, n * SZ + j + 1)
                    nc.tensor.matmul(ps[:, k % BANKS, 0:width], hot[:, k, :], ring[:, k, :],
                                     start=True, stop=True).then_inc(s_mm, 1)


def score_pass(nc, tag, K, table, width, heads, node_vals, cols, src_e, vals_e, spill=None):
    RR, SZ = 4, 8
    SL = RR * SZ
    with ExitStack() as ctx:
        m = Scope(nc, ctx, tag)
        ring = m.sb("ring", [PARTS, SL, width])
        rows = m.sb("rows", [PARTS, 2, SZ * PARTS])
        hot_t = m.sb("hot_t", [PARTS, 2, SZ, PARTS])
        ps = m.ps("ps", [PARTS, 2, 512])
        s_row = [m.sem(f"s_row{q}") for q in range(RR)]
        s_spill = [m.sem(f"s_spill{q}") for q in range(RR)]
        s_dst = [m.sem(f"s_dst{h}") for h in range(2)]
        s_hot, s_mm, s_src, s_val, s_agate, s_spilled = (
            m.sem(n) for n in ("s_hot", "s_mm", "s_src", "s_val", "s_agate", "s_spilled"))
        pool_eng = [None]

        def free(n, q, r):
            pool_eng[0].wait_ge(s_src, n + 1)
            if spill is not None:
                pool_eng[0].wait_ge(s_spilled, n + 1)
        parts = gather_runs(nc, nc.gpsimd, m, table, K["src_e"], ring, RR, SZ, free, lambda q, j: s_row[q])
        next(parts)
        block = ctx.enter_context(nc.Block())

        @block.gpsimd
        def _(pool):
            pool_eng[0] = pool
            next(parts)

        @block.sync
        def _(sp):
            sp.sem_inc(s_spilled, RR)
            for n, q, r in runs(sp, RR, SZ):
                sp.wait_ge(s_hot, n + 1)
                sp.dma_start(rows[:, q % 2, :], K["dst_rows_d"][bass.ds(n * SZ * PARTS, SZ * PARTS)]
                             .partition_broadcast(PARTS)).then_inc(s_dst[q % 2], 16)
                if spill is not None:
                    sp.wait_ge(s_row[q], 16 * SZ * (r + 1))
                    sp.dma_start(spill[bass.ds(n, 1)].squeeze(0),
                                 ring[:, q * SZ:(q + 1) * SZ, 0:PARTS]).then_inc(s_spill[q], 16)
                    sp.wait_ge(s_spill[q], 16 * (r + 1))
                    sp.sem_inc(s_spilled, 1)

        @block.vector
        def _(dve):
            dve.sem_inc(s_hot, 2)
            for n, q, r in runs(dve, RR, SZ):
                dve.wait_ge(s_dst[q % 2], 16 * (2 * r + q // 2 + 1))
                dve.wait_ge(s_mm, n * SZ + SZ)
                nc.vector.tensor_scalar(hot_t[:, q % 2, :, :].rearrange("p j e -> p (j e)"), rows[:, q % 2, :],
                                        K["iota_p"][:, 0:1], None, ALU.is_equal).then_inc(s_hot, 1)

        @block.tensor
        def _(pe):
            pe.sem_inc(s_mm, 2 * SZ)
            for n, q, r in runs(pe, RR, SZ):
                for j, t in enumerate(tile_ids(nc, mybir.EngineType.PE, K, n, SZ)):
                    if j == 0:
                        pe.wait_ge(s_hot, n + 3)
                        pe.wait_ge(s_val, n + 1)
                    nc.tensor.matmul(ps[:, q % 2, j * cols:(j + 1) * cols], hot_t[:, q % 2, j, :],
                                     node_vals[:, bass.ds(t, 1), :].squeeze(1),
                                     start=True, stop=True).then_inc(s_mm, 1)

        @block.scalar
        def _(act):
            act.sem_inc(s_src, RR)
            act.sem_inc(s_val, 2)
            for n, q, r in runs(act, RR, SZ):
                act.wait_ge(s_mm, n * SZ + SZ + 2 * SZ)
                act.sem_inc(s_agate, 1)
                nc.scalar.activation(vals_e[:, at_items(n, SZ), :], ps[:, q % 2, 0:SZ * cols]
                                     .rearrange("p (j c) -> p j c", c=cols), ACT.Copy).then_inc(s_val, 1)
                act.wait_ge(s_row[q], 16 * SZ * (r + 1))
                act.sem_inc(s_agate, 1)
                nc.scalar.activation(src_e[:, at_items(n, SZ), :], ring[:, q * SZ:(q + 1) * SZ, width - heads:width],
                                     ACT.Copy).then_inc(s_src, 1)


def attention_pass(nc, K, spill, w_e, max_e, acc):
    heads, c = 4, 32
    W = PARTS + 2 * heads + 13
    RR, SZ, BANKS = 4, 8, 8
    SL = RR * SZ
    with ExitStack() as ctx:
        m = Scope(nc, ctx, "p0")
        ring = m.sb("ring", [PARTS, SL, PARTS])
        msg = m.sb("msg", [PARTS, SL, W])
        hot = m.sb("hot", [PARTS, SL, PARTS])
        ps = m.ps("ps", [PARTS, BANKS, 512])
        s_row = [m.sem(f"s_row{q}") for q in range(RR)]
        s_hot, s_mm, s_add, s_zero, s_msg, s_aux, s_agate, s_gate = (
            m.sem(n) for n in ("s_hot", "s_mm", "s_add", "s_zero", "s_msg", "s_aux", "s_agate", "s_gate"))
        block = ctx.enter_context(nc.Block())

        @block.sync
        def _(sp):
            for n, q, r in runs(sp, RR, SZ):
                sp.wait_ge(s_msg, n + 1)
                sp.dma_start(ring[:, q * SZ:(q + 1) * SZ, :], spill[bass.ds(n, 1)].squeeze(0))\
                  .then_inc(s_row[q], 16)

        @block.gpsimd
        def _(pool):
            pool.sem_inc(s_msg, RR)
            for n, q, r in runs(pool, RR, SZ):
                part = slice(q * SZ, (q + 1) * SZ)
                pool.wait_ge(s_mm, n * SZ + SZ)
                pool.wait_ge(s_row[q], 16 * (r + 1))
                pool.sem_inc(s_gate, 1)
                nc.gpsimd.tensor_tensor(
                    msg[:, part, 0:PARTS].rearrange("p j (h c) -> p j h c", c=c),
                    ring[:, part, :].rearrange("p j (h c) -> p j h c", c=c),
                    bc(w_e[:, at_items(n, SZ), :].unsqueeze(3), [PARTS, SZ, heads, c]), ALU.mult).then_inc(s_msg, 1)

        @block.scalar
        def _(act):
            for n, q, r in runs(act, RR, SZ):
                part = slice(q * SZ, (q + 1) * SZ)
                act.wait_ge(s_mm, n * SZ + SZ)
                act.sem_inc(s_agate, 1)
                nc.scalar.activation(msg[:, part, PARTS:PARTS + heads], w_e[:, at_items(n, SZ), :], ACT.Copy)\
                  .then_inc(s_aux, 1)
                nc.scalar.activation(msg[:, part, PARTS + heads:PARTS + 2 * heads], max_e[:, at_items(n, SZ), :],
                                     ACT.Copy).then_inc(s_aux, 1)

        @block.vector
        def _(dve):
            v = nc.vector
            v.memset(acc[:, :, :], 0.0).then_inc(s_zero, 1)
            dve.wait_ge(s_zero, 1)
            dve.sem_inc(s_add, BANKS)

            def make_hot(n, q):
                part = slice(q * SZ, (q + 1) * SZ)
                dve.wait_ge(s_mm, n * SZ + SZ)
                one_hots(nc, K, hot[:, part, :], n, SZ).then_inc(s_hot, 1)
                at = PARTS + 2 * heads
                for c0, cols, types in ((at, 4, K["et4_e"]), (at + 4, 9, K["et9_e"])):
                    v.tensor_tensor(msg[:, part, c0:c0 + cols], bc(K["iota"][:, 0:cols].unsqueeze(1), [PARTS, SZ, cols]),
                                    bc(types[:, at_items(n, SZ)].unsqueeze(2), [PARTS, SZ, cols]),
                                    ALU.is_equal).then_inc(s_hot, 1)

            make_hot(0, 0)
            for n, q, r in runs(dve, RR, SZ):
                make_hot(n + 1, (q + 1) % RR)
                tiles = tile_ids(nc, mybir.EngineType.DVE, K, n, SZ)
                for j, t in enumerate(tiles):
                    dve.wait_ge(s_mm, n * SZ + j + 1 + SL)
                    dve.wait_ge(s_add, n * SZ + j + BANKS)
                    row = acc[:, bass.ds(t, 1), :].squeeze(1)
                    v.tensor_tensor(row, ps[:, (q * SZ + j) % BANKS, 0:W], row, ALU.add).then_inc(s_add, 1)

        @block.tensor
        def _(pe):
            pe.sem_inc(s_mm, SL)
            for n, q, r in runs(pe, RR, SZ):
                pe.wait_ge(s_hot, 3 * (n + 1))
                pe.wait_ge(s_msg, n + 1 + RR)
                pe.wait_ge(s_aux, 2 * (n + 1))
                for j in range(SZ):
                    k = q * SZ + j
                    pe.wait_ge(s_add, n * SZ + j + 1)
                    nc.tensor.matmul(ps[:, k % BANKS, 0:W], hot[:, k, :], msg[:, k, :],
                                     start=True, stop=True).then_inc(s_mm, 1)


def attention2_pass(nc, K, xs_table, w_e, max_e, acc):
    heads, c = 2, 256
    W = heads * c + 2 * heads
    RR, SZ, BANKS = 4, 4, 4
    SL = RR * SZ
    HW = 8
    with ExitStack() as ctx:
        m = Scope(nc, ctx, "p6")
        ring = m.sb("ring", [PARTS, SL, c])
        aux = m.sb("aux", [PARTS, SL, 2 * heads])
        hot = m.sb("hot", [PARTS, SL, PARTS])
        hot_w = m.sb("hot_w", [PARTS, HW, heads, PARTS])
        ps = m.ps("ps", [PARTS, BANKS, 2, 512])
        s_row = [m.sem(f"s_row{j}") for j in range(SL)]
        s_hot, s_mm, s_add, s_zero, s_aux, s_agate, s_w = (
            m.sem(n) for n in ("s_hot", "s_mm", "s_add", "s_zero", "s_aux", "s_agate", "s_w"))
        pool_eng = [None]

        def free(n, q, r):
            pool_eng[0].wait_ge(s_mm, n * SZ + SZ)
        parts = gather_runs(nc, nc.gpsimd, m, xs_table, K["src_e"], ring, RR, SZ, free,
                            lambda q, j: s_row[q * SZ + j])
        next(parts)
        block = ctx.enter_context(nc.Block())

        @block.gpsimd
        def _(pool):
            pool_eng[0] = pool
            next(parts)

        @block.scalar
        def _(act):
            a = nc.scalar
            for n, q, r in runs(act, RR, SZ):
                part = slice(q * SZ, (q + 1) * SZ)
                act.wait_ge(s_mm, n * SZ + SZ)
                act.sem_inc(s_agate, 1)
                a.activation(aux[:, part, 0:heads], w_e[:, at_items(n, SZ), :], ACT.Copy).then_inc(s_aux, 1)
                a.activation(aux[:, part, heads:2 * heads], max_e[:, at_items(n, SZ), :], ACT.Copy).then_inc(s_aux, 1)
                act.wait_ge(s_aux, 2 * (n + 1))
                act.sem_inc(s_agate, 1)
                act.wait_ge(s_hot, n + 1)
                act.sem_inc(s_agate, 1)
                for j in range(SZ):
                    k = q * SZ + j
                    act.wait_ge(s_mm, n * SZ + j + 1 + SL - HW)
                    for hd in range(heads):
                        a.activation(hot_w[:, k % HW, hd, :], hot[:, k, :], ACT.Copy,
                                     scale=aux[:, k, hd:hd + 1]).then_inc(s_w, 1)

        @block.vector
        def _(dve):
            v = nc.vector
            v.memset(acc[:, :, :], 0.0).then_inc(s_zero, 1)
            dve.wait_ge(s_zero, 1)
            dve.sem_inc(s_add, 2 * BANKS)

            def make_hot(n, q):
                dve.wait_ge(s_mm, n * SZ + SZ)
                one_hots(nc, K, hot[:, q * SZ:(q + 1) * SZ, :], n, SZ).then_inc(s_hot, 1)

            make_hot(0, 0)
            make_hot(1, 1)
            for n, q, r in runs(dve, RR, SZ):
                make_hot(n + 2, (q + 2) % RR)
                tiles = tile_ids(nc, mybir.EngineType.DVE, K, n, SZ)
                for j, t in enumerate(tiles):
                    bank = (q * SZ + j) % BANKS
                    dve.wait_ge(s_mm, n * SZ + j + 1 + SL)
                    for k, (c0, c1) in enumerate(((0, heads * c), (heads * c, W))):
                        dve.wait_ge(s_add, 2 * (n * SZ + j) + k + 2 * BANKS - 1)
                        row = acc[:, bass.ds(t, 1), c0:c1].squeeze(1)
                        v.tensor_tensor(row, ps[:, bank, k, 0:c1 - c0], row, ALU.add).then_inc(s_add, 1)

        @block.tensor
        def _(pe):
            pe.sem_inc(s_mm, SL)
            for n, q, r in runs(pe, RR, SZ):
                for j in range(SZ):
                    k = q * SZ + j
                    pe.wait_ge(s_row[k], r * 16 + 16)
                    pe.wait_ge(s_w, 2 * (n * SZ + j + 1))
                    pe.wait_ge(s_add, 2 * (n * SZ + j) + 2)
                    for hd in range(heads):
                        nc.tensor.matmul(ps[:, k % BANKS, 0, hd * c:(hd + 1) * c], hot_w[:, k % HW, hd, :],
                                         ring[:, k, :], start=True, stop=True)
                    nc.tensor.matmul(ps[:, k % BANKS, 1, 0:2 * heads], hot[:, k, :], aux[:, k, :],
                                     start=True, stop=True).then_inc(s_mm, 1)


def softmax_numerators(nc, tag, K, heads, src_e, dst_e, w_e, max_e):
    with ExitStack() as ctx:
        m = Scope(nc, ctx, tag)
        score = m.sb("score", [PARTS, ITEMS, heads])
        rows_a = m.sb("rows_a", [ITEM_ROWS, heads, ROW])
        rows_b = m.sb("rows_b", [ITEM_ROWS, heads, ROW])
        ends = m.sb("ends", [ITEM_ROWS, 2, heads])
        ends_t = m.sb("ends_t", [heads, 2, ITEM_ROWS])
        carry_t = m.sb("carry_t", [heads, ITEM_ROWS + 2])
        carry = m.sb("carry", [ITEM_ROWS, 2, heads])
        ps = m.ps("ps", [PARTS, 4, 512])
        ps_s = m.ps("ps_s", [PARTS, 512])
        s_v, s_pe, s_exp = m.sem("s_v"), m.sem("s_pe"), m.sem("s_exp")
        marks, turns = {}, [0]
        block = ctx.enter_context(nc.Block())
        QUARTERS = 2 * heads
        E1, C1, E2, C2 = QUARTERS + 1, QUARTERS + 2, QUARTERS + 3, QUARTERS + 4

        @block.vector
        def _(dve):
            v = nc.vector
            d = Chain(dve, s_v)
            d.op(v.tensor_tensor, score[:, :, :], src_e, dst_e, ALU.add)
            d.op(v.scalar_tensor_tensor, score[:, :, :], score[:, :, :], 0.2, score[:, :, :], ALU.mult, ALU.max)
            d.mark("score")
            for q in range(QUARTERS):
                hd, half = q // 2, q % 2
                dve.wait_ge(s_pe, q + 1)
                d.op(v.tensor_copy, rows_a[:, hd, half * 512:half * 512 + 512], ps[0:ITEM_ROWS, q % 4, :])
                d.mark(f"forth{q}")
            for way in range(2):
                brk = K["brk"][:, 0:ROW] if way == 0 else K["brk"][:, 1:ROW + 1][:, ::-1]
                for hd in range(heads):
                    if way == 0:
                        a, b = rows_a[:, hd, :], rows_b[:, hd, :]
                    else:
                        a, b = rows_b[:, hd, :][:, ::-1], rows_a[:, hd, :][:, ::-1]
                    d.op(v.tensor_tensor_scan, b, brk, a, -BIG, ALU.add, ALU.max)
                    d.op(v.tensor_copy, ends[:, 0, hd:hd + 1], b[:, ROW - 1:ROW])
                    d.op(v.tensor_copy, ends[:, 1, hd:hd + 1], K["row_brk"][:, way:way + 1])
                d.mark(f"ends{way}")
                dve.wait_ge(s_pe, (E1, E2)[way])
                d.op(v.tensor_copy, ends_t[:, :, :], ps_s[0:heads, 0:2 * ITEM_ROWS]
                     .rearrange("p (a r) -> p a r", a=2))
                d.op(v.memset, carry_t[:, :], -BIG)
                if way == 0:
                    d.op(v.tensor_tensor_scan, carry_t[:, 1:ITEM_ROWS + 1], ends_t[:, 1, :], ends_t[:, 0, :],
                         -BIG, ALU.add, ALU.max)
                else:
                    d.op(v.tensor_tensor_scan, carry_t[:, 1:ITEM_ROWS + 1][:, ::-1], ends_t[:, 1, :][:, ::-1],
                         ends_t[:, 0, :][:, ::-1], -BIG, ALU.add, ALU.max)
                d.mark(f"carry{way}")
                dve.wait_ge(s_pe, (C1, C2)[way])
                d.op(v.tensor_copy, carry[:, way, :], ps_s[0:ITEM_ROWS, 256:256 + heads])
                for hd in range(heads):
                    if way == 0:
                        a, b = rows_a[:, hd, :], rows_b[:, hd, :]
                    else:
                        a, b = rows_b[:, hd, :][:, ::-1], rows_a[:, hd, :][:, ::-1]
                    d.op(v.tensor_tensor_scan, b, brk, a, carry[:, way, hd:hd + 1], ALU.add, ALU.max)
            d.mark("max")
            for q in range(QUARTERS):
                hd, half = q // 2, q % 2
                dve.wait_ge(s_pe, C2 + q + 1)
                d.op(v.tensor_copy,
                     max_e[:, :, hd].rearrange("p (i j) -> p j i", j=LANES)[:, 4 * half:4 * half + 4, :],
                     ps[:, q % 4, 0:4 * ITEM_ROWS].rearrange("p (j i) -> p j i", j=4))
                d.mark(f"back{q}")
            d.op(v.tensor_tensor, w_e, score[:, :, :], max_e, ALU.subtract)
            d.mark("shifted")
            d.op(v.tensor_tensor, max_e, max_e, bc(K["last_e"][:, 0:ITEMS].unsqueeze(2), [PARTS, ITEMS, heads]), ALU.mult)
            marks.update(d.marks)

        @block.tensor
        def _(pe):
            pe.wait_ge(s_v, marks["score"] + 1)
            for q in range(QUARTERS):
                hd, half = q // 2, q % 2
                if q >= 4:
                    pe.wait_ge(s_v, marks[f"forth{q - 4}"] + 1)
                for j in range(4):
                    view = score[:, :, hd].rearrange("p (i j) -> p j i", j=LANES)
                    ins = nc.tensor.transpose(ps[0:ITEM_ROWS, q % 4, j * PARTS:(j + 1) * PARTS],
                                              view[:, 4 * half + j, :], K["ident"][:, :])
                ins.then_inc(s_pe, 1)
            for way in range(2):
                pe.wait_ge(s_v, marks[f"ends{way}"] + 1)
                for a in range(2):
                    ins = nc.tensor.transpose(ps_s[0:heads, a * ITEM_ROWS:(a + 1) * ITEM_ROWS], ends[:, a, :],
                                              K["ident"][0:ITEM_ROWS, 0:ITEM_ROWS])
                ins.then_inc(s_pe, 1)
                pe.wait_ge(s_v, marks[f"carry{way}"] + 1)
                off = 0 if way == 0 else 2
                nc.tensor.transpose(ps_s[0:ITEM_ROWS, 256:256 + heads], carry_t[:, off:off + ITEM_ROWS],
                                    K["ident"][0:heads, 0:heads]).then_inc(s_pe, 1)
            pe.wait_ge(s_v, marks["max"] + 1)
            for q in range(QUARTERS):
                hd, half = q // 2, q % 2
                if q >= 4:
                    pe.wait_ge(s_v, marks[f"back{q - 4}"] + 1)
                for j in range(4):
                    at = (4 * half + j) * PARTS
                    ins = nc.tensor.transpose(ps[:, q % 4, j * ITEM_ROWS:(j + 1) * ITEM_ROWS],
                                              rows_a[:, hd, at:at + PARTS], K["ident"][0:ITEM_ROWS, 0:ITEM_ROWS])
                ins.then_inc(s_pe, 1)

        @block.scalar
        def _(act):
            act.wait_ge(s_v, marks["shifted"] + 1)
            nc.scalar.activation(w_e, w_e, ACT.Exp).then_inc(s_exp, 1)
            act.wait_ge(s_exp, 1)


def copy_in(nc, K, x, table):
    with ExitStack() as ctx:
        m = Scope(nc, ctx, "ci")
        rest = NODE_ROWS - NODES
        zero = m.sb("zero", [rest, PARTS])
        s_z, s_d = m.sem("s_z"), m.sem("s_d")
        block = ctx.enter_context(nc.Block())

        @block.vector
        def _(dve):
            nc.vector.memset(zero[:, :], 0.0).then_inc(s_z, 1)
            nc.vector.memset(K["eps"][:, :], 1e-5).then_inc(s_z, 1)
            for n in ("dst_e", "et4_e", "et9_e"):
                nc.vector.memset(K[n][:, ITEMS:ITEMS + 8], -1.0).then_inc(s_z, 1)

        @block.sync
        def _(sp):
            sp.dma_start(table[0:NODES, :].rearrange("(p r) d -> p (r d)", p=125),
                         x.rearrange("(p r) d -> p (r d)", p=125)).then_inc(s_d, 16)
            sp.wait_ge(s_z, 2)
            sp.dma_start(table[NODES:NODE_ROWS, :], zero[:, :]).then_inc(s_d, 16)
            sp.wait_ge(s_d, 32)


def copy_out(nc, table, out):
    with ExitStack() as ctx:
        m = Scope(nc, ctx, "co")
        s_d = m.sem("s_d")
        block = ctx.enter_context(nc.Block())

        @block.sync
        def _(sp):
            sp.dma_start(out.rearrange("(p r) d -> p (r d)", p=125),
                         table[0:NODES, :].rearrange("(p r) d -> p (r d)", p=125)).then_inc(s_d, 16)
            sp.wait_ge(s_d, 16)


def type_weights(nc, K, vals_e, w7_e):
    with ExitStack() as ctx:
        m = Scope(nc, ctx, "tw")
        t = m.sb("t", [PARTS, ITEMS])
        s_v = m.sem("s_v")
        block = ctx.enter_context(nc.Block())

        @block.vector
        def _(dve):
            v = nc.vector
            d = Chain(dve, s_v)
            d.op(v.memset, w7_e[:, ITEMS:ITEMS + 8], 0.0)
            for r in range(4):
                to = w7_e if r == 0 else t
                d.op(v.scalar_tensor_tensor, to[:, 0:ITEMS], K["et4_e"][:, 0:ITEMS], float(r), vals_e[:, :, 2 + r],
                     ALU.is_equal, ALU.mult)
                if r:
                    d.op(v.tensor_tensor, w7_e[:, 0:ITEMS], w7_e[:, 0:ITEMS], t[:, :], ALU.add)
            dve.wait_ge(s_v, d.n + 1)


def build(nc, I, out):
    with ExitStack() as ctx:
        g = Scope(nc, ctx, "k")
        K = {}
        K["ident"] = g.sb("ident", [PARTS, PARTS])
        K["iota_i"] = g.sb("iota_i", [PARTS, PARTS], I32)
        K["iota"] = g.sb("iota", [PARTS, PARTS])
        K["iota_pi"] = g.sb("iota_pi", [PARTS, 1], I32)
        K["iota_p"] = g.sb("iota_p", [PARTS, 1])
        K["eps"] = g.sb("eps", [PARTS, 1])
        K["tiles"] = g.sb("tiles", [1, ITEMS], I32)
        for n in ("src_e", "xt_e"):
            K[n] = g.sb(n, [PARTS, ITEMS], I32)
        for n in ("dst_e", "et4_e", "et9_e", "last_e"):
            K[n] = g.sb(n, [PARTS, ITEMS + 8])
        K["brk"] = g.sb("brk", [ITEM_ROWS, ROW + 1])
        K["row_brk"] = g.sb("row_brk", [ITEM_ROWS, 2])
        K["inv_deg"] = g.sb("inv_deg", [PARTS, TILES])
        K["inv4"] = g.sb("inv4", [PARTS, TILES, 4])
        K["counts"] = g.sb("counts", [PARTS, TILES, 10])

        def dram(name, *shape, dt=FP32):
            return nc.dram_tensor(name, list(shape), dt).ap()
        K["zero_i"] = g.sb("zero_i", [16, 8], I32)
        for n in ("src", "dst", "et4", "et9"):
            K["edges_" + n] = dram("edges_" + n, EDGES + PARTS, dt=I32)
        K["tiles_d"] = dram("tiles_d", ITEMS, dt=I32)
        K["dst_rows_d"] = dram("dst_rows_d", ITEMS * PARTS)
        x0, x1, x2, x3, x4, hid, skip_t = (dram(n, NODE_ROWS, PARTS) for n in
                                           ("x0", "x1", "x2", "x3", "x4", "hid", "skip_t"))
        h_t = dram("h_t", NODE_ROWS, PARTS + 4)
        spill = dram("spill", ITEMS // 8, PARTS, 8, PARTS)
        prepare(nc, I["src"], I["dst"], I["edge_type_4"], I["edge_type_9"], K)
        copy_in(nc, K, I["x"], x0)

        with ExitStack() as c:
            s = Scope(nc, c, "l0")
            K["scores"] = s.sb("scores", [PARTS, TILES, 8])
            K["scores_tmp"] = s.sb("scores_tmp", [PARTS, GROUP, 8])
            w_e = s.sb("w_e", [PARTS, ITEMS, 4])
            max_e = s.sb("max_e", [PARTS, ITEMS, 4])
            attention_in(nc, K, I, x0, h_t, skip_t)
            score_pass(nc, "s0", K, h_t, PARTS + 4, 4, K["scores"][:, :, 4:8], 4, w_e, max_e, spill)
            softmax_numerators(nc, "m0", K, 4, w_e[:, :, :], max_e[:, :, :], w_e[:, :, :], max_e[:, :, :])
            acc = s.sb("acc", [PARTS, TILES, 149])
            attention_pass(nc, K, spill, w_e, max_e, acc)
            attention_out(nc, K, I, acc, x0, h_t, skip_t, x1)

        with ExitStack() as c:
            acc = Scope(nc, c, "l1").sb("acc", [PARTS, TILES, PARTS])
            W1, W2 = I["L1_gnn_W1"], I["L1_gnn_W2"]
            edge_pass(nc, "p1", x1, PARTS, K["src_e"], K, acc)
            sage(nc, "n2", K, x1, acc, PARTS, PARTS, W1[0:PARTS, :], W1[PARTS:, :], I["L1_gnn_b1"], hid)
            edge_pass(nc, "p2", hid, PARTS, K["src_e"], K, acc)
            sage(nc, "n3", K, hid, acc, PARTS, PARTS, W2[0:PARTS, :], W2[PARTS:, :], I["L1_gnn_b2"], x2, residual=x1)

        with ExitStack() as c:
            acc = Scope(nc, c, "l2").sb("acc", [PARTS, TILES, PARTS])
            edge_pass(nc, "p3", x2, PARTS, K["src_e"], K, acc)
            gated_update(nc, K, I, acc, x2, x3)


        xs1, xs = (dram(n, NODE_ROWS, 256) for n in ("xs1", "xs"))
        xs_turned, xg_turned = (dram(n, 2, PARTS, NODE_ROWS) for n in ("xs_turned", "xg_turned"))
        mix = dram("mix", NODE_ROWS, 2 * 256)
        xt = dram("xt", NODE_ROWS, 4 * PARTS)
        score2 = dram("score2", NODE_ROWS, 2)
        with ExitStack() as c:
            acc = Scope(nc, c, "l3a").sb("acc", [PARTS, TILES, PARTS])
            edge_pass(nc, "p4", x3, PARTS, K["src_e"], K, acc)
            sage(nc, "n5", K, x3, acc, PARTS, 256, I["L3_gnn_sage1_Wr"], I["L3_gnn_sage1_Wl"], I["L3_gnn_sage1_b"],
                 xs1)
        with ExitStack() as c:
            acc = Scope(nc, c, "l3b").sb("acc", [PARTS, TILES, 256])
            edge_pass(nc, "p5", xs1, 256, K["src_e"], K, acc)
            sage(nc, "n55", K, xs1, acc, 256, 256, I["L3_gnn_sage2_Wr"], I["L3_gnn_sage2_Wl"], I["L3_gnn_sage2_b"],
                 xs)
        with ExitStack() as c:
            s = Scope(nc, c, "l3c")
            K["own"] = s.sb("own", [PARTS, TILES, 4])
            w7_e = s.sb("w7_e", [PARTS, ITEMS + 8])
            with ExitStack() as c2:
                s = Scope(nc, c2, "l3d")
                w_e = s.sb("w_e", [PARTS, ITEMS, 2])
                max_e = s.sb("max_e", [PARTS, ITEMS, 2])
                with ExitStack() as c3:
                    s3 = Scope(nc, c3, "l3e")
                    K["expand"] = s3.sb("expand", [PARTS, TILES, 6])
                    vals_e = s3.sb("vals_e", [PARTS, ITEMS, 6])
                    attention2_in(nc, K, I, xs, score2, xs_turned)
                    score_pass(nc, "s3", K, score2, 2, 2, K["expand"], 6, w_e, vals_e)
                    type_weights(nc, K, vals_e, w7_e)
                    softmax_numerators(nc, "m3", K, 2, w_e[:, :, :], vals_e[:, :, 0:2], w_e[:, :, :],
                                       max_e[:, :, :])
                acc = s.sb("acc", [PARTS, TILES, 516])
                attention2_pass(nc, K, xs, w_e, max_e, acc)
                attention2_mix(nc, K, acc, xs, mix)
            attention2_out(nc, K, I, mix, xg_turned, xt)
            acc = Scope(nc, c, "l3f").sb("acc", [PARTS, TILES, PARTS])
            edge_pass(nc, "p7", xt.rearrange("n (r d) -> (n r) d", d=PARTS), PARTS, K["xt_e"], K, acc,
                      weight_e=w7_e)
            fuse(nc, K, I, acc, x3, xs_turned, xg_turned, x4)
        copy_out(nc, x4, out)


_INS = ['x', 'src', 'dst', 'edge_type_4', 'edge_type_9', 'L0_gnn_W', 'L0_gnn_att_src', 'L0_gnn_att_dst',
        'L0_gnn_gat_bias', 'L0_gnn_skip_W', 'L0_gnn_skip_b', 'L0_gnn_ln_g', 'L0_gnn_ln_b', 'L1_gnn_W1',
        'L1_gnn_b1', 'L1_gnn_W2', 'L1_gnn_b2', 'L2_gnn_b_msg', 'L2_gnn_edge_embed', 'L2_gnn_b_ih', 'L2_gnn_b_hh',
        'L3_gnn_sage1_Wl', 'L3_gnn_sage1_Wr', 'L3_gnn_sage1_b', 'L3_gnn_sage2_Wl', 'L3_gnn_sage2_Wr',
        'L3_gnn_sage2_b', 'L3_gnn_gat_W', 'L3_gnn_gat_att_src', 'L3_gnn_gat_att_dst', 'L3_gnn_gat_b',
        'L3_gnn_rgcn_Wrel', 'L3_gnn_rgcn_Wroot', 'L3_gnn_rgcn_b', 'L3_gnn_fusion_W', 'L3_gnn_fusion_b']


def kernel(**inputs):
    import numpy as _np
    import concourse.bacc as _bacc
    from concourse import mybir as _mybir
    from concourse.bass_utils import run_bass_kernel_spmd as _run

    laid = {name: inputs[name] for name in _INS}
    for name in ("W_msg", "W_ih", "W_hh"):
        laid[f"L2_{name}_T"] = _np.asarray(inputs[f"L2_gnn_{name}"]).T
    nc = _bacc.Bacc("TRN2", target_bir_lowering=False, num_devices=1)
    arrays, args = {}, {}
    for name, a in laid.items():
        a = _np.ascontiguousarray(a)
        arrays[f"in_{name}"] = a
        args[name] = nc.dram_tensor(f"in_{name}", a.shape, _mybir.dt.from_np(a.dtype), kind="ExternalInput").ap()
    out = nc.dram_tensor("out_0", (NODES, PARTS), _mybir.dt.float32, kind="ExternalOutput").ap()
    build(nc, args, out)
    r = _run(nc, [arrays], core_ids=[0])
    return r.results[0]["out_0"]
```
